# Optimizing a Trainium2 kernel written in Bass

```python
import numpy as np
import jax
import jax.numpy as jnp

def _softmax(x, axis=-1):
    return jax.nn.softmax(x, axis=axis)

def _gelu(x):
    return jax.nn.gelu(x, approximate=True)

def _silu(x):
    return jax.nn.silu(x)

def _sigmoid(x):
    return jax.nn.sigmoid(x)

def _layernorm(x, axis=-1, eps=1e-05):
    m = jnp.mean(x, axis=axis, keepdims=True)
    v = jnp.var(x, axis=axis, keepdims=True)
    return (x - m) / jnp.sqrt(v + eps)

def _scatter_add(tgt, idx, src, axis=0):
    return tgt.at[idx].add(src)

def _segment_sum(src, seg, n):
    return jax.ops.segment_sum(src, seg, n)
kernel_name = 'mk_gnn_resnorm_d4_gnn_r32_7c7878'

def setup_inputs(seed: int=0):
    np.random.seed(seed)
    _w = jnp.asarray

    def _rec_inputs():
        import jax
        import jax.numpy as jnp
        _gk = jax.random.key(seed)
        x = -2.02e-06 + 0.01 * jax.random.normal(jax.random.fold_in(_gk, 1), (50000, 128), jnp.float32)
        src = jax.random.randint(jax.random.fold_in(_gk, 2), (50000,), 0, 50000, jnp.int32)
        dst = jnp.minimum((50000 * jax.random.uniform(jax.random.fold_in(_gk, 3), (50000,)) ** 2.0).astype(jnp.int32), 49999)
        _o = jnp.argsort(dst, stable=True)
        src = src[_o]
        dst = dst[_o]
        edge_attr_16 = 0.000268479 + 0.999861 * jax.random.normal(jax.random.fold_in(_gk, 12), (50000, 16), jnp.float32)
        edge_type_8 = jax.random.randint(jax.random.fold_in(_gk, 14), (50000,), 0, 8, jnp.int32)
        edge_weight = jax.random.uniform(jax.random.fold_in(_gk, 15), (50000,), jnp.float32, 0.0, 9.99999)
        return (x, src, dst, edge_attr_16, edge_type_8, edge_weight)
    x, src, dst, edge_attr_16, edge_type_8, edge_weight = _rec_inputs()

    def _L0_gnn_setup():
        import jax, jax.numpy as jnp
        import numpy as np
        EPS = 1e-07
        MIN_NORM = 1e-15
        PROJ_EPS = 0.004
        C = 1.0
        HEADS = 4
        NEG_SLOPE = 0.2

        def artanh(x):
            x = jnp.clip(x, -1.0 + EPS, 1.0 - EPS)
            return 0.5 * (jnp.log1p(x) - jnp.log1p(-x))

        def _norm(x):
            return jnp.clip(jnp.linalg.norm(x, axis=-1, keepdims=True), MIN_NORM)

        def proj(x, c):
            n = _norm(x)
            maxnorm = (1.0 - PROJ_EPS) / jnp.sqrt(c)
            return jnp.where(n > maxnorm, x / n * maxnorm, x)

        def expmap0(u, c):
            sc = jnp.sqrt(c)
            n = _norm(u)
            return jnp.tanh(sc * n) * u / (sc * n)

        def logmap0(p, c):
            sc = jnp.sqrt(c)
            n = _norm(p)
            return artanh(sc * n) * p / (sc * n)

        def mobius_add(x, y, c):
            x2 = jnp.sum(x * x, -1, keepdims=True)
            y2 = jnp.sum(y * y, -1, keepdims=True)
            xy = jnp.sum(x * y, -1, keepdims=True)
            num = (1 + 2 * c * xy + c * y2) * x + (1 - c * x2) * y
            den = 1 + 2 * c * xy + c * c * x2 * y2
            return num / jnp.clip(den, MIN_NORM)

        def mobius_matvec(m, x, c):
            sc = jnp.sqrt(c)
            xn = _norm(x)
            mx = x @ m.T
            mxn = _norm(mx)
            res = jnp.tanh(mxn / xn * artanh(sc * xn)) * mx / (mxn * sc)
            zero = jnp.all(mx == 0, axis=-1, keepdims=True)
            return jnp.where(zero, 0.0, res)

        def segment_softmax(scores, seg, n):
            smax = jax.ops.segment_max(scores, seg, num_segments=n)
            smax = jnp.where(jnp.isfinite(smax), smax, 0.0)
            ex = jnp.exp(scores - smax[seg])
            den = jax.ops.segment_sum(ex, seg, num_segments=n)
            return ex / jnp.clip(den[seg], MIN_NORM)
        key = jax.random.key(seed)
        ks = jax.random.split(key, 6)
        N, D_IN, D_OUT, E = (50000, 128, 128, 25000)
        x = 0.01 * jax.random.normal(ks[0], (N, D_IN), dtype=jnp.float32)
        W = (math := np.sqrt(2.0 * 6.0 / (D_IN + D_OUT))) * jax.random.uniform(ks[1], (D_OUT, D_IN), dtype=jnp.float32, minval=-1.0, maxval=1.0)
        lin_bias = jnp.zeros((D_OUT,), jnp.float32)
        att = 0.1 * jax.random.normal(ks[2], (1, HEADS, 2 * (D_OUT // HEADS)), dtype=jnp.float32)
        conv_bias = jnp.zeros((D_OUT,), jnp.float32)
        src = jax.random.randint(ks[3], (E,), 0, N, dtype=jnp.int32)
        dst = (src + 1 + jax.random.randint(ks[4], (E,), 0, N - 1, dtype=jnp.int32)) % N
        return {'x': x, 'W': W, 'lin_bias': lin_bias, 'att': att, 'conv_bias': conv_bias, 'edge_src': src, 'edge_dst': dst}
    _L0_gnn_all = _L0_gnn_setup()
    _L0_gnn_in = {k: v for k, v in _L0_gnn_all.items() if k in ('W', 'lin_bias', 'att', 'conv_bias')}
    del _L0_gnn_all

    def _L1_gnn_setup():
        import jax, jax.numpy as jnp
        import numpy as np
        NEG_SLOPE = 0.2
        key = jax.random.key(seed)
        k1, k2, k3, k4, k5, k6 = jax.random.split(key, 6)
        N, E, IN, OUT = (50000, 25000, 128, 128)
        x = jax.random.normal(k1, (N, IN), dtype=jnp.float32)
        edge_index = jax.random.randint(k2, (2, E), 0, N, dtype=jnp.int64)
        W = jax.random.normal(k3, (IN, OUT), dtype=jnp.float32) / np.sqrt(IN)
        att_src = jax.random.normal(k4, (OUT,), dtype=jnp.float32) / np.sqrt(OUT)
        att_dst = jax.random.normal(k5, (OUT,), dtype=jnp.float32) / np.sqrt(OUT)
        bias = jnp.zeros((OUT,), dtype=jnp.float32)
        return {'x': x, 'edge_index': edge_index, 'W': W, 'att_src': att_src, 'att_dst': att_dst, 'bias': bias}
    _L1_gnn_all = _L1_gnn_setup()
    _L1_gnn_in = {k: v for k, v in _L1_gnn_all.items() if k in ('W', 'att_src', 'att_dst', 'bias')}
    del _L1_gnn_all

    def _L2_gnn_setup():
        import jax, jax.numpy as jnp
        import numpy as np
        N_NODES = 3125
        N_EDGES = 18750
        H = 128
        T = 8
        L = 2

        def _gru_cell(x, h, wih, whh, bih, bhh):
            gi = x @ wih.T + bih
            gh = h @ whh.T + bhh
            i_r, i_z, i_n = jnp.split(gi, 3, axis=-1)
            h_r, h_z, h_n = jnp.split(gh, 3, axis=-1)
            r = jax.nn.sigmoid(i_r + h_r)
            z = jax.nn.sigmoid(i_z + h_z)
            n = jnp.tanh(i_n + r * h_n)
            return (1.0 - z) * n + z * h
        key = jax.random.key(seed)
        ks = jax.random.split(key, 12)
        s = 1.0 / np.sqrt(H)
        inp = {'node_features': jax.random.normal(ks[0], (N_NODES, H), dtype=jnp.float32), 'edge_index': jax.random.randint(ks[1], (2, N_EDGES), 0, N_NODES, dtype=jnp.int64), 'edge_type': jax.random.randint(ks[2], (N_EDGES,), 0, T, dtype=jnp.int64), 'node_proj_w': jax.random.uniform(ks[3], (H, H), jnp.float32, -s, s), 'node_proj_b': jax.random.uniform(ks[4], (H,), jnp.float32, -s, s), 'edge_W': jax.random.uniform(ks[5], (L, T, H, H), jnp.float32, -s, s), 'edge_b': jax.random.uniform(ks[6], (L, T, H), jnp.float32, -s, s), 'gru_wih': jax.random.uniform(ks[7], (L, 3 * H, H), jnp.float32, -s, s), 'gru_whh': jax.random.uniform(ks[8], (L, 3 * H, H), jnp.float32, -s, s), 'gru_bih': jax.random.uniform(ks[9], (L, 3 * H), jnp.float32, -s, s), 'gru_bhh': jax.random.uniform(ks[10], (L, 3 * H), jnp.float32, -s, s), 'out_w': jax.random.uniform(ks[11], (H, H), jnp.float32, -s, s), 'out_b': jnp.zeros((H,), jnp.float32)}
        return inp
    _L2_gnn_all = _L2_gnn_setup()
    _L2_gnn_in = {k: v for k, v in _L2_gnn_all.items() if k in ('node_proj_w', 'node_proj_b', 'edge_W', 'edge_b', 'gru_wih', 'gru_whh', 'gru_bih', 'gru_bhh', 'out_w', 'out_b')}
    del _L2_gnn_all

    def _L3_gnn_setup():
        import jax, jax.numpy as jnp
        import numpy as np
        N_NODES = 3125
        N_EDGES = 20000
        HIDDEN = 128
        FILTERS = 128
        RADIAL = 50
        CUTOFF = 10.0

        def _linear_params(key, d_in, d_out):
            kw, kb = jax.random.split(key)
            bound = 1.0 / np.sqrt(d_in)
            W = jax.random.uniform(kw, (d_in, d_out), jnp.float32, -bound, bound)
            b = jax.random.uniform(kb, (d_out,), jnp.float32, -bound, bound)
            return (W, b)

        def _gaussian_smearing(d):
            offsets = jnp.linspace(0.0, CUTOFF, RADIAL, dtype=d.dtype)
            coeff = -0.5 / (offsets[1] - offsets[0]) ** 2
            diff = d[:, None] - offsets[None, :]
            return jnp.exp(coeff * diff * diff)
        key = jax.random.key(seed)
        ks = jax.random.split(key, 12)
        x = jax.random.normal(ks[0], (N_NODES, HIDDEN), jnp.float32)
        edge_index = jax.random.randint(ks[1], (2, N_EDGES), 0, N_NODES, jnp.int64 if jax.config.jax_enable_x64 else jnp.int32)
        edge_attr = jax.random.normal(ks[2], (N_EDGES, 16), jnp.float32)
        distances = jax.random.uniform(ks[3], (N_EDGES,), jnp.float32, 0.0, CUTOFF)
        Wm1, bm1 = _linear_params(ks[4], 2 * HIDDEN + RADIAL, FILTERS)
        Wm2, bm2 = _linear_params(ks[5], FILTERS, FILTERS)
        Wm3, bm3 = _linear_params(ks[6], FILTERS, HIDDEN)
        Wu1, bu1 = _linear_params(ks[7], 2 * HIDDEN, HIDDEN)
        Wu2, bu2 = _linear_params(ks[8], HIDDEN, HIDDEN)
        Wi1, bi1 = _linear_params(ks[9], HIDDEN, HIDDEN)
        Wi2, bi2 = _linear_params(ks[10], HIDDEN, HIDDEN)
        return {'x': x, 'edge_index': edge_index, 'edge_attr': edge_attr, 'distances': distances, 'Wm1': Wm1, 'bm1': bm1, 'Wm2': Wm2, 'bm2': bm2, 'Wm3': Wm3, 'bm3': bm3, 'Wu1': Wu1, 'bu1': bu1, 'Wu2': Wu2, 'bu2': bu2, 'Wi1': Wi1, 'bi1': bi1, 'Wi2': Wi2, 'bi2': bi2}
    _L3_gnn_all = _L3_gnn_setup()
    _L3_gnn_in = {k: v for k, v in _L3_gnn_all.items() if k in ('Wm1', 'bm1', 'Wm2', 'bm2', 'Wm3', 'bm3', 'Wu1', 'bu1', 'Wu2', 'bu2', 'Wi1', 'bi1', 'Wi2', 'bi2')}
    del _L3_gnn_all
    return {'x': x, 'src': src, 'dst': dst, 'edge_attr_16': edge_attr_16, 'edge_type_8': edge_type_8, 'edge_weight': edge_weight, 'L0_gnn_W': _L0_gnn_in['W'], 'L0_gnn_lin_bias': _L0_gnn_in['lin_bias'], 'L0_gnn_att': _L0_gnn_in['att'], 'L0_gnn_conv_bias': _L0_gnn_in['conv_bias'], 'L1_gnn_W': _L1_gnn_in['W'], 'L1_gnn_att_src': _L1_gnn_in['att_src'], 'L1_gnn_att_dst': _L1_gnn_in['att_dst'], 'L1_gnn_bias': _L1_gnn_in['bias'], 'L2_gnn_node_proj_w': _L2_gnn_in['node_proj_w'], 'L2_gnn_node_proj_b': _L2_gnn_in['node_proj_b'], 'L2_gnn_edge_W': _L2_gnn_in['edge_W'], 'L2_gnn_edge_b': _L2_gnn_in['edge_b'], 'L2_gnn_gru_wih': _L2_gnn_in['gru_wih'], 'L2_gnn_gru_whh': _L2_gnn_in['gru_whh'], 'L2_gnn_gru_bih': _L2_gnn_in['gru_bih'], 'L2_gnn_gru_bhh': _L2_gnn_in['gru_bhh'], 'L2_gnn_out_w': _L2_gnn_in['out_w'], 'L2_gnn_out_b': _L2_gnn_in['out_b'], 'L3_gnn_Wm1': _L3_gnn_in['Wm1'], 'L3_gnn_bm1': _L3_gnn_in['bm1'], 'L3_gnn_Wm2': _L3_gnn_in['Wm2'], 'L3_gnn_bm2': _L3_gnn_in['bm2'], 'L3_gnn_Wm3': _L3_gnn_in['Wm3'], 'L3_gnn_bm3': _L3_gnn_in['bm3'], 'L3_gnn_Wu1': _L3_gnn_in['Wu1'], 'L3_gnn_bu1': _L3_gnn_in['bu1'], 'L3_gnn_Wu2': _L3_gnn_in['Wu2'], 'L3_gnn_bu2': _L3_gnn_in['bu2'], 'L3_gnn_Wi1': _L3_gnn_in['Wi1'], 'L3_gnn_bi1': _L3_gnn_in['bi1'], 'L3_gnn_Wi2': _L3_gnn_in['Wi2'], 'L3_gnn_bi2': _L3_gnn_in['bi2']}

def reference(x, src, dst, edge_attr_16, edge_type_8, edge_weight, L0_gnn_W, L0_gnn_lin_bias, L0_gnn_att, L0_gnn_conv_bias, L1_gnn_W, L1_gnn_att_src, L1_gnn_att_dst, L1_gnn_bias, L2_gnn_node_proj_w, L2_gnn_node_proj_b, L2_gnn_edge_W, L2_gnn_edge_b, L2_gnn_gru_wih, L2_gnn_gru_whh, L2_gnn_gru_bih, L2_gnn_gru_bhh, L2_gnn_out_w, L2_gnn_out_b, L3_gnn_Wm1, L3_gnn_bm1, L3_gnn_Wm2, L3_gnn_bm2, L3_gnn_Wm3, L3_gnn_bm3, L3_gnn_Wu1, L3_gnn_bu1, L3_gnn_Wu2, L3_gnn_bu2, L3_gnn_Wi1, L3_gnn_bi1, L3_gnn_Wi2, L3_gnn_bi2):
    import jax
    import jax.numpy as jnp

    def _L0_gnn_ref(x, W, lin_bias, att, conv_bias, edge_src, edge_dst):
        import jax, jax.numpy as jnp
        import numpy as np
        EPS = 1e-07
        MIN_NORM = 1e-15
        PROJ_EPS = 0.004
        C = 1.0
        HEADS = 4
        NEG_SLOPE = 0.2

        def artanh(x):
            x = jnp.clip(x, -1.0 + EPS, 1.0 - EPS)
            return 0.5 * (jnp.log1p(x) - jnp.log1p(-x))

        def _norm(x):
            return jnp.clip(jnp.linalg.norm(x, axis=-1, keepdims=True), MIN_NORM)

        def proj(x, c):
            n = _norm(x)
            maxnorm = (1.0 - PROJ_EPS) / jnp.sqrt(c)
            return jnp.where(n > maxnorm, x / n * maxnorm, x)

        def expmap0(u, c):
            sc = jnp.sqrt(c)
            n = _norm(u)
            return jnp.tanh(sc * n) * u / (sc * n)

        def logmap0(p, c):
            sc = jnp.sqrt(c)
            n = _norm(p)
            return artanh(sc * n) * p / (sc * n)

        def mobius_add(x, y, c):
            x2 = jnp.sum(x * x, -1, keepdims=True)
            y2 = jnp.sum(y * y, -1, keepdims=True)
            xy = jnp.sum(x * y, -1, keepdims=True)
            num = (1 + 2 * c * xy + c * y2) * x + (1 - c * x2) * y
            den = 1 + 2 * c * xy + c * c * x2 * y2
            return num / jnp.clip(den, MIN_NORM)

        def mobius_matvec(m, x, c):
            sc = jnp.sqrt(c)
            xn = _norm(x)
            mx = x @ m.T
            mxn = _norm(mx)
            res = jnp.tanh(mxn / xn * artanh(sc * xn)) * mx / (mxn * sc)
            zero = jnp.all(mx == 0, axis=-1, keepdims=True)
            return jnp.where(zero, 0.0, res)

        def segment_softmax(scores, seg, n):
            smax = jax.ops.segment_max(scores, seg, num_segments=n)
            smax = jnp.where(jnp.isfinite(smax), smax, 0.0)
            ex = jnp.exp(scores - smax[seg])
            den = jax.ops.segment_sum(ex, seg, num_segments=n)
            return ex / jnp.clip(den[seg], MIN_NORM)
        N = x.shape[0]
        H = HEADS
        h = proj(mobius_matvec(W, x, C), C)
        hyp_bias = proj(expmap0(lin_bias, C), C)
        h = proj(mobius_add(h, hyp_bias, C), C)
        D = h.shape[-1] // H
        loops = jnp.arange(N, dtype=edge_src.dtype)
        src = jnp.concatenate([edge_src, loops])
        dst = jnp.concatenate([edge_dst, loops])
        log_x = logmap0(h, C).reshape(N, H, D)
        x_i = log_x[dst]
        x_j = log_x[src]
        att_i, att_j = (att[0, :, :D], att[0, :, D:])
        alpha = jnp.einsum('ehd,hd->eh', x_i, att_i) + jnp.einsum('ehd,hd->eh', x_j, att_j)
        alpha = jax.nn.leaky_relu(alpha, NEG_SLOPE)
        alpha = segment_softmax(alpha, dst, N)
        msg = x_j * alpha[:, :, None]
        out = jax.ops.segment_sum(msg, dst, num_segments=N)
        out = out.reshape(N, H * D) + conv_bias
        out = jax.nn.relu(out)
        return proj(expmap0(out, C), C)

    def _L1_gnn_ref(x, edge_index, W, att_src, att_dst, bias):
        import jax, jax.numpy as jnp
        import numpy as np
        NEG_SLOPE = 0.2
        N = x.shape[0]
        loop = jnp.arange(N, dtype=edge_index.dtype)
        src = jnp.concatenate([edge_index[0], loop])
        dst = jnp.concatenate([edge_index[1], loop])
        h = x @ W
        a_s = h @ att_src
        a_d = h @ att_dst
        e = jax.nn.leaky_relu(a_s[src] + a_d[dst], NEG_SLOPE)
        m = jax.ops.segment_max(e, dst, num_segments=N)
        p = jnp.exp(e - m[dst])
        denom = jax.ops.segment_sum(p, dst, num_segments=N)
        alpha = p / denom[dst]
        out = jax.ops.segment_sum(h[src] * alpha[:, None], dst, num_segments=N)
        return out + bias

    def _L2_gnn_ref(node_features, edge_index, edge_type, node_proj_w, node_proj_b, edge_W, edge_b, gru_wih, gru_whh, gru_bih, gru_bhh, out_w, out_b):
        import jax, jax.numpy as jnp
        import numpy as np
        N_NODES = 3125
        N_EDGES = 18750
        H = 128
        T = 8
        L = 2

        def _gru_cell(x, h, wih, whh, bih, bhh):
            gi = x @ wih.T + bih
            gh = h @ whh.T + bhh
            i_r, i_z, i_n = jnp.split(gi, 3, axis=-1)
            h_r, h_z, h_n = jnp.split(gh, 3, axis=-1)
            r = jax.nn.sigmoid(i_r + h_r)
            z = jax.nn.sigmoid(i_z + h_z)
            n = jnp.tanh(i_n + r * h_n)
            return (1.0 - z) * n + z * h
        num_nodes = node_features.shape[0]
        src, dst = (edge_index[0], edge_index[1])
        h = jax.nn.relu(node_features @ node_proj_w.T + node_proj_b)
        for l in range(L):
            trans = jnp.einsum('nh,tdh->tnd', h, edge_W[l])
            msgs = trans[edge_type, src]
            agg = jax.ops.segment_sum(msgs, dst, num_segments=num_nodes)
            h = _gru_cell(agg, h, gru_wih[l], gru_whh[l], gru_bih[l], gru_bhh[l])
            h = jax.nn.relu(h)
        return h @ out_w.T + out_b

    def _L3_gnn_ref(x, edge_index, edge_attr, distances, Wm1, bm1, Wm2, bm2, Wm3, bm3, Wu1, bu1, Wu2, bu2, Wi1, bi1, Wi2, bi2):
        import jax, jax.numpy as jnp
        import numpy as np
        N_NODES = 3125
        N_EDGES = 20000
        HIDDEN = 128
        FILTERS = 128
        RADIAL = 50
        CUTOFF = 10.0

        def _linear_params(key, d_in, d_out):
            kw, kb = jax.random.split(key)
            bound = 1.0 / np.sqrt(d_in)
            W = jax.random.uniform(kw, (d_in, d_out), jnp.float32, -bound, bound)
            b = jax.random.uniform(kb, (d_out,), jnp.float32, -bound, bound)
            return (W, b)

        def _gaussian_smearing(d):
            offsets = jnp.linspace(0.0, CUTOFF, RADIAL, dtype=d.dtype)
            coeff = -0.5 / (offsets[1] - offsets[0]) ** 2
            diff = d[:, None] - offsets[None, :]
            return jnp.exp(coeff * diff * diff)
        silu = jax.nn.silu
        radial = _gaussian_smearing(distances)
        row, col = (edge_index[0], edge_index[1])
        edge_features = jnp.concatenate([x[row], x[col], radial], axis=-1)
        h = silu(edge_features @ Wm1 + bm1)
        h = silu(h @ Wm2 + bm2)
        messages = h @ Wm3 + bm3
        out = jax.ops.segment_sum(messages, col, num_segments=x.shape[0])
        u = silu(jnp.concatenate([x, out], axis=-1) @ Wu1 + bu1)
        u = u @ Wu2 + bu2
        u = silu(u @ Wi1 + bi1)
        return u @ Wi2 + bi2
    edge_index = jnp.stack([src, dst])
    x = _layernorm(x + _L0_gnn_ref(x, L0_gnn_W, L0_gnn_lin_bias, L0_gnn_att, L0_gnn_conv_bias, src, dst), axis=-1)
    x = _layernorm(x + _L1_gnn_ref(x, edge_index, L1_gnn_W, L1_gnn_att_src, L1_gnn_att_dst, L1_gnn_bias), axis=-1)
    x = _layernorm(x + _L2_gnn_ref(x, edge_index, edge_type_8, L2_gnn_node_proj_w, L2_gnn_node_proj_b, L2_gnn_edge_W, L2_gnn_edge_b, L2_gnn_gru_wih, L2_gnn_gru_whh, L2_gnn_gru_bih, L2_gnn_gru_bhh, L2_gnn_out_w, L2_gnn_out_b), axis=-1)
    x = _layernorm(x + _L3_gnn_ref(x, edge_index, edge_attr_16, edge_weight, L3_gnn_Wm1, L3_gnn_bm1, L3_gnn_Wm2, L3_gnn_bm2, L3_gnn_Wm3, L3_gnn_bm3, L3_gnn_Wu1, L3_gnn_bu1, L3_gnn_Wu2, L3_gnn_bu2, L3_gnn_Wi1, L3_gnn_bi1, L3_gnn_Wi2, L3_gnn_bi2), axis=-1)
    return x

_drawn_inputs = setup_inputs


def setup_inputs(seed=0):
    import zlib

    import numpy as np

    out = dict(_drawn_inputs(seed))
    spreads = {'L0_gnn_lin_bias': (0.0, 0.1),
     'L0_gnn_conv_bias': (0.0, 0.1),
     'L1_gnn_bias': (0.0, 0.1),
     'L2_gnn_out_b': (0.0, 0.1)}
    factors = {'edge_weight': 8.0,
     'L0_gnn_att': 51.953,
     'L1_gnn_att_src': 8.0,
     'L1_gnn_att_dst': 29.873,
     'L2_gnn_node_proj_b': 8.0,
     'L2_gnn_edge_W': 2.952,
     'L2_gnn_gru_wih': 2.71,
     'L2_gnn_gru_whh': 2.953,
     'L2_gnn_gru_bih': 4.42,
     'L2_gnn_gru_bhh': 8.0,
     'L3_gnn_Wm1': 8.0,
     'L3_gnn_bm1': 8.0,
     'L3_gnn_Wm2': 8.0,
     'L3_gnn_bm2': 8.0,
     'L3_gnn_Wm3': 8.0,
     'L3_gnn_bm3': 47.855,
     'L3_gnn_Wu1': 3.38,
     'L3_gnn_bu1': 8.0,
     'L3_gnn_bu2': 7.279,
     'L3_gnn_Wi1': 2.847,
     'L3_gnn_bi1': 4.427}
    for name, (base, spread) in spreads.items():
        noise = np.random.default_rng([zlib.crc32(name.encode()), seed]).standard_normal(out[name].shape)
        drawn = base * np.exp(spread * noise) if base else spread * noise
        out[name] = jnp.asarray(drawn.astype(out[name].dtype))
    for name, factor in factors.items():
        out[name] = (out[name] * factor).astype(out[name].dtype)
    return out
```

```python
from contextlib import ExitStack

import concourse.bass as bass
from concourse import mybir

F32 = mybir.dt.float32
I32 = mybir.dt.int32
ALU = mybir.AluOpType
ACT = mybir.ActivationFunctionType
AX_X = mybir.AxisListType.X

P = 128
D = 128
N = 50000
E = 50000
HEADS = 4
TYPES = 8
RADIAL = 50
CUTOFF = 10.0

Q = 4
CHUNK = P * Q
NCHUNK = -(-N // CHUNK)
NPAD = NCHUNK * CHUNK
COLS = NCHUNK * Q
KC = 14
NB = 4
ECHUNK = -(-E // (P * KC))
KE = ECHUNK * KC
assert ECHUNK % NB == 0 and NCHUNK % 2 == 0 and NPAD == P * KE
ROW = D + 2 * HEADS
TROW = D + HEADS
DEN = D
MAXC = D + HEADS
LOWEST = -1.0e30
SKIP = 1 << 20
EPS = 1e-5
MIN_NORM = 1e-15
MAX_NORM = 1.0 - 0.004
SLOPE = 0.2


def pair(i, b):
    return i * 2 + (b + 1)


class Own:

    def __init__(self, eng, sem, i=None, per=0):
        self.eng, self.sem, self.per, self.n = eng, sem, per, 0
        self.base = None if i is None else eng.snap(i * per)

    def mark(self, ins):
        self.n += 1
        ins.then_inc(self.sem, 1)
        return self.n

    def wait(self, n=None):
        n = self.n if n is None else n
        self.eng.wait_ge(self.sem, n if self.base is None else self.base + n)

    def link(self, ins):
        self.mark(ins)
        self.wait()

    def end(self):
        assert self.base is None or self.n == self.per, (self.sem, self.n, self.per)


def gated(eng, sem, value, gate):
    eng.wait_ge(sem, value)
    eng.sem_inc(gate, 1)


class Program:

    def __init__(self, nc, ins, out, ctx):
        self.nc, self.ins, self.out, self.ctx = nc, ins, out, ctx

        def table(name, shape, dt=F32):
            return nc.dram_tensor(name, shape, dt, kind="Internal").ap()

        self.edge_idx = table("edge_idx", [ECHUNK, P, 3, KC], I32)
        self.edge_fac = table("edge_fac", [ECHUNK, P, 2, KC])
        self.type_rows = table("type_rows", [KE, P])
        self.dist_rows = table("dist_rows", [KE, P])
        self.mx = table("mx", [NPAD, ROW])
        self.seg = table("seg", [NPAD, ROW])
        self.t = [table(f"t{n}", [NPAD, TROW]) for n in range(2)]
        self.ai = [table(f"ai{n}", [NPAD, HEADS]) for n in range(2)]
        self.x = [None] + [table(f"x{n}", [NPAD, D]) for n in (1, 2, 3)]
        self.ht = [table(f"ht{n}", [NCHUNK, P, CHUNK]) for n in range(2)]
        self.hr = [table(f"hr{n}", [NPAD, D]) for n in range(2)]
        self.ta = table("ta", [NPAD, D])
        self.tb = table("tb", [NPAD, D])

        self.ident = self.sb("ident", [P, P])
        self.ones = self.sb("ones", [P, P])
        self.half = self.sb("half", [P, 2 * Q])
        self.mhalf = self.sb("mhalf", [P, 2 * Q])
        self.w0aug = self.sb("w0aug", [P, ROW + 1])
        self.yrow = self.sb("yrow", [P, ROW])
        self.y2 = self.sb("y2", [P, 1])
        self.w1aug = self.sb("w1aug", [P, D + 2])
        self.bias0 = self.sb("bias0", [P, D])
        self.bias1 = self.sb("bias1", [P, D])
        self.outb = self.sb("outb", [P, D])
        self.sxx = self.sb("sxx", [P, COLS])
        self.smm = self.sb("smm", [P, COLS])
        self.sxy = self.sb("sxy", [P, COLS])
        self.alpha = self.sb("alpha", [P, COLS])
        self.beta = self.sb("beta", [P, COLS])
        self.bi2 = self.sb("bi2", [P, D])
        self.bab = self.sb("bab", [P, 2, D])
        self.bm2 = self.sb("bm2", [P, D])
        self.projw = self.sb("projw", [P, D])
        self.projb = self.sb("projb", [P, 1])
        self.wih = [self.sb(f"wih{n}", [P, 3 * D]) for n in range(2)]
        self.whh = [self.sb(f"whh{n}", [P, 3 * D]) for n in range(2)]
        self.gb = [self.sb(f"gb{n}", [P, 4]) for n in range(2)]
        self.outw = self.sb("outw", [P, D])
        self.wm1 = self.sb("wm1", [P, 2 * D])
        self.wr = self.sb("wr", [RADIAL, D])
        self.wm2 = self.sb("wm2", [P, D])
        self.wu1a = self.sb("wu1a", [P, D])
        self.wc = self.sb("wc", [P, D])
        self.bc = self.sb("bc", [2 * HEADS, D])
        self.bu1 = self.sb("bu1", [P, 2])
        self.wd = self.sb("wd", [P, D])
        self.bd = self.sb("bd", [P, 2])
        self.wi2 = self.sb("wi2", [P, D])
        self.noff = self.sb("noff", [RADIAL, 1])
        self.cross = self.sb("cross", [P, P])
        self.cross_t = self.sb("cross_t", [P, P])
        self.low_t = self.sb("low_t", [P, P])
        self.last = self.sb("last", [P, ROW])
        self.first_i = self.sb("first_i", [P, 1], I32)
        self.fix_i = self.sb("fix_i", [P, 1], I32)

    def sb(self, name, shape, dt=F32):
        return self.ctx.enter_context(self.nc.sbuf_tensor(name, shape, dt))

    def indirect_sem(self, name):
        return self.ctx.enter_context(self.nc.semaphore(name))

    def sem(self, name):
        s = self.sem_ctx.enter_context(self.nc.semaphore(name))
        self.sems.append(s)
        return s


def rows(table, c, q=Q):
    r = table.rearrange("(c p q) d -> c p q d", p=P, q=q)
    return r[bass.ds(c, 1)].rearrange("c p q d -> (c p) q d")



def phase_weights(g):
    nc, ins = g.nc, g.ins
    with ExitStack() as ctx:
        def sb(name, shape, dt=F32):
            return ctx.enter_context(nc.sbuf_tensor(name, shape, dt))

        w0 = sb("w_w0", [P, D])
        attm = sb("w_attm", [P, 2 * HEADS])
        linb = sb("w_linb", [P, 1])
        w1t = sb("w_w1t", [P, D])
        att1 = sb("w_att1", [P, 2])
        bih = [sb(f"w_bih{n}", [P, 3]) for n in range(2)]
        bhh = [sb(f"w_bhh{n}", [P, 3]) for n in range(2)]
        wm2 = sb("w_wm2", [P, D])
        wm3t = sb("w_wm3t", [P, D])
        wu1b = sb("w_wu1b", [P, D])
        bm3 = sb("w_bm3", [P, 1])
        bu1 = sb("w_bu1", [P, 1])
        wu2t = sb("w_wu2t", [P, D])
        wi1 = sb("w_wi1", [P, D])
        bu2 = sb("w_bu2", [P, 1])
        bi1 = sb("w_bi1", [P, 1])
        wi2 = sb("w_wi2", [P, D])
        zeros = sb("w_zeros", [P, P])
        rim = sb("w_rim", [P, ROW])
        b2 = sb("w_b2", [P, 1])
        sc = sb("w_sc", [P, 8])
        y = sb("w_y", [P, 1])
        ybc = sb("w_ybc", [P, P])
        offi = sb("w_offi", [RADIAL, 1], I32)
        offf = sb("w_offf", [RADIAL, 1])
        rowz = sb("w_rowz", [P, NPAD // P // 49 * ROW])
        pw = ctx.enter_context(nc.psum_tensor("w_pw", [P, 8, 512], F32))

        loaded = g.sem("w_loaded")
        made = g.sem("w_made")
        norm2 = g.sem("w_norm2")
        root = g.sem("w_root")
        tanh = g.sem("w_tanh")
        yready = g.sem("w_yready")
        folded = g.sem("w_folded")
        ch = g.sem("w_chain")
        chp = g.sem("w_chain_pool")
        zeroed = g.sem("w_zeroed")
        zrow = g.sem("w_zrow")
        done = g.sem("w_done")

        loads = [
            (g.w0aug[:, 0:D], ins["w0t"]), (w0[:, :], ins["w0"]), (attm[:, :], ins["attm"]),
            (linb[:, :], ins["lin_bias"]), (g.w1aug[:, 0:D], ins["w1"]), (w1t[:, :], ins["w1t"]),
            (att1[:, :], ins["att1"]), (g.projw[:, :], ins["projwt"]), (g.projb[:, :], ins["projb"]),
            (g.wih[0][:, :], ins["wiht"][0]), (g.wih[1][:, :], ins["wiht"][1]),
            (g.whh[0][:, :], ins["whht"][0]), (g.whh[1][:, :], ins["whht"][1]),
            (bih[0][:, :], ins["biht"][0]), (bih[1][:, :], ins["biht"][1]),
            (bhh[0][:, :], ins["bhht"][0]), (bhh[1][:, :], ins["bhht"][1]),
            (g.outw[:, :], ins["outwt"]), (g.wm1[:, 0:D], ins["wm1"][0:D]),
            (g.wm1[:, D:2 * D], ins["wm1"][D:2 * D]), (g.wr[:, :], ins["wm1"][2 * D:2 * D + RADIAL]),
            (wm2[:, :], ins["wm2"]), (wm3t[:, :], ins["wm3t"]), (g.wu1a[:, :], ins["wu1"][0:D]),
            (wu1b[:, :], ins["wu1"][D:2 * D]), (bm3[:, :], ins["bm3"]), (bu1[:, :], ins["bu1"]),
            (wu2t[:, :], ins["wu2t"]), (wi1[:, :], ins["wi1"]), (bu2[:, :], ins["bu2"]),
            (bi1[:, :], ins["bi1"]), (wi2[:, :], ins["wi2"]),
        ]
        for tile, name in ((g.bias0, "conv_bias"), (g.bias1, "bias1"), (g.outb, "out_b"),
                           (g.bi2, "bi2"), (g.bab[:, 1, :], "bm1"), (g.bm2, "bm2")):
            loads.append((tile if name == "bm1" else tile[:, :], ins[name].to_broadcast([P, D])))

        with nc.Block() as block:
            @block.sync
            def _(sp):
                for dst, src in loads:
                    sp.dma_start(dst, src).then_inc(loaded, 16)
                sp.wait_ge(loaded, 16 * len(loads))

            @block.gpsimd
            def _(pool):
                own = Own(pool, chp)
                pool.memset(g.ones[:, :], 1.0).then_inc(made, 1)
                pool.memset(g.half[:, :], 0.5).then_inc(made, 1)
                pool.memset(g.mhalf[:, :], -0.5).then_inc(made, 1)
                pool.iota(offi[:, :], pattern=[[0, 1]], base=0, channel_multiplier=1).then_inc(made, 1)
                own.link(pool.memset(g.ident[:, :], 0.0))
                pool.affine_select(out=g.ident[:, :], in_=g.ident[:, :], compare_op=ALU.not_equal,
                                   fill=1.0, base=0, pattern=[[-1, P]], channel_multiplier=1).then_inc(made, 1)
                pool.wait_ge(norm2, 2)
                pool.wait_ge(made, 5)
                pool.tensor_tensor(sc[:, 1:2], sc[:, 0:1], g.half[:, 0:1], ALU.pow).then_inc(root, 1)

            @block.scalar
            def _(act):
                act.wait_ge(zrow, 1)
                zr = g.seg.rearrange("(n p r) d -> n p (r d)", n=49, p=P)
                for n in range(49):
                    act.dma_start(zr[n], rowz[:, :]).then_inc(zeroed, 16)
                act.wait_ge(root, 1)
                nc.scalar.activation(sc[:, 2:3], sc[:, 1:2], ACT.Tanh).then_inc(tanh, 1)
                act.wait_ge(zeroed, 16 * 49)

            @block.tensor
            def _(pe):
                pe.wait_ge(ch, 1)
                pe.wait_ge(made, 5)
                nc.tensor.matmul(pw[:, 0, 0:1], g.ones[:, :], b2[:, :], start=True, stop=True).then_inc(norm2, 1)
                pe.wait_ge(loaded, 16 * len(loads))
                mm = nc.tensor.matmul
                mm(pw[:, 1, 0:8], w0[:, :], attm[:, :], start=True, stop=True)
                mm(pw[:, 2, 0:2], w1t[:, :], att1[:, :], start=True, stop=True)
                mm(pw[:, 3, 0:D], wm3t[:, :], wu1b[:, :], start=True, stop=True)
                mm(pw[0:1, 4, 0:D], bm3[:, :], wu1b[:, :], start=True, stop=True)
                mm(pw[:, 5, 0:D], wu2t[:, :], wi1[:, :], start=True, stop=True)
                mm(pw[:, 6, 0:1], wi1[:, :], bu2[:, :], start=True, stop=True).then_inc(folded, 1)
                pe.wait_ge(yready, 1)
                mm(pw[:, 7, 0:1], w0[:, :], y[:, :], start=True, stop=True).then_inc(folded, 1)
                mm(pw[:, 0, 0:ROW], ybc[:, :], rim[:, :], start=True, stop=True)
                mm(pw[:, 0, 256:257], ybc[:, :], y[:, :], start=True, stop=True).then_inc(folded, 1)

            @block.vector
            def _(v):
                own = Own(v, ch)
                v.wait_ge(loaded, 16 * len(loads))
                own.mark(nc.vector.tensor_tensor(b2[:, :], linb[:, :], linb[:, :], ALU.mult))
                own.link(nc.vector.memset(rowz[:, :], 0.0))
                nc.vector.memset(rowz[:, :].rearrange("p (r d) -> p r d", d=ROW)[:, :, MAXC:ROW],
                                 LOWEST).then_inc(zrow, 1)
                v.wait_ge(made, 5)
                own.mark(nc.vector.tensor_copy(offf[:, :], offi[:, :]))
                own.mark(nc.vector.tensor_copy(rim[:, 0:D], g.ident[:, :]))
                own.mark(nc.vector.tensor_copy(rim[:, D:ROW], attm[:, :]))
                own.wait()
                own.mark(nc.vector.tensor_scalar(g.noff[:, :], offf[:, :], -CUTOFF / (RADIAL - 1), None, ALU.mult))
                for n in range(2):
                    own.link(nc.vector.tensor_tensor(sc[:, 3:5], bih[n][:, 0:2], bhh[n][:, 0:2], ALU.add))
                    own.mark(nc.vector.tensor_scalar(g.gb[n][:, 0:2], sc[:, 3:5], 0.5, None, ALU.mult))
                    own.mark(nc.vector.tensor_copy(g.gb[n][:, 2:3], bih[n][:, 2:3]))
                    own.mark(nc.vector.tensor_copy(g.gb[n][:, 3:4], bhh[n][:, 2:3]))
                    own.wait()
                own.mark(nc.vector.tensor_scalar(g.wm2[:, :], wm2[:, :], 0.5, None, ALU.mult))
                own.mark(nc.vector.tensor_scalar(g.wi2[:, :], wi2[:, :], 0.5, None, ALU.mult))
                own.mark(nc.vector.tensor_copy(g.bu1[:, 0:1], bu1[:, :]))
                own.mark(nc.vector.tensor_scalar(g.bu1[:, 1:2], bu1[:, :], 0.5, None, ALU.mult))
                own.mark(nc.vector.memset(g.bc[:, :], 0.0))
                own.mark(nc.vector.memset(g.bab[:, 0, :], 0.0))
                own.wait()
                v.wait_ge(norm2, 1)
                nc.vector.tensor_scalar(sc[:, 0:1], pw[:, 0, 0:1], MIN_NORM ** 2, None, ALU.max).then_inc(norm2, 1)
                v.wait_ge(folded, 1)
                own.mark(nc.vector.tensor_copy(g.w0aug[:, D:ROW], pw[:, 1, 0:8]))
                own.mark(nc.vector.tensor_copy(g.w1aug[:, D:D + 2], pw[:, 2, 0:2]))
                own.mark(nc.vector.tensor_scalar(g.wc[:, :], pw[:, 3, 0:D], 0.5, None, ALU.mult))
                own.mark(nc.vector.tensor_copy(g.bc[0:1, :], pw[0:1, 4, 0:D]))
                own.mark(nc.vector.tensor_scalar(g.wd[:, :], pw[:, 5, 0:D], 0.5, None, ALU.mult))
                own.link(nc.vector.tensor_tensor(g.bd[:, 0:1], pw[:, 6, 0:1], bi1[:, :], ALU.add))
                own.mark(nc.vector.tensor_scalar(g.bd[:, 1:2], g.bd[:, 0:1], 0.5, None, ALU.mult))
                v.wait_ge(tanh, 1)
                own.mark(nc.vector.tensor_scalar(sc[:, 5:6], sc[:, 2:3], MAX_NORM, None, ALU.min))
                own.link(nc.vector.reciprocal(sc[:, 6:7], sc[:, 1:2]))
                own.link(nc.vector.tensor_tensor(sc[:, 7:8], sc[:, 5:6], sc[:, 6:7], ALU.mult))
                own.link(nc.vector.tensor_tensor(y[:, :], sc[:, 7:8], linb[:, :], ALU.mult))
                nc.vector.tensor_scalar(ybc[:, :], g.ones[:, :], y[:, 0:1], None, ALU.mult).then_inc(yready, 1)
                v.wait_ge(folded, 3)
                own.mark(nc.vector.tensor_copy(g.w0aug[:, ROW:ROW + 1], pw[:, 7, 0:1]))
                own.mark(nc.vector.tensor_copy(g.yrow[:, :], pw[:, 0, 0:ROW]))
                own.mark(nc.vector.tensor_copy(g.y2[:, :], pw[:, 0, 256:257]))
                own.wait()



def phase_edges(g):
    nc, ins = g.nc, g.ins
    with ExitStack() as ctx:
        def sb(name, shape, dt=F32):
            return ctx.enter_context(nc.sbuf_tensor(name, shape, dt))

        src_i = sb("e_src", [P, KE], I32)
        dst_i = sb("e_dst", [P, KE], I32)
        typ_i = sb("e_typ", [P, KE], I32)
        next_i = sb("e_nexti", [P, 1], I32)
        dist = sb("e_dist", [P, KE])
        dst = sb("e_dstf", [P, KE + 1])
        typ = sb("e_typf", [P, KE])
        same = sb("e_same", [P, KE])
        fac = sb("e_fac", [P, 2, KE])
        sct = sb("e_sct", [P, KE])
        sct_i = sb("e_scti", [P, KE], I32)
        sm = sb("e_sm", [P, 4])
        dg = sb("e_dg", [P, P])
        firstb = sb("e_firstb", [P, P])
        tri = sb("e_tri", [P, P])
        rowsb = sb("e_rows", [KE // 4, 2, 4, P])
        pt = ctx.enter_context(nc.psum_tensor("e_pt", [P, 4, 512], F32))
        loaded = g.sem("e_loaded")
        pre = g.sem("e_pre")
        cast = g.sem("e_cast")
        trid = g.sem("e_trid")
        turned = g.sem("e_turned")
        ch = g.sem("e_chain")
        ready = g.sem("e_ready")
        stored = g.sem("e_stored")
        K4 = KE // 4
        with nc.Block() as block:
            @block.sync
            def _(sp):
                sp.dma_start(src_i[:, :], ins["src"]).then_inc(loaded, 16)
                sp.dma_start(dst_i[:, :], ins["dst"]).then_inc(loaded, 16)
                sp.dma_start(typ_i[:, :], ins["etype"]).then_inc(loaded, 16)
                sp.dma_start(dist[:, :], ins["dist"]).then_inc(loaded, 16)
                sp.wait_ge(pre, 1)
                with nc.allow_non_contiguous_dma(reason="one word of each partition"):
                    sp.dma_start(next_i[0:P - 1, :], ins["dst"][1:P, 0:1]).then_inc(loaded, 16)
                sp.wait_ge(ready, 2)
                for c in range(ECHUNK):
                    k = slice(c * KC, (c + 1) * KC)
                    sp.dma_start(g.edge_idx[c, :, 0, :], src_i[:, k]).then_inc(stored, 16)
                    sp.dma_start(g.edge_idx[c, :, 1, :], dst_i[:, k]).then_inc(stored, 16)
                    sp.dma_start(g.edge_idx[c, :, 2, :], sct_i[:, k]).then_inc(stored, 16)
                    sp.dma_start(g.edge_fac[c], fac[:, :, k]).then_inc(stored, 16)
                sp.wait_ge(ready, 3)
                for n, t in enumerate((g.type_rows, g.dist_rows)):
                    sp.dma_start(t.rearrange("(a k) p -> k a p", a=4), rowsb[:, n, :, :]).then_inc(stored, 16)
                sp.wait_ge(stored, 16 * (4 * ECHUNK + 2))

            @block.gpsimd
            def _(pool):
                own = Own(pool, cast)
                own.link(pool.memset(tri[:, :], 1.0))
                pool.affine_select(out=tri[:, :], in_=tri[:, :], compare_op=ALU.is_gt, fill=0.0, base=0,
                                   pattern=[[1, P]], channel_multiplier=-1).then_inc(trid, 1)

            @block.tensor
            def _(pe):
                pe.wait_ge(ready, 1)
                for n, t in enumerate((typ, dist)):
                    for a in range(4):
                        last = nc.tensor.transpose(pt[0:K4, n, a * P:(a + 1) * P], t[:, a * K4:(a + 1) * K4],
                                                   g.ident[:, :])
                last.then_inc(turned, 1)
                nc.tensor.matmul(pt[:, 2, 0:P], g.ones[:, :], dg[:, :], start=True, stop=True).then_inc(turned, 1)
                pe.wait_ge(ready, 4)
                nc.tensor.transpose(pt[:, 3, 0:P], g.cross[:, :], g.ident[:, :]).then_inc(turned, 1)

            @block.vector
            def _(v):
                own = Own(v, ch)
                nc.vector.memset(next_i[:, :], NPAD).then_inc(pre, 1)
                v.wait_ge(loaded, 16 * 5)
                own.mark(nc.vector.tensor_copy(typ[:, :], typ_i[:, :]))
                own.mark(nc.vector.tensor_copy(dst[:, 0:KE], dst_i[:, :]))
                own.mark(nc.vector.tensor_copy(dst[:, KE:KE + 1], next_i[:, :]))
                own.mark(nc.vector.tensor_copy(g.first_i[:, :], dst_i[:, 0:1]))
                own.wait()
                nc.vector.tensor_scalar(dg[:, :], g.ident[:, :], dst[:, 0:1], None, ALU.mult).then_inc(ready, 1)
                own.link(nc.vector.tensor_tensor(same[:, :], dst[:, 0:KE], dst[:, 1:KE + 1], ALU.is_equal))
                own.link(nc.vector.scalar_tensor_tensor(sct[:, :], same[:, :], float(SKIP), dst[:, 0:KE],
                                                        ALU.mult, ALU.add))
                own.mark(nc.vector.tensor_copy(sct_i[:, :], sct[:, :]))
                own.mark(nc.vector.memset(fac[:, 0, 0:1], 0.0))
                own.link(nc.vector.tensor_copy(fac[:, 0, 1:KE], same[:, 0:KE - 1]))
                nc.vector.tensor_scalar(fac[:, 1, :], fac[:, 0, :], -LOWEST, LOWEST, ALU.mult,
                                        ALU.add).then_inc(ready, 1)
                v.wait_ge(turned, 1)
                own.mark(nc.vector.tensor_copy(rowsb[:, 0, :, :], pt[0:K4, 0, :].rearrange("k (a p) -> k a p", a=4)))
                nc.vector.tensor_copy(rowsb[:, 1, :, :],
                                      pt[0:K4, 1, :].rearrange("k (a p) -> k a p", a=4)).then_inc(ready, 1)
                v.wait_ge(turned, 2)
                v.wait_ge(trid, 1)
                own.link(nc.vector.tensor_copy(firstb[:, :], pt[:, 2, 0:P]))
                nc.vector.scalar_tensor_tensor(g.cross[:, :], firstb[:, :], dst[:, KE - 1:KE], tri[:, :],
                                               ALU.is_equal, ALU.mult).then_inc(ready, 1)
                v.wait_ge(turned, 3)
                own.link(nc.vector.tensor_copy(g.cross_t[:, :], pt[:, 3, 0:P]))
                own.mark(nc.vector.tensor_scalar(g.low_t[:, :], g.cross_t[:, :], -LOWEST, LOWEST, ALU.mult, ALU.add))
                own.link(nc.vector.tensor_tensor(sm[:, 0:1], dst[:, 0:1], dst[:, KE:KE + 1], ALU.is_equal))
                own.link(nc.vector.scalar_tensor_tensor(sm[:, 1:2], sm[:, 0:1], float(SKIP), dst[:, 0:1],
                                                        ALU.mult, ALU.add))
                own.link(nc.vector.tensor_copy(g.fix_i[:, :], sm[:, 1:2]))



def phase_product(g):
    nc = g.nc
    with ExitStack() as ctx:
        def sb(name, shape, dt=F32):
            return ctx.enter_context(nc.sbuf_tensor(name, shape, dt))

        x = [sb(f"p_x{b}", [P, Q, D]) for b in range(2)]
        xt = [sb(f"p_xt{b}", [P, CHUNK]) for b in range(2)]
        mx = [sb(f"p_mx{b}", [P, Q, ROW]) for b in range(2)]
        x2 = [sb(f"p_x2{b}", [P, Q, D]) for b in range(2)]
        m2 = [sb(f"p_m2{b}", [P, Q, D]) for b in range(2)]
        pt = [ctx.enter_context(nc.psum_tensor(f"p_pt{b}", [P, 512], F32)) for b in range(2)]
        pm = [ctx.enter_context(nc.psum_tensor(f"p_pm{b}", [P, 2, 512], F32)) for b in range(2)]
        loaded = [g.sem(f"p_loaded{b}") for b in range(2)]
        turned = g.sem("p_turned")
        copied = g.sem("p_copied")
        product = g.sem("p_product")
        squared = g.sem("p_squared")
        moved = g.sem("p_moved")
        summed = g.sem("p_summed")
        stored = [g.sem(f"p_stored{b}") for b in range(2)]
        freed = g.sem("p_freed")
        gate = g.sem("p_gate")
        half = NCHUNK // 2
        with nc.Block() as block:
            @block.sync
            def _(sp):
                with sp.Fori(0, half) as i:
                    for b in range(2):
                        sp.wait_ge(summed, pair(i, b))
                        sp.dma_start(x[b][:, :, :], rows(g.ins["x"], i * 2 + b)).then_inc(loaded[b], 16)

            @block.gpsimd
            def _(pool):
                with pool.Fori(0, half) as i:
                    for b in range(2):
                        gated(pool, stored[b], i * 16 + 16, freed)

            @block.tensor
            def _(pe):
                with pe.Fori(0, half) as i:
                    for b in range(2):
                        pe.wait_ge(loaded[b], i * 16 + 16)
                        pe.wait_ge(copied, pair(i, b))
                        for q in range(Q):
                            last = nc.tensor.transpose(pt[b][:, q * P:(q + 1) * P], x[b][:, q, :], g.ident[:, :])
                        last.then_inc(turned, 1)
                    for b in range(2):
                        pe.wait_ge(copied, pair(i, b) + 2)
                        pe.wait_ge(summed, pair(i, b))
                        for q in range(Q):
                            o = (q % 2) * (ROW + 1)
                            last = nc.tensor.matmul(pm[b][:, q // 2, o:o + ROW + 1], xt[b][:, q * P:(q + 1) * P],
                                                    g.w0aug[:, :], start=True, stop=True)
                        last.then_inc(product, 1)

            @block.scalar
            def _(act):
                act.sem_inc(copied, 2)
                with act.Fori(0, half) as i:
                    for b in range(2):
                        act.wait_ge(turned, pair(i, b))
                        nc.scalar.copy(xt[b][:, :], pt[b][:, :]).then_inc(copied, 1)
                    for b in range(2):
                        act.wait_ge(summed, pair(i, b))
                        act.wait_ge(loaded[b], i * 16 + 16)
                        nc.scalar.activation(x2[b][:, :, :], x[b][:, :, :], ACT.Square)
                        act.wait_ge(moved, pair(i, b))
                        nc.scalar.activation(m2[b][:, :, :], mx[b][:, :, 0:D], ACT.Square).then_inc(squared, 1)
                        act.dma_start(rows(g.mx, i * 2 + b), mx[b][:, :, :]).then_inc(stored[b], 16)

            @block.vector
            def _(v):
                v.sem_inc(summed, 2)
                v.sem_inc(freed, 2)
                with v.Fori(0, half) as i:
                    for b in range(2):
                        col = bass.ds(i * (2 * Q) + b * Q, Q)
                        v.wait_ge(product, pair(i, b))
                        v.wait_ge(freed, pair(i, b))
                        view = pm[b][:, :, 0:2 * (ROW + 1)].rearrange("p a (s c) -> p a s c", s=2)
                        nc.vector.tensor_copy(mx[b][:, :, :].rearrange("p (a s) c -> p a s c", s=2),
                                              view[:, :, :, 0:ROW]).then_inc(moved, 1)
                        v.tensor_scalar(g.sxy[:, col].rearrange("p (a s) -> p a s", s=2), view[:, :, :, ROW],
                                        1.0, None, ALU.mult)
                        v.wait_ge(squared, pair(i, b))
                        v.sem_inc(gate, 1)
                        nc.vector.tensor_reduce(g.sxx[:, col], x2[b][:, :, :], AX_X, ALU.add)
                        nc.vector.tensor_reduce(g.smm[:, col], m2[b][:, :, :], AX_X, ALU.add).then_inc(summed, 1)



def phase_map(g):
    nc = g.nc
    with ExitStack() as ctx:
        t = [ctx.enter_context(nc.sbuf_tensor(f"m_t{n}", [P, COLS], F32)) for n in range(14)]
        asked = g.sem("m_asked")
        rooted = g.sem("m_rooted")
        logged = g.sem("m_logged")
        tanhed = g.sem("m_tanhed")
        ch = g.sem("m_chain")
        tanh_asked = g.sem("m_tanh_asked")
        log_asked = g.sem("m_log_asked")
        xn, mn, n2, ratio, lg = t[0], t[1], t[2], t[3], t[4]
        xsq = t[11]
        with nc.Block() as block:
            @block.scalar
            def _(act):
                act.wait_ge(asked, 2)
                nc.scalar.activation(xn[:, :], t[6][:, :], ACT.Sqrt)
                nc.scalar.activation(mn[:, :], t[7][:, :], ACT.Sqrt).then_inc(rooted, 1)
                act.wait_ge(log_asked, 1)
                nc.scalar.activation(lg[:, :], ratio[:, :], ACT.Ln).then_inc(logged, 1)
                act.wait_ge(tanh_asked, 1)
                nc.scalar.activation(t[5][:, :], t[5][:, :], ACT.Tanh).then_inc(tanhed, 1)
                act.wait_ge(asked, 3)
                nc.scalar.activation(n2[:, :], xsq[:, :], ACT.Sqrt).then_inc(rooted, 1)
                act.wait_ge(log_asked, 2)
                nc.scalar.activation(lg[:, :], ratio[:, :], ACT.Ln).then_inc(logged, 1)

            @block.vector
            def _(v):
                own = Own(v, ch)

                def tt(o, a, b, op):
                    own.link(nc.vector.tensor_tensor(o[:, :], a[:, :], b[:, :], op))

                def ts(o, a, s1, op1, s2=None, op2=ALU.bypass):
                    own.link(nc.vector.tensor_scalar(o[:, :], a[:, :], s1, s2, op1, op2))

                def stt(o, a, s, b, op1, op2):
                    own.link(nc.vector.scalar_tensor_tensor(o[:, :], a[:, :], s, b[:, :], op1, op2))

                def ask(o, a, s1, op1, sem):
                    nc.vector.tensor_scalar(o[:, :], a[:, :], s1, None, op1).then_inc(sem, 1)

                def artanh(o, n, call, a, b, c):
                    ts(a, n, 1.0 - 1e-7, ALU.min)
                    ts(b, a, -1.0, ALU.mult, 1.0, ALU.add)
                    own.link(nc.vector.reciprocal(b[:, :], b[:, :]))
                    stt(ratio, a, 1.0, b, ALU.add, ALU.mult)
                    v.sem_inc(log_asked, 1)
                    tt(b, a, a, ALU.mult)
                    ts(c, b, 1.0 / 15, ALU.mult, 1.0 / 13, ALU.add)
                    for n_ in (11, 9, 7, 5, 3, 1):
                        tt(c, c, b, ALU.mult)
                        ts(c, c, 1.0 / n_, ALU.add)
                    tt(c, c, a, ALU.mult)
                    ts(b, a, 0.3, ALU.is_lt)
                    tt(c, c, b, ALU.mult)
                    ts(b, b, -0.5, ALU.mult, 0.5, ALU.add)
                    v.wait_ge(logged, call)
                    tt(b, b, lg, ALU.mult)
                    tt(o, b, c, ALU.add)

                def newton(r, square, w):
                    own.link(nc.vector.reciprocal(w[:, :], r[:, :]))
                    tt(w, w, square, ALU.mult)
                    tt(w, w, r, ALU.add)
                    ts(r, w, 0.5, ALU.mult)

                ask(t[6], g.sxx, MIN_NORM ** 2, ALU.max, asked)
                ask(t[7], g.smm, MIN_NORM ** 2, ALU.max, asked)
                v.wait_ge(rooted, 1)
                newton(xn, t[6], t[10])
                newton(mn, t[7], t[10])
                arg, rx, rm, c, cm = t[5], t[6], t[7], t[8], t[9]
                artanh(arg, xn, 1, t[10], t[11], t[12])
                own.link(nc.vector.reciprocal(rx[:, :], xn[:, :]))
                own.link(nc.vector.reciprocal(rm[:, :], mn[:, :]))
                tt(rx, rx, mn, ALU.mult)
                tt(arg, arg, rx, ALU.mult)
                v.sem_inc(tanh_asked, 1)
                v.wait_ge(tanhed, 1)
                ts(c, arg, MAX_NORM, ALU.min)
                tt(cm, c, rm, ALU.mult)
                x2, xy2, a, b, den, xy = t[10], t[11], t[12], t[13], t[6], t[7]
                tt(x2, c, c, ALU.mult)
                tt(xy, cm, g.sxy, ALU.mult)
                ts(a, xy, 2.0, ALU.mult, 1.0, ALU.add)
                stt(den, x2, g.y2[:, 0:1], a, ALU.mult, ALU.add)
                ts(den, den, MIN_NORM, ALU.max)
                ts(a, a, g.y2[:, 0:1], ALU.add)
                ts(b, x2, -1.0, ALU.mult, 1.0, ALU.add)
                own.link(nc.vector.reciprocal(den[:, :], den[:, :]))
                tt(a, a, den, ALU.mult)
                tt(b, b, den, ALU.mult)
                tt(xy2, a, xy, ALU.mult)
                ts(xy2, xy2, 2.0, ALU.mult)
                stt(xy2, b, g.y2[:, 0:1], xy2, ALU.mult, ALU.add)
                tt(xy2, xy2, b, ALU.mult)
                tt(x2, x2, a, ALU.mult)
                tt(x2, x2, a, ALU.mult)
                tt(n2, x2, xy2, ALU.add)
                ask(xsq, n2, MIN_NORM ** 2, ALU.max, asked)
                v.wait_ge(rooted, 2)
                newton(n2, xsq, x2)
                tt(cm, cm, a, ALU.mult)
                ts(c, n2, MAX_NORM, ALU.min)
                artanh(rx, c, 2, t[10], t[11], t[12])
                own.link(nc.vector.reciprocal(n2[:, :], n2[:, :]))
                tt(rx, rx, n2, ALU.mult)
                own.mark(nc.vector.tensor_tensor(g.alpha[:, :], rx[:, :], cm[:, :], ALU.mult))
                own.mark(nc.vector.tensor_tensor(g.beta[:, :], rx[:, :], b[:, :], ALU.mult))
                own.wait()


def phase_log(g):
    nc = g.nc
    with ExitStack() as ctx:
        def sb(name, shape, dt=F32):
            return ctx.enter_context(nc.sbuf_tensor(name, shape, dt))

        mx = [sb(f"l_mx{b}", [P, Q, ROW]) for b in range(2)]
        by = [sb(f"l_by{b}", [P, Q, ROW]) for b in range(2)]
        ab = [sb(f"l_ab{b}", [P, 2, Q]) for b in range(2)]
        r = [sb(f"l_r{b}", [P, Q, ROW]) for b in range(2)]
        loaded = [g.sem(f"l_loaded{b}") for b in range(2)]
        factors = g.sem("l_factors")
        scaled = g.sem("l_scaled")
        summed = g.sem("l_summed")
        stored = [g.sem(f"l_stored{b}") for b in range(2)]
        freed = g.sem("l_freed")
        gate = g.sem("l_gate")
        half = NCHUNK // 2
        with nc.Block() as block:
            @block.sync
            def _(sp):
                with sp.Fori(0, half) as i:
                    for b in range(2):
                        sp.wait_ge(summed, pair(i, b))
                        sp.dma_start(mx[b][:, :, :], rows(g.mx, i * 2 + b)).then_inc(loaded[b], 16)

            @block.gpsimd
            def _(pool):
                with pool.Fori(0, half) as i:
                    for b in range(2):
                        gated(pool, stored[b], i * 32 + 32, freed)

            @block.scalar
            def _(act):
                with act.Fori(0, half) as i:
                    for b in range(2):
                        act.wait_ge(factors, pair(i, b))
                        for q in range(Q):
                            last = nc.scalar.activation(by[b][:, q, :], g.yrow[:, :], ACT.Copy,
                                                        scale=ab[b][:, 1, q:q + 1])
                        last.then_inc(scaled, 1)
                    for b in range(2):
                        act.wait_ge(summed, pair(i, b) + 2)
                        act.dma_start(rows(g.t[0], i * 2 + b), r[b][:, :, 0:TROW]).then_inc(stored[b], 16)
                        act.dma_start(rows(g.ai[0], i * 2 + b), r[b][:, :, TROW:ROW]).then_inc(stored[b], 16)

            @block.vector
            def _(v):
                v.sem_inc(summed, 2)
                v.sem_inc(freed, 2)
                with v.Fori(0, half) as i:
                    for b in range(2):
                        col = bass.ds(i * (2 * Q) + b * Q, Q)
                        gated(v, summed, pair(i, b), gate)
                        nc.vector.tensor_copy(ab[b][:, 0, :], g.alpha[:, col])
                        nc.vector.tensor_copy(ab[b][:, 1, :], g.beta[:, col]).then_inc(factors, 1)
                    for b in range(2):
                        v.wait_ge(freed, pair(i, b))
                        v.wait_ge(loaded[b], i * 16 + 16)
                        v.wait_ge(scaled, pair(i, b))
                        for q in range(Q):
                            last = nc.vector.scalar_tensor_tensor(r[b][:, q, :], mx[b][:, q, :], ab[b][:, 0, q:q + 1],
                                                                  by[b][:, q, :], ALU.mult, ALU.add)
                        last.then_inc(summed, 1)



def nth(i, b):
    return i * NB + (b + 1)


def edge_lists(g, sp, idx, fac, listed, unlisted, more=None):
    with sp.Fori(0, ECHUNK // NB) as i:
        for b in range(NB):
            sp.wait_ge(unlisted, nth(i, b))
            c = bass.ds(i * NB + b, 1)
            sp.dma_start(idx[b][:, :, :], g.edge_idx[c].rearrange("c p n k -> (c p) n k")).then_inc(listed[b], 16)
            sp.dma_start(fac[b][:, :, :], g.edge_fac[c].rearrange("c p n k -> (c p) n k")).then_inc(listed[b], 16)
            if more is not None:
                more(i, b)


def edge_moves(g, pool, gathers, r, idx, listed, per_list, scattered, stated, unlisted, gate):
    passes = ECHUNK // NB

    def gather(i, b):
        gated(pool, listed[b], i * per_list + per_list, gate)
        gathers(b)

    def scatter(i, b):
        gated(pool, stated, nth(i, b), gate)
        for k in range(KC):
            pool.indirect_dma_start(
                out=g.seg, out_offset=bass.IndirectOffsetOnAxis(ap=idx[b][:, 2, k:k + 1], axis=0),
                in_=r[b][:, k, :], in_offset=None, bounds_check=NPAD - 1, oob_is_err=False
            ).then_inc(scattered[b], 16)

    def release(i, b):
        gated(pool, scattered[b], i * (16 * KC) + 16 * KC, unlisted)

    for b in range(3):
        gather(0, b)
    scatter(0, 0)
    with pool.Fori(0, passes - 1) as i:
        for b in range(NB):
            ahead = b + 3
            gather(i + ahead // NB, ahead % NB)
            release(i, b)
            scatter(i + (b + 1) // NB, (b + 1) % NB)
    last = passes - 1
    gather(last, 3)
    for b in range(NB):
        release(last, b)
        if b + 1 < NB:
            scatter(last, b + 1)


def phase_attend(g, layer, heads):
    nc = g.nc
    dh = D // heads
    pre = f"a{layer}_"
    with ExitStack() as ctx:
        def sb(name, shape, dt=F32):
            return ctx.enter_context(nc.sbuf_tensor(pre + name, shape, dt))

        idx = [sb(f"idx{b}", [P, 3, KC], I32) for b in range(NB)]
        fac = [sb(f"fac{b}", [P, 2, KC]) for b in range(NB)]
        r = [sb(f"r{b}", [P, KC, ROW]) for b in range(NB)]
        ai = [sb(f"ai{b}", [P, KC, HEADS]) for b in range(NB)]
        s = sb("s", [P, heads, KC])
        mx = sb("mx", [P, heads, KC + 1])
        dn = sb("dn", [P, heads, KC + 1])
        e = sb("e", [P, 2, heads, KC])
        tmp = sb("tmp", [P, D])
        listed = [g.sem(pre + f"listed{b}") for b in range(NB)]
        gathered = [g.indirect_sem(pre + f"gathered{b}") for b in range(NB)]
        scattered = [g.indirect_sem(pre + f"scattered{b}") for b in range(NB)]
        asked = g.sem(pre + "asked")
        raised = g.sem(pre + "raised")
        stated = g.sem(pre + "stated")
        unlisted = g.sem(pre + "unlisted")
        cleared = g.sem(pre + "cleared")
        ch = g.sem(pre + "chain")
        gate = g.sem(pre + "gate")
        passes = ECHUNK // NB
        with nc.Block() as block:
            @block.sync
            def _(sp):
                edge_lists(g, sp, idx, fac, listed, unlisted)

            @block.gpsimd
            def _(pool):
                pool.sem_inc(unlisted, NB)
                pool.wait_ge(cleared, 1)

                def gathers(b):
                    for k in range(KC):
                        pool.indirect_dma_start(
                            out=r[b][:, k, 0:TROW], out_offset=None, in_=g.t[layer],
                            in_offset=bass.IndirectOffsetOnAxis(ap=idx[b][:, 0, k:k + 1], axis=0)
                        ).then_inc(gathered[b], 16)
                        pool.indirect_dma_start(
                            out=ai[b][:, k, :], out_offset=None, in_=g.ai[layer],
                            in_offset=bass.IndirectOffsetOnAxis(ap=idx[b][:, 1, k:k + 1], axis=0)
                        ).then_inc(gathered[b], 16)

                edge_moves(g, pool, gathers, r, idx, listed, 32, scattered, stated, unlisted, gate)

            @block.scalar
            def _(act):
                with act.Fori(0, passes) as i:
                    for b in range(NB):
                        act.wait_ge(asked, nth(i, b))
                        nc.scalar.activation(e[:, :, :, :], e[:, :, :, :], ACT.Exp).then_inc(raised, 1)

            @block.vector
            def _(v):
                for b in range(NB):
                    nc.vector.memset(r[b][:, :, :], 0.0)
                nc.vector.memset(dn[:, :, :], 0.0)
                nc.vector.memset(mx[:, :, :], LOWEST).then_inc(cleared, 1)
                v.wait_ge(cleared, 1)
                per = NB * (7 + 2 * heads + (2 if heads > 1 else 1) * KC)
                with v.Fori(0, passes) as i:
                    own = Own(v, ch, i, per)
                    for b in range(NB):
                        v.wait_ge(gathered[b], i * (32 * KC) + 32 * KC)
                        own.link(nc.vector.tensor_tensor(
                            s[:, :, :], r[b][:, :, D:D + heads].rearrange("p k h -> p h k"),
                            ai[b][:, :, 0:heads].rearrange("p k h -> p h k"), ALU.add))
                        own.link(nc.vector.scalar_tensor_tensor(s[:, :, :], s[:, :, :], SLOPE, s[:, :, :],
                                                                ALU.mult, ALU.max))
                        for h in range(heads):
                            own.mark(nc.vector.tensor_tensor_scan(mx[:, h, 1:KC + 1], fac[b][:, 1, :], s[:, h, :],
                                                                  mx[:, h, 0:1], ALU.add, ALU.max))
                        own.wait()
                        own.mark(nc.vector.tensor_tensor(e[:, 1, :, :], s[:, :, :], mx[:, :, 1:KC + 1], ALU.subtract))
                        own.link(nc.vector.tensor_tensor(e[:, 0, :, :], mx[:, :, 0:KC], mx[:, :, 1:KC + 1],
                                                         ALU.subtract))
                        low = fac[b][:, 1:2, :].to_broadcast([P, heads, KC])
                        nc.vector.tensor_tensor(e[:, 0, :, :], e[:, 0, :, :], low, ALU.add).then_inc(asked, 1)
                        v.wait_ge(raised, nth(i, b))
                        for h in range(heads):
                            own.mark(nc.vector.tensor_tensor_scan(dn[:, h, 1:KC + 1], e[:, 0, h, :], e[:, 1, h, :],
                                                                  dn[:, h, 0:1], ALU.mult, ALU.add))
                        w = e[:, 1, :, :].rearrange("p h k -> p k h").unsqueeze(3).to_broadcast([P, KC, heads, dh])
                        rv = r[b][:, :, 0:D].rearrange("p k (h d) -> p k h d", h=heads)
                        own.link(nc.vector.tensor_tensor(rv, rv, w, ALU.mult))
                        for k in range(KC):
                            prev = r[b][:, k - 1, 0:D] if k else r[(b - 1) % NB][:, KC - 1, 0:D]
                            if heads == 1:
                                own.link(nc.vector.scalar_tensor_tensor(
                                    r[b][:, k, 0:D], prev, e[:, 0, 0, k:k + 1], r[b][:, k, 0:D], ALU.mult, ALU.add))
                            else:
                                f = e[:, 0, :, k:k + 1].to_broadcast([P, heads, dh])
                                own.link(nc.vector.tensor_tensor(
                                    tmp[:, :].rearrange("p (h d) -> p h d", h=heads),
                                    prev.rearrange("p (h d) -> p h d", h=heads), f, ALU.mult))
                                own.link(nc.vector.tensor_tensor(r[b][:, k, 0:D], r[b][:, k, 0:D], tmp[:, :],
                                                                 ALU.add))
                        own.mark(nc.vector.tensor_copy(r[b][:, :, DEN:DEN + heads],
                                                       dn[:, :, 1:KC + 1].rearrange("p h k -> p k h")))
                        own.link(nc.vector.tensor_copy(r[b][:, :, MAXC:MAXC + heads],
                                                       mx[:, :, 1:KC + 1].rearrange("p h k -> p k h")))
                        nc.vector.tensor_copy(dn[:, :, 0:1], dn[:, :, KC:KC + 1])
                        nc.vector.tensor_copy(mx[:, :, 0:1], mx[:, :, KC:KC + 1]).then_inc(stated, 1)
                        v.wait_ge(stated, nth(i, b))
                    own.end()
                nc.vector.tensor_copy(g.last[:, :], r[NB - 1][:, KC - 1, :]).then_inc(cleared, 1)
                v.wait_ge(cleared, 2)


def phase_join(g, tag, heads):
    nc = g.nc
    pre = f"j{tag}_"
    nh = max(heads, 1)
    dh = D // nh
    with ExitStack() as ctx:
        def sb(name, shape, dt=F32):
            return ctx.enter_context(nc.sbuf_tensor(pre + name, shape, dt))

        row = sb("row", [P, ROW])
        new = sb("new", [P, ROW])
        dgm = sb("dgm", [P, nh, P])
        w = sb("w", [P, nh, P])
        wt = sb("wt", [P, nh, P])
        mc = sb("mc", [P, nh])
        mn = sb("mn", [P, nh])
        e = sb("e", [P, 2, nh])
        t = sb("t", [P, D])
        pa = ctx.enter_context(nc.psum_tensor(pre + "pa", [P, 512], F32))
        pb = ctx.enter_context(nc.psum_tensor(pre + "pb", [P, 512], F32))
        pc = ctx.enter_context(nc.psum_tensor(pre + "pc", [P, 512], F32))
        got = g.indirect_sem(pre + "got")
        put = g.indirect_sem(pre + "put")
        ready = g.sem(pre + "ready")
        spread = g.sem(pre + "spread")
        raised = g.sem(pre + "raised")
        ch = g.sem(pre + "chain")
        with nc.Block() as block:
            @block.gpsimd
            def _(pool):
                pool.indirect_dma_start(out=row[:, :], out_offset=None, in_=g.seg,
                                        in_offset=bass.IndirectOffsetOnAxis(ap=g.first_i[:, 0:1], axis=0)
                                        ).then_inc(got, 16)
                pool.wait_ge(ready, 4 if heads else 1)
                pool.indirect_dma_start(out=g.seg, out_offset=bass.IndirectOffsetOnAxis(ap=g.fix_i[:, 0:1], axis=0),
                                        in_=new[:, :], in_offset=None, bounds_check=NPAD - 1, oob_is_err=False
                                        ).then_inc(put, 16)
                pool.wait_ge(put, 16)

            if not heads:
                @block.tensor
                def _(pe):
                    nc.tensor.matmul(pc[:, 0:TROW], g.cross[:, :], g.last[:, 0:TROW], start=True,
                                     stop=True).then_inc(spread, 1)

                @block.vector
                def _(v):
                    own = Own(v, ch)
                    v.wait_ge(got, 16)
                    own.mark(nc.vector.tensor_copy(new[:, TROW:ROW], row[:, TROW:ROW]))
                    v.wait_ge(spread, 1)
                    nc.vector.tensor_tensor(new[:, 0:TROW], row[:, 0:TROW], pc[:, 0:TROW], ALU.add).then_inc(ready, 1)
                return

            @block.tensor
            def _(pe):
                pe.wait_ge(ready, 1)
                nc.tensor.matmul(pa[:, 0:nh * P], g.ones[:, :], dgm[:, :, :].rearrange("p h f -> p (h f)"),
                                 start=True, stop=True).then_inc(spread, 1)
                pe.wait_ge(ready, 3)
                for h in range(nh):
                    last = nc.tensor.transpose(pb[:, h * P:(h + 1) * P], w[:, h, :], g.ident[:, :])
                last.then_inc(spread, 1)
                pe.wait_ge(raised, 3)
                for h in range(nh):
                    nc.tensor.matmul(pc[:, h * dh:(h + 1) * dh], wt[:, h, :], g.last[:, h * dh:(h + 1) * dh],
                                     start=True, stop=True)
                    last = nc.tensor.matmul(pc[:, DEN + h:DEN + h + 1], wt[:, h, :], g.last[:, DEN + h:DEN + h + 1],
                                            start=True, stop=True)
                last.then_inc(spread, 1)

            @block.scalar
            def _(act):
                act.wait_ge(ready, 2)
                nc.scalar.activation(w[:, :, :], w[:, :, :], ACT.Exp).then_inc(raised, 1)
                act.wait_ge(raised, 2)
                nc.scalar.activation(e[:, :, :], e[:, :, :], ACT.Exp)
                act.wait_ge(spread, 2)
                nc.scalar.copy(wt[:, :, :].rearrange("p h f -> p (h f)"), pb[:, 0:nh * P]).then_inc(raised, 1)

            @block.vector
            def _(v):
                own = Own(v, ch)
                for h in range(nh):
                    last = nc.vector.tensor_scalar(dgm[:, h, :], g.ident[:, :], g.last[:, MAXC + h:MAXC + h + 1],
                                                   None, ALU.mult)
                last.then_inc(ready, 1)
                v.wait_ge(spread, 1)
                low = g.low_t[:, :].unsqueeze(1).to_broadcast([P, nh, P])
                own.link(nc.vector.tensor_tensor(w[:, :, :], pa[:, 0:nh * P].rearrange("p (h f) -> p h f", h=nh), low,
                                                 ALU.add))
                own.link(nc.vector.tensor_reduce(mc[:, :], w[:, :, :], AX_X, ALU.max))
                nc.vector.tensor_tensor(w[:, :, :], w[:, :, :], mc[:, :].unsqueeze(2).to_broadcast([P, nh, P]),
                                        ALU.subtract).then_inc(ready, 1)
                v.wait_ge(raised, 1)
                cross = g.cross_t[:, :].unsqueeze(1).to_broadcast([P, nh, P])
                nc.vector.tensor_tensor(w[:, :, :], w[:, :, :], cross, ALU.mult).then_inc(ready, 1)
                v.wait_ge(got, 16)
                own.link(nc.vector.tensor_copy(new[:, :], row[:, :]))
                mr = row[:, MAXC:MAXC + nh]
                own.link(nc.vector.tensor_tensor(mn[:, :], mr, mc[:, :], ALU.max))
                own.mark(nc.vector.tensor_tensor(e[:, 0, :], mr, mn[:, :], ALU.subtract))
                own.mark(nc.vector.tensor_copy(new[:, MAXC:MAXC + nh], mn[:, :]))
                nc.vector.tensor_tensor(e[:, 1, :], mc[:, :], mn[:, :], ALU.subtract).then_inc(raised, 1)
                v.wait_ge(raised, 3)
                v.wait_ge(spread, 3)

                def bc(a):
                    return a.unsqueeze(2).to_broadcast([P, nh, dh])

                def hv(a):
                    return a.rearrange("p (h d) -> p h d", h=nh)

                own.mark(nc.vector.tensor_tensor(hv(new[:, 0:D]), hv(row[:, 0:D]), bc(e[:, 0, :]), ALU.mult))
                own.mark(nc.vector.tensor_tensor(new[:, DEN:DEN + nh], row[:, DEN:DEN + nh], e[:, 0, :], ALU.mult))
                own.mark(nc.vector.tensor_tensor(hv(t[:, :]), hv(pc[:, 0:D]), bc(e[:, 1, :]), ALU.mult))
                own.link(nc.vector.tensor_tensor(mn[:, :], pc[:, DEN:DEN + nh], e[:, 1, :], ALU.mult))
                own.mark(nc.vector.tensor_tensor(new[:, 0:D], new[:, 0:D], t[:, :], ALU.add))
                nc.vector.tensor_tensor(new[:, DEN:DEN + nh], new[:, DEN:DEN + nh], mn[:, :],
                                        ALU.add).then_inc(ready, 1)



def norm_stats(nc, own, gate, src, st, mv, ve):
    for q in range(Q):
        own.mark(nc.vector.bn_stats(st[:, q, :], src[:, q, :]))
    own.wait()
    own.eng.sem_inc(gate, 1)
    for q in range(Q):
        own.mark(nc.vector.bn_aggr(mv[:, q, :], st[:, q, :]))
    own.wait()
    return nc.vector.tensor_scalar(ve[:, :], mv[:, :, 1], EPS, None, ALU.add)


def norm_apply(nc, dst, src, mv, rs):
    for q in range(Q):
        last = nc.vector.tensor_scalar(dst[:, q, :], src[:, q, :], mv[:, q, 0:1], rs[:, q:q + 1],
                                       ALU.subtract, ALU.mult)
    return last


def phase_settle(g, layer, heads):
    nc = g.nc
    dh = D // heads
    pre = f"s{layer}_"
    first = layer == 0
    bias = g.bias0 if first else g.bias1
    with ExitStack() as ctx:
        def sb(name, shape, dt=F32):
            return [ctx.enter_context(nc.sbuf_tensor(f"{pre}{name}{b}", shape, dt)) for b in range(2)]

        x = sb("x", [P, Q, D])
        ag = sb("ag", [P, Q, ROW])
        se = sb("se", [P, Q, TROW])
        ai = sb("ai", [P, Q, HEADS])
        s = sb("s", [P, Q, heads])
        m = sb("m", [P, Q, heads])
        e = sb("e", [P, 2, Q, heads])
        den = sb("den", [P, Q, heads])
        o = sb("o", [P, Q, D])
        sq = sb("sq", [P, Q, D])
        nr = sb("nr", [P, 4, Q])
        st = sb("st", [P, Q, 6])
        mv = sb("mv", [P, Q, 2])
        ve = sb("ve", [P, Q])
        rs = sb("rs", [P, Q])
        xn = sb("xn", [P, Q, D])
        xt = sb("xt", [P, CHUNK])
        tr = sb("tr", [P, Q, TROW])
        ao = sb("ao", [P, Q, HEADS])
        hr = sb("hr", [P, Q, D])
        pt = [ctx.enter_context(nc.psum_tensor(f"{pre}pt{b}", [P, 512], F32)) for b in range(2)]
        pm = [ctx.enter_context(nc.psum_tensor(f"{pre}pm{b}", [P, 2, 512], F32)) for b in range(2)]
        loaded = [g.sem(f"{pre}loaded{b}") for b in range(2)]
        asked = g.sem(pre + "asked")
        raised = g.sem(pre + "raised")
        biased = g.sem(pre + "biased")
        squared = g.sem(pre + "squared")
        normasked = g.sem(pre + "normasked")
        rooted = g.sem(pre + "rooted")
        tanhed = g.sem(pre + "tanhed")
        varasked = g.sem(pre + "varasked")
        scale = g.sem(pre + "scale")
        normed = g.sem(pre + "normed")
        turned = g.sem(pre + "turned")
        copied = g.sem(pre + "copied")
        product = g.sem(pre + "product")
        hidden = g.sem(pre + "hidden")
        back = g.sem(pre + "back")
        moved = g.sem(pre + "moved")
        stored = [g.sem(f"{pre}stored{b}") for b in range(2)]
        freed = g.sem(pre + "freed")
        ch = g.sem(pre + "chain")
        gate = g.sem(pre + "gate")
        half = NCHUNK // 2
        xsrc = g.ins["x"] if first else g.x[1]
        nstores = 3
        with nc.Block() as block:
            @block.sync
            def _(sp):
                with sp.Fori(0, half) as i:
                    for b in range(2):
                        c = i * 2 + b
                        sp.wait_ge(normed, pair(i, b))
                        for dst, src in ((x, xsrc), (ag, g.seg), (se, g.t[layer]), (ai, g.ai[layer])):
                            sp.dma_start(dst[b][:, :, :], rows(src, c)).then_inc(loaded[b], 16)

            @block.gpsimd
            def _(pool):
                with pool.Fori(0, half) as i:
                    if first:
                        for b in range(2):
                            pool.wait_ge(normasked, pair(i, b))
                            pool.tensor_tensor(nr[b][:, 1, :], nr[b][:, 0, :], g.half[:, 0:Q],
                                               ALU.pow).then_inc(rooted, 1)
                    for b in range(2):
                        pool.wait_ge(varasked, pair(i, b))
                        pool.tensor_tensor(rs[b][:, :], ve[b][:, :], g.mhalf[:, 0:Q], ALU.pow).then_inc(scale, 1)
                    for b in range(2):
                        gated(pool, stored[b], i * (16 * nstores) + 16 * nstores, freed)

            @block.scalar
            def _(act):
                act.sem_inc(copied, 2)
                with act.Fori(0, half) as i:
                    for b in range(2):
                        act.wait_ge(asked, pair(i, b))
                        nc.scalar.activation(e[b][:, :, :, :], e[b][:, :, :, :], ACT.Exp).then_inc(raised, 1)
                    if first:
                        for b in range(2):
                            act.wait_ge(biased, pair(i, b))
                            nc.scalar.activation(xn[b][:, :, :], o[b][:, :, :], ACT.Relu).then_inc(squared, 1)
                            act.wait_ge(squared, i * 4 + (2 * b + 1))
                            nc.scalar.activation(sq[b][:, :, :], xn[b][:, :, :], ACT.Square).then_inc(squared, 1)
                        for b in range(2):
                            act.wait_ge(rooted, pair(i, b))
                            nc.scalar.activation(nr[b][:, 2, :], nr[b][:, 1, :], ACT.Tanh).then_inc(tanhed, 1)
                    for b in range(2):
                        c = i * 2 + b
                        act.wait_ge(normed, pair(i, b) + 2)
                        act.dma_start(rows(g.x[layer + 1], c), xn[b][:, :, :]).then_inc(stored[b], 16)
                        act.wait_ge(turned, pair(i, b))
                        nc.scalar.copy(xt[b][:, :], pt[b][:, :]).then_inc(copied, 1)
                    if first:
                        for b in range(2):
                            c = i * 2 + b
                            act.wait_ge(moved, pair(i, b) + 2)
                            act.dma_start(rows(g.t[1], c), tr[b][:, :, :]).then_inc(stored[b], 16)
                            act.dma_start(rows(g.ai[1], c), ao[b][:, :, :]).then_inc(stored[b], 16)
                    else:
                        for b in range(2):
                            act.wait_ge(product, pair(i, b))
                            nc.scalar.activation(xt[b][:, :], pm[b][:, 0, :], ACT.Relu,
                                                 bias=g.projb[:, 0:1]).then_inc(hidden, 1)
                        for b in range(2):
                            act.wait_ge(hidden, pair(i, b))
                            act.dma_start(g.ht[0][bass.ds(i * 2 + b, 1)].rearrange("c p n -> (c p) n"),
                                          xt[b][:, :]).then_inc(stored[b], 16)
                            act.wait_ge(moved, pair(i, b) + 2)
                            act.dma_start(rows(g.hr[0], i * 2 + b), hr[b][:, :, :]).then_inc(stored[b], 16)

            @block.tensor
            def _(pe):
                with pe.Fori(0, half) as i:
                    for b in range(2):
                        pe.wait_ge(normed, pair(i, b) + 2)
                        pe.wait_ge(copied, pair(i, b))
                        pe.wait_ge(moved, pair(i, b))
                        for q in range(Q):
                            last = nc.tensor.transpose(pt[b][:, q * P:(q + 1) * P], xn[b][:, q, :], g.ident[:, :])
                        last.then_inc(turned, 1)
                    for b in range(2):
                        pe.wait_ge(copied, pair(i, b) + 2)
                        if first:
                            for q in range(Q):
                                w = (q % 2) * (D + 2)
                                last = nc.tensor.matmul(pm[b][:, q // 2, w:w + D + 2], xt[b][:, q * P:(q + 1) * P],
                                                        g.w1aug[:, :], start=True, stop=True)
                            last.then_inc(product, 1)
                        else:
                            nc.tensor.matmul(pm[b][:, 0, :], g.projw[:, :], xt[b][:, :], start=True,
                                             stop=True).then_inc(product, 1)
                    if not first:
                        for b in range(2):
                            pe.wait_ge(hidden, pair(i, b))
                            for q in range(Q):
                                last = nc.tensor.transpose(pt[b][:, q * P:(q + 1) * P], xt[b][:, q * P:(q + 1) * P],
                                                           g.ident[:, :])
                            last.then_inc(back, 1)

            @block.vector
            def _(v):
                for b in range(2):
                    nc.vector.memset(tr[b][:, :, :], 0.0)
                    last = nc.vector.memset(ao[b][:, :, :], 0.0)
                last.then_inc(gate, 1)
                v.wait_ge(gate, 1)
                v.sem_inc(normed, 2)
                v.sem_inc(moved, 2)
                v.sem_inc(freed, 2)
                per = 2 * (30 if first else 21)
                with v.Fori(0, half) as i:
                    own = Own(v, ch, i, per)
                    for b in range(2):
                        v.wait_ge(loaded[b], i * 64 + 64)
                        own.link(nc.vector.tensor_tensor(s[b][:, :, :], se[b][:, :, D:D + heads],
                                                         ai[b][:, :, 0:heads], ALU.add))
                        own.link(nc.vector.scalar_tensor_tensor(s[b][:, :, :], s[b][:, :, :], SLOPE, s[b][:, :, :],
                                                                ALU.mult, ALU.max))
                        ms = ag[b][:, :, MAXC:MAXC + heads]
                        own.link(nc.vector.tensor_tensor(m[b][:, :, :], ms, s[b][:, :, :], ALU.max))
                        own.link(nc.vector.tensor_tensor(e[b][:, 0, :, :], ms, m[b][:, :, :], ALU.subtract))
                        nc.vector.tensor_tensor(e[b][:, 1, :, :], s[b][:, :, :], m[b][:, :, :],
                                                ALU.subtract).then_inc(asked, 1)
                    for b in range(2):
                        v.wait_ge(raised, pair(i, b))
                        own.link(nc.vector.tensor_tensor(den[b][:, :, :], ag[b][:, :, DEN:DEN + heads],
                                                         e[b][:, 0, :, :], ALU.mult))
                        own.link(nc.vector.tensor_tensor(den[b][:, :, :], den[b][:, :, :], e[b][:, 1, :, :], ALU.add))
                        if first:
                            own.link(nc.vector.tensor_scalar(den[b][:, :, :], den[b][:, :, :], MIN_NORM, None,
                                                             ALU.max))
                        own.link(nc.vector.reciprocal(den[b][:, :, :], den[b][:, :, :]))
                        for n in range(2):
                            own.mark(nc.vector.tensor_tensor(e[b][:, n, :, :], e[b][:, n, :, :], den[b][:, :, :],
                                                             ALU.mult))
                        own.wait()

                        def hv(a):
                            return a.rearrange("p q (h d) -> p q h d", h=heads)

                        def w(n):
                            return e[b][:, n, :, :].unsqueeze(3).to_broadcast([P, Q, heads, dh])

                        own.mark(nc.vector.tensor_tensor(hv(ag[b][:, :, 0:D]), hv(ag[b][:, :, 0:D]), w(0), ALU.mult))
                        own.link(nc.vector.tensor_tensor(hv(se[b][:, :, 0:D]), hv(se[b][:, :, 0:D]), w(1), ALU.mult))
                        own.link(nc.vector.tensor_tensor(o[b][:, :, :], ag[b][:, :, 0:D], se[b][:, :, 0:D], ALU.add))
                        bb = bias[:, :].unsqueeze(1).to_broadcast([P, Q, D])
                        v.wait_ge(freed, pair(i, b))
                        nc.vector.tensor_tensor(o[b][:, :, :], o[b][:, :, :], bb, ALU.add).then_inc(biased, 1)
                        if not first:
                            v.wait_ge(biased, pair(i, b))
                            own.mark(nc.vector.tensor_tensor(o[b][:, :, :], o[b][:, :, :], x[b][:, :, :], ALU.add))
                    if first:
                        for b in range(2):
                            v.wait_ge(squared, i * 4 + (2 * b + 2))
                            own.link(nc.vector.tensor_reduce(nr[b][:, 0, :], sq[b][:, :, :], AX_X, ALU.add))
                            nc.vector.tensor_scalar(nr[b][:, 0, :], nr[b][:, 0, :], MIN_NORM ** 2, None,
                                                    ALU.max).then_inc(normasked, 1)
                        for b in range(2):
                            v.wait_ge(rooted, pair(i, b))
                            own.mark(nc.vector.reciprocal(nr[b][:, 3, :], nr[b][:, 1, :]))
                            v.wait_ge(tanhed, pair(i, b))
                            own.mark(nc.vector.tensor_scalar(nr[b][:, 2, :], nr[b][:, 2, :], MAX_NORM, None, ALU.min))
                            own.wait()
                            own.link(nc.vector.tensor_tensor(nr[b][:, 3, :], nr[b][:, 3, :], nr[b][:, 2, :],
                                                             ALU.mult))
                            for q in range(Q):
                                own.mark(nc.vector.scalar_tensor_tensor(
                                    o[b][:, q, :], xn[b][:, q, :], nr[b][:, 3, q:q + 1], x[b][:, q, :],
                                    ALU.mult, ALU.add))
                    for b in range(2):
                        own.wait()
                        norm_stats(nc, own, gate, o[b], st[b], mv[b], ve[b]).then_inc(varasked, 1)
                    for b in range(2):
                        v.wait_ge(scale, pair(i, b))
                        norm_apply(nc, xn[b], o[b], mv[b], rs[b]).then_inc(normed, 1)
                    for b in range(2):
                        if first:
                            v.wait_ge(product, pair(i, b))
                            view = pm[b][:, :, 0:2 * (D + 2)].rearrange("p a (s c) -> p a s c", s=2)
                            own.mark(nc.vector.tensor_copy(
                                tr[b][:, :, 0:D + 1].rearrange("p (a s) c -> p a s c", s=2), view[:, :, :, 0:D + 1]))
                            nc.vector.tensor_copy(ao[b][:, :, 0:1].rearrange("p (a s) c -> p a s c", s=2),
                                                  view[:, :, :, D + 1:D + 2]).then_inc(moved, 1)
                        else:
                            v.wait_ge(back, pair(i, b))
                            nc.vector.tensor_copy(hr[b][:, :, :].rearrange("p q d -> p (q d)"),
                                                  pt[b][:, :]).then_inc(moved, 1)
                    own.end()



def phase_relate(g, n):
    nc = g.nc
    pre = f"r{n}_"
    with ExitStack() as ctx:
        def sb(name, shape, dt=F32):
            return ctx.enter_context(nc.sbuf_tensor(pre + name, shape, dt))

        idx = [sb(f"idx{b}", [P, 3, KC], I32) for b in range(NB)]
        fac = [sb(f"fac{b}", [P, 2, KC]) for b in range(NB)]
        r = [sb(f"r{b}", [P, KC, ROW]) for b in range(NB)]
        ty = [sb(f"ty{b}", [P, KC, P]) for b in range(NB)]
        w = sb("w", [P, TYPES, D])
        ht = [sb(f"ht{b}", [P, P]) for b in range(2)]
        hm = [sb(f"hm{b}", [P, TYPES, P]) for b in range(2)]
        pt = [ctx.enter_context(nc.psum_tensor(f"{pre}pt{b}", [P, 512], F32)) for b in range(2)]
        pm = [ctx.enter_context(nc.psum_tensor(f"{pre}pm{b}", [P, 512], F32)) for b in range(2)]
        wloaded = g.sem(pre + "wloaded")
        listed = [g.sem(pre + f"listed{b}") for b in range(NB)]
        gathered = [g.indirect_sem(pre + f"gathered{b}") for b in range(NB)]
        scattered = [g.indirect_sem(pre + f"scattered{b}") for b in range(NB)]
        turned = g.sem(pre + "turned")
        copied = g.sem(pre + "copied")
        masked = g.sem(pre + "masked")
        product = g.sem(pre + "product")
        added = g.sem(pre + "added")
        stated = g.sem(pre + "stated")
        unlisted = g.sem(pre + "unlisted")
        cleared = g.sem(pre + "cleared")
        gate = g.sem(pre + "gate")
        passes = ECHUNK // NB
        per = NB * KC
        assert per % 2 == 0
        with nc.Block() as block:
            @block.sync
            def _(sp):
                sp.dma_start(w[:, :, :], g.ins["edgew"][n]).then_inc(wloaded, 16)

                def types(i, b):
                    k0 = i * (NB * KC) + b * KC
                    src = g.type_rows[bass.ds(k0, KC)].rearrange("k p -> (k p)").unsqueeze(0).to_broadcast([P, KC * P])
                    sp.dma_start(ty[b][:, :, :].rearrange("p k e -> p (k e)"), src).then_inc(listed[b], 16)

                edge_lists(g, sp, idx, fac, listed, unlisted, types)

            @block.gpsimd
            def _(pool):
                pool.sem_inc(unlisted, NB)
                pool.wait_ge(cleared, 1)

                def gathers(b):
                    for k in range(KC):
                        pool.indirect_dma_start(
                            out=r[b][:, k, 0:D], out_offset=None, in_=g.hr[n],
                            in_offset=bass.IndirectOffsetOnAxis(ap=idx[b][:, 0, k:k + 1], axis=0)
                        ).then_inc(gathered[b], 16)

                edge_moves(g, pool, gathers, r, idx, listed, 48, scattered, stated, unlisted, gate)

            @block.tensor
            def _(pe):
                pe.wait_ge(wloaded, 16)
                with pe.Fori(0, passes) as i:
                    for j in range(per + 1):
                        if j < per:
                            b, k = divmod(j, KC)
                            if k == 0:
                                pe.wait_ge(gathered[b], i * (16 * KC) + 16 * KC)
                            pe.wait_ge(copied, i * per + (j + 1))
                            nc.tensor.transpose(pt[j % 2][:, 0:P], r[b][:, k, 0:D], g.ident[:, :]).then_inc(turned, 1)
                        if j > 0:
                            u = j - 1
                            pe.wait_ge(masked, i * per + (u + 3))
                            pe.wait_ge(added, i * per + (u + 1))
                            for t in range(TYPES):
                                last = nc.tensor.matmul(pm[u % 2][:, 0:D], hm[u % 2][:, t, :], w[:, t, :],
                                                        start=(t == 0), stop=(t == TYPES - 1))
                            last.then_inc(product, 1)

            @block.scalar
            def _(act):
                act.sem_inc(copied, 2)
                with act.Fori(0, passes) as i:
                    for j in range(per):
                        act.wait_ge(turned, i * per + (j + 1))
                        act.wait_ge(masked, i * per + (j + 1))
                        nc.scalar.copy(ht[j % 2][:, :], pt[j % 2][:, 0:P]).then_inc(copied, 1)

            @block.vector
            def _(v):
                for b in range(NB):
                    last = nc.vector.memset(r[b][:, :, :], 0.0)
                last.then_inc(cleared, 1)
                v.wait_ge(cleared, 1)
                v.sem_inc(masked, 2)
                v.sem_inc(added, 2)
                with v.Fori(0, passes) as i:
                    for j in range(per + 1):
                        if j < per:
                            b, k = divmod(j, KC)
                            if k == 0:
                                v.wait_ge(listed[b], i * 48 + 48)
                                v.sem_inc(gate, 1)
                            v.wait_ge(copied, i * per + (j + 3))
                            if j >= 2:
                                v.wait_ge(product, i * per + (j - 1))
                            for t in range(TYPES):
                                last = nc.vector.scalar_tensor_tensor(hm[j % 2][:, t, :], ty[b][:, k, :], float(t),
                                                                      ht[j % 2][:, :], ALU.is_equal, ALU.mult)
                            last.then_inc(masked, 1)
                        if j > 0:
                            b, k = divmod(j - 1, KC)
                            v.wait_ge(product, i * per + j)
                            v.wait_ge(added, i * per + (j + 1))
                            prev = r[b][:, k - 1, 0:D] if k else r[(b - 1) % NB][:, KC - 1, 0:D]
                            nc.vector.scalar_tensor_tensor(r[b][:, k, 0:D], prev, fac[b][:, 0, k:k + 1],
                                                           pm[(j - 1) % 2][:, 0:D], ALU.mult,
                                                           ALU.add).then_inc(added, 1)
                            if k == KC - 1:
                                v.wait_ge(added, i * per + (j + 2))
                                v.sem_inc(stated, 1)
                nc.vector.tensor_copy(g.last[:, :], r[NB - 1][:, KC - 1, :]).then_inc(cleared, 1)
                v.wait_ge(cleared, 2)


def phase_gru(g, n):
    nc = g.nc
    pre = f"g{n}_"
    final = n == 1
    with ExitStack() as ctx:
        def sb(name, shape, dt=F32):
            return [ctx.enter_context(nc.sbuf_tensor(f"{pre}{name}{b}", shape, dt)) for b in range(2)]

        ag = sb("ag", [P, Q, D])
        h = sb("h", [P, CHUNK])
        x = sb("x", [P, Q, D])
        at = sb("at", [P, CHUNK])
        tr = sb("tr", [P, CHUNK])
        tz = sb("tz", [P, CHUNK])
        hn = sb("hn", [P, CHUNK])
        c = sb("c", [P, CHUNK])
        hy = sb("hy", [P, CHUNK])
        hr = sb("hr", [P, Q, D])
        st = sb("st", [P, Q, 6])
        mv = sb("mv", [P, Q, 2])
        ve = sb("ve", [P, Q])
        rs = sb("rs", [P, Q])
        xn = sb("xn", [P, Q, D])
        xt = sb("xt", [P, CHUNK])
        ab = sb("ab", [P, 2, Q, D])
        pa = [ctx.enter_context(nc.psum_tensor(f"{pre}pa{b}", [P, 512], F32)) for b in range(2)]
        pg = [ctx.enter_context(nc.psum_tensor(f"{pre}pg{k}", [P, 512], F32)) for k in range(4)]
        pb = [ctx.enter_context(nc.psum_tensor(f"{pre}pb{b}", [P, 512], F32)) for b in range(2)]
        loaded = [g.sem(f"{pre}loaded{b}") for b in range(2)]
        turned = g.sem(pre + "turned")
        copied = g.sem(pre + "copied")
        gates = g.sem(pre + "gates")
        squashed = g.sem(pre + "squashed")
        casked = g.sem(pre + "casked")
        cand = g.sem(pre + "cand")
        hidden = g.sem(pre + "hidden")
        back = g.sem(pre + "back")
        moved = g.sem(pre + "moved")
        varasked = g.sem(pre + "varasked")
        scale = g.sem(pre + "scale")
        normed = g.sem(pre + "normed")
        turned2 = g.sem(pre + "turned2")
        copied2 = g.sem(pre + "copied2")
        product = g.sem(pre + "product")
        drawn = g.sem(pre + "drawn")
        stored = [g.sem(f"{pre}stored{b}") for b in range(2)]
        freed = g.sem(pre + "freed")
        ch = g.sem(pre + "chain")
        gate = g.sem(pre + "gate")
        half = NCHUNK // 2
        nload = 3 if final else 2
        nstore = 3 if final else 2
        gb = g.gb[n]
        with nc.Block() as block:
            @block.sync
            def _(sp):
                with sp.Fori(0, half) as i:
                    for b in range(2):
                        sp.wait_ge(moved, pair(i, b))
                        ci = i * 2 + b
                        sp.dma_start(ag[b][:, :, :], rows(g.seg, ci)[:, :, 0:D]).then_inc(loaded[b], 16)
                        sp.dma_start(h[b][:, :], g.ht[n][bass.ds(ci, 1)].rearrange(
                            "c p n -> (c p) n")).then_inc(loaded[b], 16)
                        if final:
                            sp.dma_start(x[b][:, :, :], rows(g.x[2], ci)).then_inc(loaded[b], 16)

            @block.gpsimd
            def _(pool):
                with pool.Fori(0, half) as i:
                    if final:
                        for b in range(2):
                            pool.wait_ge(varasked, pair(i, b))
                            pool.tensor_tensor(rs[b][:, :], ve[b][:, :], g.mhalf[:, 0:Q], ALU.pow).then_inc(scale, 1)
                    for b in range(2):
                        gated(pool, stored[b], i * (16 * nstore) + 16 * nstore, freed)

            @block.tensor
            def _(pe):
                with pe.Fori(0, half) as i:
                    for b in range(2):
                        pe.wait_ge(loaded[b], i * (16 * nload) + 16 * nload)
                        pe.wait_ge(copied, pair(i, b))
                        if final:
                            pe.wait_ge(copied2, pair(i, b))
                        for q in range(Q):
                            last = nc.tensor.transpose(pa[b][:, q * P:(q + 1) * P], ag[b][:, q, :], g.ident[:, :])
                        last.then_inc(turned, 1)
                    for b in range(2):
                        pe.wait_ge(copied, pair(i, b) + 2)
                        pe.wait_ge(casked, pair(i, b))
                        if final:
                            pe.wait_ge(drawn, pair(i, 0))
                        for k in range(4):
                            wi, wh = g.wih[n], g.whh[n]
                            ks = slice(min(k, 2) * D, (min(k, 2) + 1) * D)
                            if k < 3:
                                last = nc.tensor.matmul(pg[k][:, :], wi[:, ks], at[b][:, :], start=True, stop=(k == 2))
                            if k != 2:
                                last = nc.tensor.matmul(pg[k][:, :], wh[:, ks], h[b][:, :], start=(k == 3), stop=True)
                        last.then_inc(gates, 1)
                    for b in range(2):
                        pe.wait_ge(hidden, pair(i, b) + 2)
                        pe.wait_ge(moved, pair(i, b))
                        for q in range(Q):
                            hq = hy[b][:, q * P:(q + 1) * P]
                            if final:
                                last = nc.tensor.matmul(pb[b][:, q * P:(q + 1) * P], hq, g.outw[:, :], start=True,
                                                        stop=True)
                            else:
                                last = nc.tensor.transpose(pb[b][:, q * P:(q + 1) * P], hq, g.ident[:, :])
                        last.then_inc(back, 1)
                    if final:
                        for b in range(2):
                            pe.wait_ge(normed, pair(i, b))
                            for q in range(Q):
                                last = nc.tensor.transpose(pa[b][:, q * P:(q + 1) * P], xn[b][:, q, :], g.ident[:, :])
                            last.then_inc(turned2, 1)
                        for b in range(2):
                            pe.wait_ge(copied2, pair(i, b) + 2)
                            for q in range(Q):
                                last = nc.tensor.matmul(pg[2 * b + q // 2][:, (q % 2) * 2 * D:(q % 2 + 1) * 2 * D],
                                                        xt[b][:, q * P:(q + 1) * P], g.wm1[:, :], start=True,
                                                        stop=True)
                            last.then_inc(product, 1)

            @block.scalar
            def _(act):
                act.sem_inc(copied, 2)
                act.sem_inc(copied2, 2)
                with act.Fori(0, half) as i:
                    for b in range(2):
                        act.wait_ge(turned, pair(i, b))
                        nc.scalar.copy(at[b][:, :], pa[b][:, :]).then_inc(copied, 1)
                    for b in range(2):
                        act.wait_ge(gates, pair(i, b))
                        nc.scalar.activation(tr[b][:, :], pg[0][:, :], ACT.Tanh, bias=gb[:, 0:1], scale=0.5)
                        nc.scalar.activation(tz[b][:, :], pg[1][:, :], ACT.Tanh, bias=gb[:, 1:2], scale=0.5)
                        nc.scalar.activation(hn[b][:, :], pg[3][:, :], ACT.Identity,
                                             bias=gb[:, 3:4]).then_inc(squashed, 1)
                        act.wait_ge(casked, pair(i, b) + 1)
                        nc.scalar.activation(c[b][:, :], c[b][:, :], ACT.Tanh, bias=gb[:, 2:3]).then_inc(cand, 1)
                    if final:
                        for b in range(2):
                            ci = i * 2 + b
                            act.wait_ge(normed, pair(i, b))
                            act.dma_start(rows(g.x[3], ci), xn[b][:, :, :]).then_inc(stored[b], 16)
                            act.wait_ge(turned2, pair(i, b))
                            nc.scalar.copy(xt[b][:, :], pa[b][:, :]).then_inc(copied2, 1)
                        for b in range(2):
                            ci = i * 2 + b
                            act.wait_ge(drawn, pair(i, b) + 2)
                            for k, t in enumerate((g.ta, g.tb)):
                                act.dma_start(rows(t, ci), ab[b][:, k, :, :]).then_inc(stored[b], 16)
                    else:
                        for b in range(2):
                            ci = i * 2 + b
                            act.wait_ge(hidden, pair(i, b) + 2)
                            act.dma_start(g.ht[1][bass.ds(ci, 1)].rearrange("c p n -> (c p) n"),
                                          hy[b][:, :]).then_inc(stored[b], 16)
                            act.wait_ge(moved, pair(i, b) + 2)
                            act.dma_start(rows(g.hr[1], ci), hr[b][:, :, :]).then_inc(stored[b], 16)

            @block.vector
            def _(v):
                v.sem_inc(casked, 1)
                v.sem_inc(hidden, 2)
                v.sem_inc(moved, 2)
                v.sem_inc(freed, 2)
                v.sem_inc(drawn, 2)
                per = 2 * (15 if final else 4)
                with v.Fori(0, half) as i:
                    own = Own(v, ch, i, per)
                    for b in range(2):
                        v.wait_ge(squashed, pair(i, b))
                        v.wait_ge(freed, pair(i, b))
                        own.link(nc.vector.scalar_tensor_tensor(hn[b][:, :], tr[b][:, :], 1.0, hn[b][:, :],
                                                                ALU.add, ALU.mult))
                        nc.vector.scalar_tensor_tensor(c[b][:, :], hn[b][:, :], 0.5, pg[2][:, :],
                                                       ALU.mult, ALU.add).then_inc(casked, 1)
                    for b in range(2):
                        v.wait_ge(cand, pair(i, b))
                        own.link(nc.vector.tensor_tensor(h[b][:, :], h[b][:, :], c[b][:, :], ALU.subtract))
                        own.link(nc.vector.scalar_tensor_tensor(h[b][:, :], tz[b][:, :], 1.0, h[b][:, :],
                                                                ALU.add, ALU.mult))
                        own.link(nc.vector.scalar_tensor_tensor(h[b][:, :], h[b][:, :], 0.5, c[b][:, :],
                                                                ALU.mult, ALU.add))
                        nc.vector.tensor_scalar(hy[b][:, :], h[b][:, :], 0.0, None, ALU.max).then_inc(hidden, 1)
                    if not final:
                        for b in range(2):
                            v.wait_ge(back, pair(i, b))
                            v.wait_ge(hidden, pair(i, b) + 2)
                            nc.vector.tensor_copy(hr[b][:, :, :].rearrange("p q d -> p (q d)"),
                                                  pb[b][:, :]).then_inc(moved, 1)
                    else:
                        ob = g.outb[:, :].unsqueeze(1).to_broadcast([P, Q, D])
                        for b in range(2):
                            v.wait_ge(back, pair(i, b))
                            own.link(nc.vector.tensor_tensor(hr[b][:, :, :],
                                                             pb[b][:, :].rearrange("p (q d) -> p q d", q=Q),
                                                             x[b][:, :, :], ALU.add))
                            own.link(nc.vector.tensor_tensor(hr[b][:, :, :], hr[b][:, :, :], ob, ALU.add))
                            norm_stats(nc, own, gate, hr[b], st[b], mv[b], ve[b]).then_inc(varasked, 1)
                        for b in range(2):
                            v.wait_ge(scale, pair(i, b))
                            own.mark(norm_apply(nc, xn[b], hr[b], mv[b], rs[b]))
                            own.wait()
                            v.sem_inc(normed, 1)
                            v.sem_inc(moved, 1)
                        for b in range(2):
                            v.wait_ge(product, pair(i, b))
                            for k in range(2):
                                view = pg[2 * b + k][:, :].rearrange("p (q a d) -> p a q d", q=2, a=2)
                                last = nc.vector.tensor_tensor(
                                    ab[b][:, :, 2 * k:2 * k + 2, :], view,
                                    g.bab[:, :, :].unsqueeze(2).to_broadcast([P, 2, 2, D]), ALU.add)
                            last.then_inc(drawn, 1)
                    own.end()



def phase_filter(g):
    nc = g.nc
    pre = "f_"
    with ExitStack() as ctx:
        def sb(name, shape, dt=F32):
            return ctx.enter_context(nc.sbuf_tensor(pre + name, shape, dt))

        idx = [sb(f"idx{b}", [P, 3, KC], I32) for b in range(NB)]
        fac = [sb(f"fac{b}", [P, 2, KC]) for b in range(NB)]
        r = [sb(f"r{b}", [P, KC, ROW]) for b in range(NB)]
        bd = [sb(f"bd{b}", [P, KC, D]) for b in range(NB)]
        ra = [sb(f"ra{b}", [RADIAL, KC, P]) for b in range(NB)]
        dg = sb("dg", [P, KC + 1])
        t1 = [sb(f"t1{b}", [P, P]) for b in range(2)]
        h1 = [sb(f"h1{b}", [P, P]) for b in range(2)]
        t2 = [sb(f"t2{b}", [P, P]) for b in range(2)]
        h2 = [sb(f"h2{b}", [P, P]) for b in range(2)]
        p1 = [ctx.enter_context(nc.psum_tensor(f"{pre}p1{b}", [P, 512], F32)) for b in range(2)]
        p2 = [ctx.enter_context(nc.psum_tensor(f"{pre}p2{b}", [P, 512], F32)) for b in range(2)]
        listed = [g.sem(pre + f"listed{b}") for b in range(NB)]
        gathered = [g.indirect_sem(pre + f"gathered{b}") for b in range(NB)]
        scattered = [g.indirect_sem(pre + f"scattered{b}") for b in range(NB)]
        radial = g.sem(pre + "radial")
        sqd = g.sem(pre + "sqd")
        summed = g.sem(pre + "summed")
        tanh1 = g.sem(pre + "tanh1")
        silu1 = g.sem(pre + "silu1")
        summed2 = g.sem(pre + "summed2")
        tanh2 = g.sem(pre + "tanh2")
        silu2 = g.sem(pre + "silu2")
        added = g.sem(pre + "added")
        stated = g.sem(pre + "stated")
        degrees = g.sem(pre + "degrees")
        unlisted = g.sem(pre + "unlisted")
        cleared = g.sem(pre + "cleared")
        gate = g.sem(pre + "gate")
        passes = ECHUNK // NB
        per = NB * KC
        coeff = -0.5 / (CUTOFF / (RADIAL - 1)) ** 2
        with nc.Block() as block:
            @block.sync
            def _(sp):
                def distances(i, b):
                    k0 = i * (NB * KC) + b * KC
                    src = g.dist_rows[bass.ds(k0, KC)].rearrange("k p -> (k p)").unsqueeze(0)
                    sp.dma_start(ra[b][:, :, :].rearrange("p k e -> p (k e)"),
                                 src.to_broadcast([RADIAL, KC * P])).then_inc(listed[b], 16)

                edge_lists(g, sp, idx, fac, listed, unlisted, distances)

            @block.gpsimd
            def _(pool):
                pool.sem_inc(unlisted, NB)
                pool.wait_ge(cleared, 1)

                def gathers(b):
                    for k in range(KC):
                        pool.indirect_dma_start(
                            out=r[b][:, k, 0:D], out_offset=None, in_=g.ta,
                            in_offset=bass.IndirectOffsetOnAxis(ap=idx[b][:, 0, k:k + 1], axis=0)
                        ).then_inc(gathered[b], 16)
                        pool.indirect_dma_start(
                            out=bd[b][:, k, :], out_offset=None, in_=g.tb,
                            in_offset=bass.IndirectOffsetOnAxis(ap=idx[b][:, 1, k:k + 1], axis=0)
                        ).then_inc(gathered[b], 16)

                edge_moves(g, pool, gathers, r, idx, listed, 48, scattered, stated, unlisted, gate)

            @block.tensor
            def _(pe):
                with pe.Fori(0, passes) as i:
                    for j in range(per + 1):
                        if j < per:
                            b, k = divmod(j, KC)
                            if k == 0:
                                pe.wait_ge(gathered[b], i * (32 * KC) + 32 * KC)
                                pe.wait_ge(radial, nth(i, b))
                            pe.wait_ge(silu1, i * per + (j + 1))
                            o = p1[j % 2][:, 0:P]
                            nc.tensor.matmul(o, r[b][:, k, 0:D], g.ident[:, :], start=True, stop=False)
                            nc.tensor.matmul(o, bd[b][:, k, :], g.ident[:, :], start=False, stop=False)
                            nc.tensor.matmul(o, g.wr[:, :], ra[b][:, k, :], start=False,
                                             stop=True).then_inc(summed, 1)
                        if j > 0:
                            u = j - 1
                            pe.wait_ge(silu1, i * per + (u + 3))
                            pe.wait_ge(added, i * per + (u + 1))
                            o = p2[u % 2][:, 0:D]
                            nc.tensor.matmul(o, h1[u % 2][:, :], g.wm2[:, :], start=True, stop=False)
                            nc.tensor.matmul(o, g.ones[0:1, :], g.bm2[0:1, :], start=False,
                                             stop=True).then_inc(summed2, 1)

            @block.scalar
            def _(act):
                with act.Fori(0, passes) as i:
                    for j in range(per + 2):
                        if j < per:
                            b, k = divmod(j, KC)
                            if k == 0:
                                act.wait_ge(listed[b], i * 48 + 48)
                                nc.scalar.activation(ra[b][:, :, :], ra[b][:, :, :], ACT.Square,
                                                     bias=g.noff[:, 0:1]).then_inc(sqd, 1)
                                act.wait_ge(sqd, nth(i, b))
                                nc.scalar.activation(ra[b][:, :, :], ra[b][:, :, :], ACT.Exp,
                                                     scale=coeff).then_inc(radial, 1)
                            act.wait_ge(summed, i * per + (j + 1))
                            nc.scalar.activation(t1[j % 2][:, :], p1[j % 2][:, 0:P], ACT.Tanh,
                                                 scale=0.5).then_inc(tanh1, 1)
                        if 1 <= j <= per:
                            u = j - 1
                            act.wait_ge(summed2, i * per + (u + 1))
                            nc.scalar.activation(t2[u % 2][:, :], p2[u % 2][:, 0:D], ACT.Tanh,
                                                 scale=0.5).then_inc(tanh2, 1)

            @block.vector
            def _(v):
                for b in range(NB):
                    nc.vector.memset(r[b][:, :, :], 0.0)
                nc.vector.memset(dg[:, :], 0.0).then_inc(cleared, 1)
                v.wait_ge(cleared, 1)
                v.sem_inc(silu1, 2)
                v.sem_inc(added, 2)
                with v.Fori(0, passes) as i:
                    for j in range(per + 1):
                        if j < per:
                            v.wait_ge(tanh1, i * per + (j + 1))
                            nc.vector.scalar_tensor_tensor(h1[j % 2][:, :], t1[j % 2][:, :], 1.0,
                                                           p1[j % 2][:, 0:P], ALU.add, ALU.mult).then_inc(silu1, 1)
                        if j > 0:
                            u = j - 1
                            b, k = divmod(u, KC)
                            v.wait_ge(tanh2, i * per + (u + 1))
                            v.wait_ge(added, i * per + (u + 2))
                            nc.vector.scalar_tensor_tensor(h2[u % 2][:, :], t2[u % 2][:, :], 1.0,
                                                           p2[u % 2][:, 0:D], ALU.add, ALU.mult).then_inc(silu2, 1)
                            v.wait_ge(silu2, i * per + (u + 1))
                            prev = r[b][:, k - 1, 0:D] if k else r[(b - 1) % NB][:, KC - 1, 0:D]
                            nc.vector.scalar_tensor_tensor(r[b][:, k, 0:D], prev, fac[b][:, 0, k:k + 1],
                                                           h2[u % 2][:, :], ALU.mult, ALU.add).then_inc(added, 1)
                            if k == KC - 1:
                                nc.vector.tensor_tensor_scan(dg[:, 1:KC + 1], fac[b][:, 0, :],
                                                             g.ones[:, 0:KC], dg[:, 0:1], ALU.mult,
                                                             ALU.add).then_inc(degrees, 1)
                                v.wait_ge(degrees, i * (2 * NB) + (2 * b + 1))
                                nc.vector.tensor_copy(r[b][:, :, DEN], dg[:, 1:KC + 1])
                                nc.vector.tensor_copy(dg[:, 0:1], dg[:, KC:KC + 1]).then_inc(degrees, 1)
                                v.wait_ge(degrees, i * (2 * NB) + (2 * b + 2))
                                v.wait_ge(added, i * per + (u + 3))
                                v.sem_inc(stated, 1)
                nc.vector.tensor_copy(g.last[:, :], r[NB - 1][:, KC - 1, :]).then_inc(cleared, 1)
                v.wait_ge(cleared, 2)


def phase_update(g):
    nc = g.nc
    pre = "u_"
    with ExitStack() as ctx:
        def sb(name, shape, dt=F32):
            return [ctx.enter_context(nc.sbuf_tensor(f"{pre}{name}{b}", shape, dt)) for b in range(2)]

        x = sb("x", [P, Q, D])
        ag = sb("ag", [P, Q, ROW])
        xt = sb("xt", [P, CHUNK])
        at = sb("at", [P, CHUNK])
        dt = sb("dt", [2 * HEADS, CHUNK])
        th = sb("th", [P, CHUNK])
        u = sb("u", [P, CHUNK])
        th2 = sb("th2", [P, CHUNK])
        u2 = sb("u2", [P, CHUNK])
        y = sb("y", [P, Q, D])
        st = sb("st", [P, Q, 6])
        mv = sb("mv", [P, Q, 2])
        ve = sb("ve", [P, Q])
        rs = sb("rs", [P, Q])
        xn = sb("xn", [P, Q, D])
        px = ctx.enter_context(nc.psum_tensor(pre + "px", [P, 512], F32))
        pa = ctx.enter_context(nc.psum_tensor(pre + "pa", [P, 512], F32))
        pd = ctx.enter_context(nc.psum_tensor(pre + "pd", [P, 512], F32))
        pu = [ctx.enter_context(nc.psum_tensor(f"{pre}pu{b}", [P, 512], F32)) for b in range(2)]
        pv = [ctx.enter_context(nc.psum_tensor(f"{pre}pv{b}", [P, 512], F32)) for b in range(2)]
        py = ctx.enter_context(nc.psum_tensor(pre + "py", [P, 512], F32))
        loaded = [g.sem(f"{pre}loaded{b}") for b in range(2)]
        turned = g.sem(pre + "turned")
        copied = g.sem(pre + "copied")
        sum1 = g.sem(pre + "sum1")
        tanh1 = g.sem(pre + "tanh1")
        silu1 = g.sem(pre + "silu1")
        sum2 = g.sem(pre + "sum2")
        tanh2 = g.sem(pre + "tanh2")
        silu2 = g.sem(pre + "silu2")
        sum3 = g.sem(pre + "sum3")
        read3 = g.sem(pre + "read3")
        varasked = g.sem(pre + "varasked")
        scale = g.sem(pre + "scale")
        normed = g.sem(pre + "normed")
        stored = [g.sem(f"{pre}stored{b}") for b in range(2)]
        freed = g.sem(pre + "freed")
        ch = g.sem(pre + "chain")
        gate = g.sem(pre + "gate")
        half = NCHUNK // 2
        with nc.Block() as block:
            @block.sync
            def _(sp):
                with sp.Fori(0, half) as i:
                    for b in range(2):
                        sp.wait_ge(normed, pair(i, b))
                        sp.dma_start(x[b][:, :, :], rows(g.x[3], i * 2 + b)).then_inc(loaded[b], 16)
                        sp.dma_start(ag[b][:, :, :], rows(g.seg, i * 2 + b)).then_inc(loaded[b], 16)

            @block.gpsimd
            def _(pool):
                with pool.Fori(0, half) as i:
                    for b in range(2):
                        pool.wait_ge(varasked, pair(i, b))
                        pool.tensor_tensor(rs[b][:, :], ve[b][:, :], g.mhalf[:, 0:Q], ALU.pow).then_inc(scale, 1)
                    for b in range(2):
                        gated(pool, stored[b], i * 16 + 16, freed)

            @block.tensor
            def _(pe):
                mm = nc.tensor.matmul
                with pe.Fori(0, half) as i:
                    for b in range(2):
                        pe.wait_ge(loaded[b], i * 32 + 32)
                        pe.wait_ge(copied, pair(i, b))
                        for q in range(Q):
                            qs = slice(q * P, (q + 1) * P)
                            nc.tensor.transpose(px[:, qs], x[b][:, q, :], g.ident[:, :])
                            nc.tensor.transpose(pa[:, qs], ag[b][:, q, 0:D], g.ident[:, :])
                            last = nc.tensor.transpose(pd[0:2 * HEADS, qs], ag[b][:, q, D:ROW], g.ident[:, :])
                        last.then_inc(turned, 1)
                    for b in range(2):
                        pe.wait_ge(copied, pair(i, b) + 1)
                        mm(pu[b][:, :], g.wu1a[:, :], xt[b][:, :], start=True, stop=False)
                        mm(pu[b][:, :], g.wc[:, :], at[b][:, :], start=False, stop=False)
                        mm(pu[b][:, :], g.bc[:, :], dt[b][:, :], start=False, stop=True).then_inc(sum1, 1)
                    for b in range(2):
                        pe.wait_ge(silu1, pair(i, b))
                        mm(pv[b][:, :], g.wd[:, :], u[b][:, :], start=True, stop=True).then_inc(sum2, 1)
                    for b in range(2):
                        pe.wait_ge(silu2, pair(i, b))
                        pe.wait_ge(read3, pair(i, b))
                        for q in range(Q):
                            last = mm(py[:, q * P:(q + 1) * P], u2[b][:, q * P:(q + 1) * P], g.wi2[:, :], start=True,
                                      stop=True)
                        last.then_inc(sum3, 1)

            @block.scalar
            def _(act):
                act.sem_inc(copied, 1)
                with act.Fori(0, half) as i:
                    for b in range(2):
                        act.wait_ge(turned, pair(i, b))
                        nc.scalar.copy(xt[b][:, :], px[:, :])
                        nc.scalar.copy(at[b][:, :], pa[:, :])
                        nc.scalar.copy(dt[b][:, :], pd[0:2 * HEADS, :]).then_inc(copied, 1)
                    for b in range(2):
                        act.wait_ge(sum1, pair(i, b))
                        nc.scalar.activation(th[b][:, :], pu[b][:, :], ACT.Tanh, bias=g.bu1[:, 1:2],
                                             scale=0.5).then_inc(tanh1, 1)
                    for b in range(2):
                        act.wait_ge(sum2, pair(i, b))
                        nc.scalar.activation(th2[b][:, :], pv[b][:, :], ACT.Tanh, bias=g.bd[:, 1:2],
                                             scale=0.5).then_inc(tanh2, 1)
                    for b in range(2):
                        act.wait_ge(normed, pair(i, b) + 2)
                        act.dma_start(rows(g.out, i * 2 + b), xn[b][:, :, :]).then_inc(stored[b], 16)

            @block.vector
            def _(v):
                v.sem_inc(read3, 1)
                v.sem_inc(normed, 2)
                v.sem_inc(freed, 2)
                per = 2 * (11)
                bb = g.bi2[:, :].unsqueeze(1).to_broadcast([P, Q, D])
                with v.Fori(0, half) as i:
                    own = Own(v, ch, i, per)

                    def silu(b, o, t, p, bias, done):
                        own.link(nc.vector.tensor_scalar(o[b][:, :], p[b][:, :], bias, None, ALU.add))
                        nc.vector.scalar_tensor_tensor(o[b][:, :], t[b][:, :], 1.0, o[b][:, :], ALU.add,
                                                       ALU.mult).then_inc(done, 1)

                    for b in range(2):
                        v.wait_ge(tanh1, pair(i, b))
                        silu(b, u, th, pu, g.bu1[:, 0:1], silu1)
                    for b in range(2):
                        v.wait_ge(tanh2, pair(i, b))
                        silu(b, u2, th2, pv, g.bd[:, 0:1], silu2)
                    for b in range(2):
                        v.wait_ge(sum3, pair(i, b))
                        nc.vector.tensor_tensor(y[b][:, :, :], py[:, :].rearrange("p (q d) -> p q d", q=Q),
                                                x[b][:, :, :], ALU.add).then_inc(read3, 1)
                        v.wait_ge(read3, pair(i, b) + 1)
                        own.link(nc.vector.tensor_tensor(y[b][:, :, :], y[b][:, :, :], bb, ALU.add))
                        norm_stats(nc, own, gate, y[b], st[b], mv[b], ve[b]).then_inc(varasked, 1)
                    for b in range(2):
                        v.wait_ge(scale, pair(i, b))
                        v.wait_ge(freed, pair(i, b))
                        norm_apply(nc, xn[b], y[b], mv[b], rs[b]).then_inc(normed, 1)
                    own.end()



PHASES = [
    phase_weights, phase_edges,
    phase_product, phase_map, phase_log,
    lambda g: phase_attend(g, 0, HEADS), lambda g: phase_join(g, 0, HEADS), lambda g: phase_settle(g, 0, HEADS),
    lambda g: phase_attend(g, 1, 1), lambda g: phase_join(g, 1, 1), lambda g: phase_settle(g, 1, 1),
    lambda g: phase_relate(g, 0), lambda g: phase_join(g, 2, 0), lambda g: phase_gru(g, 0),
    lambda g: phase_relate(g, 1), lambda g: phase_join(g, 3, 0), lambda g: phase_gru(g, 1),
    phase_filter, lambda g: phase_join(g, 4, 0), phase_update,
]


def gnn_kernel(nc, ins, out):
    with ExitStack() as ctx:
        g = Program(nc, ins, out, ctx)
        for phase in PHASES:
            g.sems = []
            with ExitStack() as g.sem_ctx:
                phase(g)
                with nc.Block() as block:
                    @block.gpsimd
                    def _(pool):
                        for sem in g.sems:
                            pool.sem_clear(sem)



def kernel(**inputs):
    import numpy as np
    import concourse.bacc as bacc
    from concourse.bass_utils import run_bass_kernel_spmd

    a = {k: np.asarray(v) for k, v in inputs.items()}

    def padded(v, n, fill=0):
        out = np.full((n,) + v.shape[1:], fill, v.dtype)
        out[:v.shape[0]] = v
        return out

    def col(v):
        return v.reshape(-1, 1)

    def row(v):
        return v.reshape(1, -1)

    att = a["L0_gnn_att"][0]
    dh = D // HEADS
    attm = np.zeros((HEADS, dh, 2 * HEADS), att.dtype)
    for h in range(HEADS):
        attm[h, :, h] = att[h, dh:]
        attm[h, :, HEADS + h] = att[h, :dh]
    lay = {
        "x": padded(a["x"], NPAD),
        "src": padded(a["src"], P * KE).reshape(P, KE),
        "dst": padded(a["dst"], P * KE, N).reshape(P, KE),
        "etype": padded(a["edge_type_8"], P * KE).reshape(P, KE),
        "dist": padded(a["edge_weight"], P * KE).reshape(P, KE),
        "w0": a["L0_gnn_W"], "w0t": a["L0_gnn_W"].T, "attm": attm.reshape(D, 2 * HEADS),
        "lin_bias": col(a["L0_gnn_lin_bias"]), "conv_bias": row(a["L0_gnn_conv_bias"]),
        "w1": a["L1_gnn_W"], "w1t": a["L1_gnn_W"].T,
        "att1": np.stack([a["L1_gnn_att_src"], a["L1_gnn_att_dst"]], 1), "bias1": row(a["L1_gnn_bias"]),
        "projwt": a["L2_gnn_node_proj_w"].T, "projb": col(a["L2_gnn_node_proj_b"]),
        "edgew": a["L2_gnn_edge_W"].transpose(0, 3, 1, 2),
        "wiht": a["L2_gnn_gru_wih"].transpose(0, 2, 1), "whht": a["L2_gnn_gru_whh"].transpose(0, 2, 1),
        "biht": a["L2_gnn_gru_bih"].reshape(2, 3, D).transpose(0, 2, 1),
        "bhht": a["L2_gnn_gru_bhh"].reshape(2, 3, D).transpose(0, 2, 1),
        "outwt": a["L2_gnn_out_w"].T, "out_b": row(a["L2_gnn_out_b"]),
        "wm1": a["L3_gnn_Wm1"], "bm1": row(a["L3_gnn_bm1"]), "wm2": a["L3_gnn_Wm2"],
        "bm2": row(a["L3_gnn_bm2"]), "wm3t": a["L3_gnn_Wm3"].T, "bm3": col(a["L3_gnn_bm3"]),
        "wu1": a["L3_gnn_Wu1"], "bu1": col(a["L3_gnn_bu1"]), "wu2t": a["L3_gnn_Wu2"].T,
        "bu2": col(a["L3_gnn_bu2"]), "wi1": a["L3_gnn_Wi1"], "bi1": col(a["L3_gnn_bi1"]),
        "wi2": a["L3_gnn_Wi2"], "bi2": row(a["L3_gnn_bi2"]),
    }
    lay = {k: np.ascontiguousarray(v) for k, v in lay.items()}
    nc = bacc.Bacc("TRN2", target_bir_lowering=False, num_devices=1)
    ins = {k: nc.dram_tensor(f"in_{k}", v.shape, mybir.dt.from_np(v.dtype), kind="ExternalInput").ap()
           for k, v in lay.items()}
    out = nc.dram_tensor("out", [NPAD, D], F32, kind="ExternalOutput").ap()
    gnn_kernel(nc, ins, out)
    r = run_bass_kernel_spmd(nc, [{f"in_{k}": v for k, v in lay.items()}], core_ids=[0])
    return r.results[0]["out"][:N]
```

```python
from contextlib import ExitStack

import concourse.bass as bass
from concourse import mybir

F32 = mybir.dt.float32
I32 = mybir.dt.int32
ALU = mybir.AluOpType
ACT = mybir.ActivationFunctionType
AX_X = mybir.AxisListType.X

P = 128
D = 128
N = 50000
E = 50000
HEADS = 4
TYPES = 8
RADIAL = 50
CUTOFF = 10.0

Q = 4
CHUNK = P * Q
G = 14
B = 7
R = 2
NCHUNK = -(-N // CHUNK)
NPAD = NCHUNK * CHUNK
COLS = NCHUNK * Q
KC = 14
NB = 4
ECHUNK = -(-E // (P * KC))
KE = ECHUNK * KC
assert ECHUNK % NB == 0 and NCHUNK % G == 0 and NPAD == P * KE
assert ECHUNK == 4 * (NCHUNK // G) and G == 2 * B and KC % B == 0
ROW = D + 2 * HEADS
TROW = D + HEADS
DEN = D
MAXC = D + HEADS
LOWEST = -1.0e30
EMPTY = NPAD
SKIP = 1 << 20
EPS = 1e-5
MIN_NORM = 1e-15
MAX_NORM = 1.0 - 0.004
SLOPE = 0.2


def nth_node(i, b, ago=0):
    return i * G + (b + 1 - ago)


def turn(i, b):
    return i * (G // B) + (b // B + 1)


def step(t, lag):
    return [t - lag] if 0 <= t - lag < G else []


class Own:

    def __init__(self, eng, sem, i=None, per=0):
        self.eng, self.sem, self.per, self.n = eng, sem, per, 0
        self.base = None if i is None else eng.snap(i * per)

    def mark(self, ins):
        self.n += 1
        ins.then_inc(self.sem, 1)
        return self.n

    def wait(self, n=None):
        n = self.n if n is None else n
        self.eng.wait_ge(self.sem, n if self.base is None else self.base + n)

    def link(self, ins):
        self.mark(ins)
        self.wait()

    def end(self):
        assert self.base is None or self.n == self.per, (self.sem, self.n, self.per)


def gated(eng, sem, value, gate):
    eng.wait_ge(sem, value)
    eng.sem_inc(gate, 1)


class Program:

    def __init__(self, nc, ins, out, ctx):
        self.nc, self.ins, self.out, self.ctx = nc, ins, out, ctx

        def table(name, shape, dt=F32):
            return nc.dram_tensor(name, shape, dt, kind="Internal").ap()

        self.edge_idx = table("edge_idx", [ECHUNK, P, 2, KC], I32)
        self.place_idx = table("place_idx", [ECHUNK, P, 2, KC], I32)
        self.place = table("place", [NPAD, 1], I32)
        self.edge_fac = table("edge_fac", [ECHUNK, P, 2, KC])
        self.records = [table(f"records{n}", [NPAD, 4], I32) for n in range(2)]
        self.type_rows = table("type_rows", [KE, P])
        self.dist_rows = table("dist_rows", [KE, P])
        self.mx = table("mx", [NPAD, ROW])
        self.states = table("states", [EMPTY + P, ROW])
        self.sums = table("sums", [EMPTY + P, D])
        self.t = [table(f"t{n}", [NPAD, TROW]) for n in range(2)]
        self.ai = [table(f"ai{n}", [NPAD, HEADS]) for n in range(2)]
        self.x = [None] + [table(f"x{n}", [NPAD, D]) for n in (1, 2, 3)]
        self.ht = [table(f"ht{n}", [NCHUNK, P, CHUNK]) for n in range(2)]
        self.hr = [table(f"hr{n}", [NPAD, D]) for n in range(2)]
        self.ta = table("ta", [NPAD, D])
        self.tb = table("tb", [NPAD, D])

        self.ident = self.sb("ident", [P, P])
        self.ones = self.sb("ones", [P, P])
        self.half = self.sb("half", [P, 2 * Q])
        self.mhalf = self.sb("mhalf", [P, 2 * Q])
        self.w0aug = self.sb("w0aug", [P, ROW + 1])
        self.yrow = self.sb("yrow", [P, ROW])
        self.y2 = self.sb("y2", [P, 1])
        self.w1aug = self.sb("w1aug", [P, D + 2])
        self.bias0 = self.sb("bias0", [P, D])
        self.bias1 = self.sb("bias1", [P, D])
        self.outb = self.sb("outb", [P, D])
        self.sxx = self.sb("sxx", [P, COLS])
        self.smm = self.sb("smm", [P, COLS])
        self.sxy = self.sb("sxy", [P, COLS])
        self.alpha = self.sb("alpha", [P, COLS])
        self.beta = self.sb("beta", [P, COLS])
        self.bi2 = self.sb("bi2", [P, D])
        self.bab = self.sb("bab", [P, 2, D])
        self.bm2 = self.sb("bm2", [P, D])
        self.projw = self.sb("projw", [P, D])
        self.projb = self.sb("projb", [P, 1])
        self.wih = [self.sb(f"wih{n}", [P, 3 * D]) for n in range(2)]
        self.whh = [self.sb(f"whh{n}", [P, 3 * D]) for n in range(2)]
        self.gb = [self.sb(f"gb{n}", [P, 4]) for n in range(2)]
        self.outw = self.sb("outw", [P, D])
        self.wm1 = self.sb("wm1", [P, 2 * D])
        self.wr = self.sb("wr", [RADIAL, D])
        self.wm2 = self.sb("wm2", [P, D])
        self.wu1a = self.sb("wu1a", [P, D])
        self.wc = self.sb("wc", [P, D])
        self.bc = self.sb("bc", [2 * HEADS, D])
        self.bu1 = self.sb("bu1", [P, 2])
        self.wd = self.sb("wd", [P, D])
        self.bd = self.sb("bd", [P, 2])
        self.wi2 = self.sb("wi2", [P, D])
        self.noff = self.sb("noff", [RADIAL, 1])
        self.cross = self.sb("cross", [P, P])
        self.cross_t = self.sb("cross_t", [P, P])
        self.low_t = self.sb("low_t", [P, P])
        self.last = self.sb("last", [P, ROW])
        self.goes_on = self.sb("goes_on", [P, 1])
        self.first_i = self.sb("first_i", [P, 1], I32)
        self.first_row = self.sb("first_row", [P, 1], I32)
        self.fix_row = self.sb("fix_row", [P, 1], I32)
        self.places = self.sb("places", [P, (NCHUNK + B) * Q], I32)

    def sb(self, name, shape, dt=F32):
        return self.ctx.enter_context(self.nc.sbuf_tensor(name, shape, dt))

    def indirect_sem(self, name):
        return self.ctx.enter_context(self.nc.semaphore(name))

    def sem(self, name):
        s = self.sem_ctx.enter_context(self.nc.semaphore(name))
        self.sems.append(s)
        return s


def rows(table, c, q=Q):
    r = table.rearrange("(c p q) d -> c p q d", p=P, q=q)
    return r[bass.ds(c, 1)].rearrange("c p q d -> (c p) q d")



def phase_weights(g):
    nc, ins = g.nc, g.ins
    with ExitStack() as ctx:
        def sb(name, shape, dt=F32):
            return ctx.enter_context(nc.sbuf_tensor(name, shape, dt))

        w0 = sb("w_w0", [P, D])
        attm = sb("w_attm", [P, 2 * HEADS])
        linb = sb("w_linb", [P, 1])
        w1t = sb("w_w1t", [P, D])
        att1 = sb("w_att1", [P, 2])
        bih = [sb(f"w_bih{n}", [P, 3]) for n in range(2)]
        bhh = [sb(f"w_bhh{n}", [P, 3]) for n in range(2)]
        wm2 = sb("w_wm2", [P, D])
        wm3t = sb("w_wm3t", [P, D])
        wu1b = sb("w_wu1b", [P, D])
        bm3 = sb("w_bm3", [P, 1])
        bu1 = sb("w_bu1", [P, 1])
        wu2t = sb("w_wu2t", [P, D])
        wi1 = sb("w_wi1", [P, D])
        bu2 = sb("w_bu2", [P, 1])
        bi1 = sb("w_bi1", [P, 1])
        wi2 = sb("w_wi2", [P, D])
        zeros = sb("w_zeros", [P, P])
        rim = sb("w_rim", [P, ROW])
        b2 = sb("w_b2", [P, 1])
        sc = sb("w_sc", [P, 8])
        y = sb("w_y", [P, 1])
        ybc = sb("w_ybc", [P, P])
        offi = sb("w_offi", [RADIAL, 1], I32)
        offf = sb("w_offf", [RADIAL, 1])
        empty = sb("w_empty", [P, ROW])
        nowhere = sb("w_nowhere", [P, NPAD // P], I32)
        pw = ctx.enter_context(nc.psum_tensor("w_pw", [P, 8, 512], F32))

        loaded = g.sem("w_loaded")
        made = g.sem("w_made")
        norm2 = g.sem("w_norm2")
        root = g.sem("w_root")
        tanh = g.sem("w_tanh")
        yready = g.sem("w_yready")
        folded = g.sem("w_folded")
        ch = g.sem("w_chain")
        chp = g.sem("w_chain_pool")
        zeroed = g.sem("w_zeroed")
        zrow = g.sem("w_zrow")
        done = g.sem("w_done")

        loads = [
            (g.w0aug[:, 0:D], ins["w0t"]), (w0[:, :], ins["w0"]), (attm[:, :], ins["attm"]),
            (linb[:, :], ins["lin_bias"]), (g.w1aug[:, 0:D], ins["w1"]), (w1t[:, :], ins["w1t"]),
            (att1[:, :], ins["att1"]), (g.projw[:, :], ins["projwt"]), (g.projb[:, :], ins["projb"]),
            (g.wih[0][:, :], ins["wiht"][0]), (g.wih[1][:, :], ins["wiht"][1]),
            (g.whh[0][:, :], ins["whht"][0]), (g.whh[1][:, :], ins["whht"][1]),
            (bih[0][:, :], ins["biht"][0]), (bih[1][:, :], ins["biht"][1]),
            (bhh[0][:, :], ins["bhht"][0]), (bhh[1][:, :], ins["bhht"][1]),
            (g.outw[:, :], ins["outwt"]), (g.wm1[:, 0:D], ins["wm1"][0:D]),
            (g.wm1[:, D:2 * D], ins["wm1"][D:2 * D]), (g.wr[:, :], ins["wm1"][2 * D:2 * D + RADIAL]),
            (wm2[:, :], ins["wm2"]), (wm3t[:, :], ins["wm3t"]), (g.wu1a[:, :], ins["wu1"][0:D]),
            (wu1b[:, :], ins["wu1"][D:2 * D]), (bm3[:, :], ins["bm3"]), (bu1[:, :], ins["bu1"]),
            (wu2t[:, :], ins["wu2t"]), (wi1[:, :], ins["wi1"]), (bu2[:, :], ins["bu2"]),
            (bi1[:, :], ins["bi1"]), (wi2[:, :], ins["wi2"]),
        ]
        for tile, name in ((g.bias0, "conv_bias"), (g.bias1, "bias1"), (g.outb, "out_b"),
                           (g.bi2, "bi2"), (g.bab[:, 1, :], "bm1"), (g.bm2, "bm2")):
            loads.append((tile if name == "bm1" else tile[:, :], ins[name].to_broadcast([P, D])))

        with nc.Block() as block:
            @block.sync
            def _(sp):
                for dst, src in loads:
                    sp.dma_start(dst, src).then_inc(loaded, 16)
                sp.wait_ge(loaded, 16 * len(loads))

            @block.gpsimd
            def _(pool):
                own = Own(pool, chp)
                pool.memset(g.ones[:, :], 1.0).then_inc(made, 1)
                pool.memset(g.half[:, :], 0.5).then_inc(made, 1)
                pool.memset(g.mhalf[:, :], -0.5).then_inc(made, 1)
                pool.iota(offi[:, :], pattern=[[0, 1]], base=0, channel_multiplier=1).then_inc(made, 1)
                own.link(pool.memset(g.ident[:, :], 0.0))
                pool.affine_select(out=g.ident[:, :], in_=g.ident[:, :], compare_op=ALU.not_equal,
                                   fill=1.0, base=0, pattern=[[-1, P]], channel_multiplier=1).then_inc(made, 1)
                pool.wait_ge(norm2, 2)
                pool.wait_ge(made, 5)
                pool.tensor_tensor(sc[:, 1:2], sc[:, 0:1], g.half[:, 0:1], ALU.pow).then_inc(root, 1)

            @block.scalar
            def _(act):
                act.wait_ge(zrow, 1)
                act.dma_start(g.states[EMPTY:EMPTY + P, :], empty[:, :]).then_inc(zeroed, 16)
                act.dma_start(g.sums[EMPTY:EMPTY + P, :], empty[:, 0:D]).then_inc(zeroed, 16)
                act.dma_start(g.place.rearrange("(p n) o -> p (n o)", p=P), nowhere[:, :]).then_inc(zeroed, 16)
                act.wait_ge(root, 1)
                nc.scalar.activation(sc[:, 2:3], sc[:, 1:2], ACT.Tanh).then_inc(tanh, 1)
                act.wait_ge(zeroed, 16 * 3)

            @block.tensor
            def _(pe):
                pe.wait_ge(ch, 1)
                pe.wait_ge(made, 5)
                nc.tensor.matmul(pw[:, 0, 0:1], g.ones[:, :], b2[:, :], start=True, stop=True).then_inc(norm2, 1)
                pe.wait_ge(loaded, 16 * len(loads))
                mm = nc.tensor.matmul
                mm(pw[:, 1, 0:8], w0[:, :], attm[:, :], start=True, stop=True)
                mm(pw[:, 2, 0:2], w1t[:, :], att1[:, :], start=True, stop=True)
                mm(pw[:, 3, 0:D], wm3t[:, :], wu1b[:, :], start=True, stop=True)
                mm(pw[0:1, 4, 0:D], bm3[:, :], wu1b[:, :], start=True, stop=True)
                mm(pw[:, 5, 0:D], wu2t[:, :], wi1[:, :], start=True, stop=True)
                mm(pw[:, 6, 0:1], wi1[:, :], bu2[:, :], start=True, stop=True).then_inc(folded, 1)
                pe.wait_ge(yready, 1)
                mm(pw[:, 7, 0:1], w0[:, :], y[:, :], start=True, stop=True).then_inc(folded, 1)
                mm(pw[:, 0, 0:ROW], ybc[:, :], rim[:, :], start=True, stop=True)
                mm(pw[:, 0, 256:257], ybc[:, :], y[:, :], start=True, stop=True).then_inc(folded, 1)

            @block.vector
            def _(v):
                own = Own(v, ch)
                v.wait_ge(loaded, 16 * len(loads))
                own.mark(nc.vector.tensor_tensor(b2[:, :], linb[:, :], linb[:, :], ALU.mult))
                nc.vector.memset(nowhere[:, :], EMPTY)
                nc.vector.memset(empty[:, 0:MAXC], 0.0)
                nc.vector.memset(empty[:, MAXC:ROW], LOWEST).then_inc(zrow, 1)
                v.wait_ge(made, 5)
                own.mark(nc.vector.tensor_copy(offf[:, :], offi[:, :]))
                own.mark(nc.vector.tensor_copy(rim[:, 0:D], g.ident[:, :]))
                own.mark(nc.vector.tensor_copy(rim[:, D:ROW], attm[:, :]))
                own.wait()
                own.mark(nc.vector.tensor_scalar(g.noff[:, :], offf[:, :], -CUTOFF / (RADIAL - 1), None, ALU.mult))
                for n in range(2):
                    own.link(nc.vector.tensor_tensor(sc[:, 3:5], bih[n][:, 0:2], bhh[n][:, 0:2], ALU.add))
                    own.mark(nc.vector.tensor_scalar(g.gb[n][:, 0:2], sc[:, 3:5], 0.5, None, ALU.mult))
                    own.mark(nc.vector.tensor_copy(g.gb[n][:, 2:3], bih[n][:, 2:3]))
                    own.mark(nc.vector.tensor_copy(g.gb[n][:, 3:4], bhh[n][:, 2:3]))
                    own.wait()
                own.mark(nc.vector.tensor_scalar(g.wm2[:, :], wm2[:, :], 0.5, None, ALU.mult))
                own.mark(nc.vector.tensor_scalar(g.wi2[:, :], wi2[:, :], 0.5, None, ALU.mult))
                own.mark(nc.vector.tensor_copy(g.bu1[:, 0:1], bu1[:, :]))
                own.mark(nc.vector.tensor_scalar(g.bu1[:, 1:2], bu1[:, :], 0.5, None, ALU.mult))
                own.mark(nc.vector.memset(g.bc[:, :], 0.0))
                own.mark(nc.vector.memset(g.bab[:, 0, :], 0.0))
                own.wait()
                v.wait_ge(norm2, 1)
                nc.vector.tensor_scalar(sc[:, 0:1], pw[:, 0, 0:1], MIN_NORM ** 2, None, ALU.max).then_inc(norm2, 1)
                v.wait_ge(folded, 1)
                own.mark(nc.vector.tensor_copy(g.w0aug[:, D:ROW], pw[:, 1, 0:8]))
                own.mark(nc.vector.tensor_copy(g.w1aug[:, D:D + 2], pw[:, 2, 0:2]))
                own.mark(nc.vector.tensor_scalar(g.wc[:, :], pw[:, 3, 0:D], 0.5, None, ALU.mult))
                own.mark(nc.vector.tensor_copy(g.bc[0:1, :], pw[0:1, 4, 0:D]))
                own.mark(nc.vector.tensor_scalar(g.wd[:, :], pw[:, 5, 0:D], 0.5, None, ALU.mult))
                own.link(nc.vector.tensor_tensor(g.bd[:, 0:1], pw[:, 6, 0:1], bi1[:, :], ALU.add))
                own.mark(nc.vector.tensor_scalar(g.bd[:, 1:2], g.bd[:, 0:1], 0.5, None, ALU.mult))
                v.wait_ge(tanh, 1)
                own.mark(nc.vector.tensor_scalar(sc[:, 5:6], sc[:, 2:3], MAX_NORM, None, ALU.min))
                own.link(nc.vector.reciprocal(sc[:, 6:7], sc[:, 1:2]))
                own.link(nc.vector.tensor_tensor(sc[:, 7:8], sc[:, 5:6], sc[:, 6:7], ALU.mult))
                own.link(nc.vector.tensor_tensor(y[:, :], sc[:, 7:8], linb[:, :], ALU.mult))
                nc.vector.tensor_scalar(ybc[:, :], g.ones[:, :], y[:, 0:1], None, ALU.mult).then_inc(yready, 1)
                v.wait_ge(folded, 3)
                own.mark(nc.vector.tensor_copy(g.w0aug[:, ROW:ROW + 1], pw[:, 7, 0:1]))
                own.mark(nc.vector.tensor_copy(g.yrow[:, :], pw[:, 0, 0:ROW]))
                own.mark(nc.vector.tensor_copy(g.y2[:, :], pw[:, 0, 256:257]))
                own.wait()



def sort_edges(g, flag, src_i, dst_i, typ_i, dist, next_i):
    nc = g.nc
    digits = 256
    assert NPAD < digits * digits
    with ExitStack() as ctx:
        def sb(name, shape, dt=F32):
            return ctx.enter_context(nc.sbuf_tensor("o_" + name, shape, dt))

        rec = sb("rec", [P, KE, 4], I32)
        digit_i = sb("digit_i", [P, KE], I32)
        digit = sb("digit", [P, KE])
        ramp = sb("ramp", [P, digits])
        tri = sb("tri", [P, P])
        hot = sb("hot", [P, digits])
        seen = sb("seen", [P, digits])
        base = sb("base", [P, digits])
        upto = sb("upto", [P, digits])
        place = sb("place", [P, 1])
        place_i = sb("place_i", [P, 1], I32)
        moved = sb("moved", [P, 4], I32)
        pc = ctx.enter_context(nc.psum_tensor("o_pc", [P, 512], F32))
        pr = ctx.enter_context(nc.psum_tensor("o_pr", [P, 512], F32))
        ramped = g.sem("o_ramped")
        ch = g.sem("o_chain")
        hotch = [g.sem(f"o_count_chain{n}") for n in range(2)]
        placech = [g.sem(f"o_place_chain{n}") for n in range(2)]
        gate = g.sem("o_gate")
        gatev = g.sem("o_gatev")
        counted = g.sem("o_counted")
        totalled = g.sem("o_totalled")
        hotted = [g.sem(f"o_hotted{n}") for n in range(2)]
        ranked = [g.sem(f"o_ranked{n}") for n in range(2)]
        placed = [g.sem(f"o_placed{n}") for n in range(2)]
        put = [g.indirect_sem(f"o_put{n}") for n in range(2)]
        room = [g.sem(f"o_room{n}") for n in range(2)]
        loaded = g.sem("o_loaded")
        with nc.Block() as block:
            @block.gpsimd
            def _(pool):
                with pool.If(pool.value_load(flag[0:1, 0:1], min_val=0, max_val=1)):
                    own = Own(pool, ramped)
                    own.mark(pool.iota(ramp[:, :], pattern=[[1, digits]], base=0, channel_multiplier=0,
                                       allow_small_or_imprecise_dtypes=True))
                    own.link(pool.memset(tri[:, :], 1.0))
                    own.mark(pool.affine_select(out=tri[:, :], in_=tri[:, :], compare_op=ALU.is_gt, fill=0.0, base=0,
                                                pattern=[[1, P]], channel_multiplier=-1))
                    for n in range(2):
                        pool.sem_inc(room[n], 1)
                        with pool.Fori(0, KE) as j:
                            gated(pool, placed[n], j + 1, gate)
                            pool.indirect_dma_start(
                                out=g.records[n], out_offset=bass.IndirectOffsetOnAxis(ap=place_i[:, 0:1], axis=0),
                                in_=moved[:, :], in_offset=None, bounds_check=NPAD - 1, oob_is_err=False
                            ).then_inc(put[n], 16)
                            gated(pool, put[n], j * 16 + 16, room[n])

            @block.sync
            def _(sp):
                with sp.If(sp.value_load(flag[0:1, 0:1], min_val=0, max_val=1)):
                    sp.wait_ge(room[0], KE + 1)
                    parts = 8
                    step = KE // parts
                    by = g.records[0].rearrange("(j p) c -> p j c", p=P)
                    for a in range(parts):
                        sp.dma_start(rec[:, a * step:(a + 1) * step, :],
                                     by[:, a * step:(a + 1) * step, :]).then_inc(loaded, 16)
                    sp.wait_ge(room[1], KE + 1)
                    sp.dma_start(rec[:, :, :], g.records[1].rearrange("(p k) c -> p k c", p=P)).then_inc(loaded, 16)
                    with nc.allow_non_contiguous_dma(reason="one word of each partition"):
                        sp.dma_start(next_i[0:P - 1, :], g.records[1].rearrange("(p k) c -> p k c", p=P)[1:P, 0, 1:2]
                                     ).then_inc(loaded, 16)

            @block.tensor
            def _(pe):
                with pe.If(pe.value_load(flag[0:1, 0:1], min_val=0, max_val=1)):
                    pe.wait_ge(ramped, 3)
                    for n in range(2):
                        pe.wait_ge(counted, n + 1)
                        nc.tensor.matmul(pc[:, 0:digits], g.ones[:, :], seen[:, :], start=True,
                                         stop=True).then_inc(totalled, 1)
                        with pe.Fori(0, KE) as j:
                            pe.wait_ge(hotted[n], j + 1)
                            nc.tensor.matmul(pr[:, 0:digits], tri[:, :], hot[:, :], start=True, stop=True)
                            nc.tensor.matmul(pc[:, 0:digits], g.ones[:, :], hot[:, :], start=True,
                                             stop=True).then_inc(ranked[n], 1)

            @block.vector
            def _(v):
                with v.If(v.value_load(flag[0:1, 0:1], min_val=0, max_val=1)):
                    own = Own(v, ch)
                    own.mark(nc.vector.tensor_copy(rec[:, :, 0], src_i[:, :]))
                    own.mark(nc.vector.tensor_copy(rec[:, :, 1], dst_i[:, :]))
                    own.mark(nc.vector.tensor_copy(rec[:, :, 2], typ_i[:, :]))
                    own.link(nc.vector.tensor_copy(rec[:, :, 3], dist[:, :].bitcast(I32)))
                    v.wait_ge(ramped, 3)
                    for n in range(2):
                        if n:
                            v.wait_ge(loaded, 16 * 8)
                            own.link(nc.vector.tensor_single_scalar(digit_i[:, :], rec[:, :, 1], 8,
                                                                    op=ALU.logical_shift_right))
                        else:
                            own.link(nc.vector.tensor_single_scalar(digit_i[:, :], rec[:, :, 1], digits - 1,
                                                                    op=ALU.bitwise_and))
                        own.mark(nc.vector.tensor_copy(digit[:, :], digit_i[:, :]))
                        own.link(nc.vector.memset(seen[:, :], 0.0))
                        with v.Fori(0, KE) as j:
                            o = Own(v, hotch[n], j, 1)
                            o.mark(nc.vector.scalar_tensor_tensor(seen[:, :], ramp[:, :], digit[:, bass.ds(j, 1)],
                                                                  seen[:, :], ALU.is_equal, ALU.add))
                            o.wait()
                            o.end()
                        v.sem_inc(counted, 1)
                        v.wait_ge(totalled, n + 1)
                        own.link(nc.vector.tensor_copy(seen[:, :], pc[:, 0:digits]))
                        own.link(nc.vector.tensor_tensor_scan(upto[:, :], g.ones[:, 0:1].to_broadcast([P, digits]),
                                                              seen[:, :], 0.0, ALU.mult, ALU.add))
                        own.link(nc.vector.tensor_tensor(base[:, :], upto[:, :], seen[:, :], ALU.subtract))
                        with v.Fori(0, KE) as j:
                            o = Own(v, placech[n], j, 6)
                            o.mark(nc.vector.tensor_scalar(hot[:, :], ramp[:, :], digit[:, bass.ds(j, 1)], None,
                                                           ALU.is_equal))
                            o.wait()
                            v.sem_inc(hotted[n], 1)
                            v.wait_ge(ranked[n], j + 1)
                            o.link(nc.vector.tensor_tensor(upto[:, :], pr[:, 0:digits], base[:, :], ALU.add))
                            o.link(nc.vector.tensor_tensor(upto[:, :], upto[:, :], hot[:, :], ALU.mult))
                            o.mark(nc.vector.tensor_tensor(base[:, :], base[:, :], pc[:, 0:digits], ALU.add))
                            o.link(nc.vector.tensor_reduce(place[:, :], upto[:, :], AX_X, ALU.add))
                            gated(v, room[n], j + 1, gatev)
                            o.mark(nc.vector.tensor_copy(place_i[:, :], place[:, :]))
                            nc.vector.tensor_copy(moved[:, :].unsqueeze(1), rec[:, bass.ds(j, 1), :]).then_inc(placed[n], 1)
                            v.wait_ge(placed[n], j + 1)
                            o.end()
                    v.wait_ge(loaded, 16 * 10)
                    own.mark(nc.vector.tensor_copy(src_i[:, :], rec[:, :, 0]))
                    own.mark(nc.vector.tensor_copy(dst_i[:, :], rec[:, :, 1]))
                    own.mark(nc.vector.tensor_copy(typ_i[:, :], rec[:, :, 2]))
                    own.link(nc.vector.tensor_copy(dist[:, :].bitcast(I32), rec[:, :, 3]))


def phase_edges(g):
    nc, ins = g.nc, g.ins
    with ExitStack() as ctx:
        def sb(name, shape, dt=F32):
            return ctx.enter_context(nc.sbuf_tensor(name, shape, dt))

        src_i = sb("e_src", [P, KE], I32)
        dst_i = sb("e_dst", [P, KE], I32)
        typ_i = sb("e_typ", [P, KE], I32)
        next_i = sb("e_nexti", [P, 1], I32)
        dist = sb("e_dist", [P, KE])
        dst = sb("e_dstf", [P, KE + 1])
        typ = sb("e_typf", [P, KE])
        same = sb("e_same", [P, KE])
        fac = sb("e_fac", [P, 2, KE])
        sct = sb("e_sct", [P, KE])
        sct_i = sb("e_scti", [P, KE], I32)
        own_row = sb("e_own_row", [P, ECHUNK, KC], I32)
        dg = sb("e_dg", [P, P])
        firstb = sb("e_firstb", [P, P])
        tri = sb("e_tri", [P, P])
        rowsb = sb("e_rows", [KE // 4, 2, 4, P])
        pt = ctx.enter_context(nc.psum_tensor("e_pt", [P, 4, 512], F32))
        loaded = g.sem("e_loaded")
        pre = g.sem("e_pre")
        cast = g.sem("e_cast")
        trid = g.sem("e_trid")
        numbered = g.sem("e_numbered")
        turned = g.sem("e_turned")
        ch = g.sem("e_chain")
        ready = g.sem("e_ready")
        stored = g.sem("e_stored")
        flag = sb("e_flag", [1, 1], I32)
        disorder = sb("e_disorder", [P, 2])
        read = g.sem("e_read")
        compared = g.sem("e_compared")
        summed = g.sem("e_summed")
        och = g.sem("e_order_chain")
        K4 = KE // 4
        with nc.Block() as block:
            @block.sync
            def _(sp):
                sp.dma_start(src_i[:, :], ins["src"]).then_inc(loaded, 16)
                sp.dma_start(dst_i[:, :], ins["dst"]).then_inc(loaded, 16)
                sp.dma_start(typ_i[:, :], ins["etype"]).then_inc(loaded, 16)
                sp.dma_start(dist[:, :], ins["dist"]).then_inc(loaded, 16)
                sp.wait_ge(pre, 1)
                with nc.allow_non_contiguous_dma(reason="one word of each partition"):
                    sp.dma_start(next_i[0:P - 1, :], ins["dst"][1:P, 0:1]).then_inc(loaded, 16)

            @block.vector
            def _(v):
                own = Own(v, och)
                nc.vector.memset(next_i[:, :], NPAD).then_inc(pre, 1)
                v.wait_ge(loaded, 16 * 5)
                own.mark(nc.vector.tensor_copy(dst[:, 0:KE], dst_i[:, :]))
                own.link(nc.vector.tensor_copy(dst[:, KE:KE + 1], next_i[:, :]))
                own.link(nc.vector.tensor_tensor(same[:, :], dst[:, 0:KE], dst[:, 1:KE + 1], ALU.is_gt))
                nc.vector.tensor_reduce(disorder[:, 0:1], same[:, :], AX_X, ALU.add).then_inc(compared, 1)
                v.wait_ge(summed, 1)
                own.link(nc.vector.tensor_scalar(disorder[0:1, 1:2], pt[0:1, 0, 0:1], 0.0, None, ALU.is_gt))
                own.link(nc.vector.tensor_copy(flag[:, :], disorder[0:1, 1:2]))

            @block.tensor
            def _(pe):
                pe.wait_ge(compared, 1)
                nc.tensor.matmul(pt[0:1, 0, 0:1], g.ones[:, 0:1], disorder[:, 0:1], start=True,
                                 stop=True).then_inc(summed, 1)

        sort_edges(g, flag, src_i, dst_i, typ_i, dist, next_i)

        with nc.Block() as block:
            @block.sync
            def _(sp):
                sp.wait_ge(ready, 2)
                sp.wait_ge(numbered, 1)
                for c in range(ECHUNK):
                    k = slice(c * KC, (c + 1) * KC)
                    sp.dma_start(g.edge_idx[c, :, 0, :], src_i[:, k]).then_inc(stored, 16)
                    sp.dma_start(g.edge_idx[c, :, 1, :], dst_i[:, k]).then_inc(stored, 16)
                    sp.dma_start(g.place_idx[c, :, 0, :], sct_i[:, k]).then_inc(stored, 16)
                    sp.dma_start(g.place_idx[c, :, 1, :], own_row[:, c, :]).then_inc(stored, 16)
                    sp.dma_start(g.edge_fac[c], fac[:, :, k]).then_inc(stored, 16)
                sp.wait_ge(ready, 3)
                for n, t in enumerate((g.type_rows, g.dist_rows)):
                    sp.dma_start(t.rearrange("(a k) p -> k a p", a=4), rowsb[:, n, :, :]).then_inc(stored, 16)
                sp.wait_ge(stored, 16 * (5 * ECHUNK + 2))

            @block.gpsimd
            def _(pool):
                own = Own(pool, cast)
                pool.iota(own_row[:, :, :], pattern=[[P * KC, ECHUNK], [1, KC]], base=0,
                          channel_multiplier=KC).then_inc(numbered, 1)
                own.link(pool.memset(tri[:, :], 1.0))
                pool.affine_select(out=tri[:, :], in_=tri[:, :], compare_op=ALU.is_gt, fill=0.0, base=0,
                                   pattern=[[1, P]], channel_multiplier=-1).then_inc(trid, 1)

            @block.tensor
            def _(pe):
                pe.wait_ge(ready, 1)
                for n, t in enumerate((typ, dist)):
                    for a in range(4):
                        last = nc.tensor.transpose(pt[0:K4, n, a * P:(a + 1) * P], t[:, a * K4:(a + 1) * K4],
                                                   g.ident[:, :])
                last.then_inc(turned, 1)
                nc.tensor.matmul(pt[:, 2, 0:P], g.ones[:, :], dg[:, :], start=True, stop=True).then_inc(turned, 1)
                pe.wait_ge(ready, 4)
                nc.tensor.transpose(pt[:, 3, 0:P], g.cross[:, :], g.ident[:, :]).then_inc(turned, 1)

            @block.vector
            def _(v):
                own = Own(v, ch)
                own.mark(nc.vector.tensor_copy(typ[:, :], typ_i[:, :]))
                own.mark(nc.vector.tensor_copy(dst[:, 0:KE], dst_i[:, :]))
                own.mark(nc.vector.tensor_copy(dst[:, KE:KE + 1], next_i[:, :]))
                own.mark(nc.vector.tensor_copy(g.first_i[:, :], dst_i[:, 0:1]))
                own.wait()
                nc.vector.tensor_scalar(dg[:, :], g.ident[:, :], dst[:, 0:1], None, ALU.mult).then_inc(ready, 1)
                own.link(nc.vector.tensor_tensor(same[:, :], dst[:, 0:KE], dst[:, 1:KE + 1], ALU.is_equal))
                own.link(nc.vector.scalar_tensor_tensor(sct[:, :], same[:, :], float(SKIP), dst[:, 0:KE],
                                                        ALU.mult, ALU.add))
                own.mark(nc.vector.tensor_copy(sct_i[:, :], sct[:, :]))
                own.mark(nc.vector.memset(fac[:, 0, 0:1], 0.0))
                own.link(nc.vector.tensor_copy(fac[:, 0, 1:KE], same[:, 0:KE - 1]))
                nc.vector.tensor_scalar(fac[:, 1, :], fac[:, 0, :], -LOWEST, LOWEST, ALU.mult,
                                        ALU.add).then_inc(ready, 1)
                v.wait_ge(turned, 1)
                own.mark(nc.vector.tensor_copy(rowsb[:, 0, :, :], pt[0:K4, 0, :].rearrange("k (a p) -> k a p", a=4)))
                nc.vector.tensor_copy(rowsb[:, 1, :, :],
                                      pt[0:K4, 1, :].rearrange("k (a p) -> k a p", a=4)).then_inc(ready, 1)
                v.wait_ge(turned, 2)
                v.wait_ge(trid, 1)
                own.link(nc.vector.tensor_copy(firstb[:, :], pt[:, 2, 0:P]))
                nc.vector.scalar_tensor_tensor(g.cross[:, :], firstb[:, :], dst[:, KE - 1:KE], tri[:, :],
                                               ALU.is_equal, ALU.mult).then_inc(ready, 1)
                v.wait_ge(turned, 3)
                own.link(nc.vector.tensor_copy(g.cross_t[:, :], pt[:, 3, 0:P]))
                own.mark(nc.vector.tensor_scalar(g.low_t[:, :], g.cross_t[:, :], -LOWEST, LOWEST, ALU.mult, ALU.add))
                own.link(nc.vector.tensor_tensor(g.goes_on[:, :], dst[:, 0:1], dst[:, KE:KE + 1], ALU.is_equal))



def place_list(g, sp, i, b, plist, plisted, used):
    if b % B == 0:
        h = b // B
        sp.wait_ge(used, i * 2 + (h + 1))
        sp.dma_start(plist[h][:, :, :], g.place_idx[bass.ds(i * 2 + h + g.placed_lists, 1)].rearrange(
            "c p n k -> (c p) n k")).then_inc(plisted[h], 16)


def place_edges(g, pool, i, b, plist, plisted, placed, used, gate):
    h, part = divmod(b, B)
    if part == 0:
        gated(pool, plisted[h], i * 16 + 16, gate)
    for k in range(part * (KC // B), (part + 1) * (KC // B)):
        pool.indirect_dma_start(
            out=g.place, out_offset=bass.IndirectOffsetOnAxis(ap=plist[h][:, 0, k:k + 1], axis=0),
            in_=plist[h][:, 1, k:k + 1], in_offset=None, bounds_check=NPAD - 1, oob_is_err=False
        ).then_inc(placed[h], 16)
    if part == B - 1:
        gated(pool, placed[h], i * (16 * KC) + 16 * KC, used)


def phase_product(g):
    nc = g.nc
    with ExitStack() as ctx:
        def sb(name, shape, dt=F32):
            return ctx.enter_context(nc.sbuf_tensor(name, shape, dt))

        x = [sb(f"p_x{b}", [P, Q, D]) for b in range(B)]
        xt = [sb(f"p_xt{b}", [P, CHUNK]) for b in range(B)]
        mx = [sb(f"p_mx{b}", [P, Q, ROW]) for b in range(B)]
        x2 = [sb(f"p_x2{b}", [P, Q, D]) for b in range(B)]
        m2 = [sb(f"p_m2{b}", [P, Q, D]) for b in range(B)]
        pt = [ctx.enter_context(nc.psum_tensor(f"p_pt{b}", [P, 512], F32)) for b in range(R)]
        pm = [ctx.enter_context(nc.psum_tensor(f"p_pm{b}", [P, 2, 512], F32)) for b in range(R)]
        loaded = [g.sem(f"p_loaded{b}") for b in range(B)]
        turned = g.sem("p_turned")
        copied = g.sem("p_copied")
        product = g.sem("p_product")
        squared = g.sem("p_squared")
        moved = g.sem("p_moved")
        summed = g.sem("p_summed")
        stored = [g.sem(f"p_stored{b}") for b in range(B)]
        freed = g.sem("p_freed")
        gate = g.sem("p_gate")
        plist = [sb(f"p_plist{h}", [P, 2, KC], I32) for h in range(2)]
        plisted = [g.sem(f"p_plisted{h}") for h in range(2)]
        placed = [g.indirect_sem(f"p_placed{h}") for h in range(2)]
        used = g.sem("p_used")
        pgate = g.sem("p_pgate")
        passes = NCHUNK // G
        g.placed_lists = 0 * (ECHUNK // 2)
        with nc.Block() as block:
            @block.sync
            def _(sp):
                with sp.Fori(0, passes) as i:
                    for b in range(G):
                        sp.wait_ge(summed, nth_node(i, b))
                        sp.dma_start(x[b % B][:, :, :], rows(g.ins["x"], i * G + b)).then_inc(loaded[b % B], 16)
                        place_list(g, sp, i, b, plist, plisted, used)

            @block.gpsimd
            def _(pool):
                pool.sem_inc(used, 2)
                with pool.Fori(0, passes) as i:
                    for t in range(G + 5):
                        for b in step(t, 5):
                            gated(pool, stored[b % B], turn(i, b) * 16, freed)
                        for b in step(t, 0):
                            place_edges(g, pool, i, b, plist, plisted, placed, used, pgate)

            @block.tensor
            def _(pe):
                with pe.Fori(0, passes) as i:
                    for t in range(G + 1):
                        for b in step(t, 1):
                            pe.wait_ge(copied, nth_node(i, b) + R)
                            pe.wait_ge(moved, nth_node(i, b))
                            for q in range(Q):
                                o = (q % 2) * (ROW + 1)
                                last = nc.tensor.matmul(pm[b % R][:, q // 2, o:o + ROW + 1], xt[b % B][:, q * P:(q + 1) * P],
                                                        g.w0aug[:, :], start=True, stop=True)
                            last.then_inc(product, 1)
                        for b in step(t, 0):
                            pe.wait_ge(loaded[b % B], turn(i, b) * 16)
                            pe.wait_ge(copied, nth_node(i, b))
                            for q in range(Q):
                                last = nc.tensor.transpose(pt[b % R][:, q * P:(q + 1) * P], x[b % B][:, q, :], g.ident[:, :])
                            last.then_inc(turned, 1)

            @block.scalar
            def _(act):
                act.sem_inc(copied, R)
                with act.Fori(0, passes) as i:
                    for t in range(G + 2):
                        for b in step(t, 2):
                            act.wait_ge(summed, nth_node(i, b))
                            act.wait_ge(loaded[b % B], turn(i, b) * 16)
                            nc.scalar.activation(x2[b % B][:, :, :], x[b % B][:, :, :], ACT.Square)
                            act.wait_ge(moved, nth_node(i, b) + R)
                            nc.scalar.activation(m2[b % B][:, :, :], mx[b % B][:, :, 0:D], ACT.Square).then_inc(squared, 1)
                            act.dma_start(rows(g.mx, i * G + b), mx[b % B][:, :, :]).then_inc(stored[b % B], 16)
                        for b in step(t, 0):
                            act.wait_ge(turned, nth_node(i, b))
                            act.wait_ge(freed, nth_node(i, b))
                            nc.scalar.copy(xt[b % B][:, :], pt[b % R][:, :]).then_inc(copied, 1)

            @block.vector
            def _(v):
                v.sem_inc(summed, B)
                v.sem_inc(moved, R)
                v.sem_inc(freed, B)
                with v.Fori(0, passes) as i:
                    for t in range(G + 2):
                        for b in step(t, 2):
                            col = bass.ds(i * (G * Q) + b * Q, Q)
                            v.wait_ge(squared, nth_node(i, b))
                            v.sem_inc(gate, 1)
                            nc.vector.tensor_reduce(g.sxx[:, col], x2[b % B][:, :, :], AX_X, ALU.add)
                            nc.vector.tensor_reduce(g.smm[:, col], m2[b % B][:, :, :], AX_X, ALU.add).then_inc(summed, 1)
                        for b in step(t, 1):
                            col = bass.ds(i * (G * Q) + b * Q, Q)
                            v.wait_ge(product, nth_node(i, b))
                            v.wait_ge(freed, nth_node(i, b))
                            view = pm[b % R][:, :, 0:2 * (ROW + 1)].rearrange("p a (s c) -> p a s c", s=2)
                            v.tensor_scalar(g.sxy[:, col].rearrange("p (a s) -> p a s", s=2), view[:, :, :, ROW],
                                            1.0, None, ALU.mult)
                            nc.vector.tensor_copy(mx[b % B][:, :, :].rearrange("p (a s) c -> p a s c", s=2),
                                                  view[:, :, :, 0:ROW]).then_inc(moved, 1)



def phase_map(g):
    nc = g.nc
    with ExitStack() as ctx:
        t = [ctx.enter_context(nc.sbuf_tensor(f"m_t{n}", [P, COLS], F32)) for n in range(14)]
        asked = g.sem("m_asked")
        rooted = g.sem("m_rooted")
        logged = g.sem("m_logged")
        tanhed = g.sem("m_tanhed")
        ch = g.sem("m_chain")
        tanh_asked = g.sem("m_tanh_asked")
        log_asked = g.sem("m_log_asked")
        xn, mn, n2, ratio, lg = t[0], t[1], t[2], t[3], t[4]
        xsq = t[11]
        with nc.Block() as block:
            @block.scalar
            def _(act):
                act.wait_ge(asked, 2)
                nc.scalar.activation(xn[:, :], t[6][:, :], ACT.Sqrt)
                nc.scalar.activation(mn[:, :], t[7][:, :], ACT.Sqrt).then_inc(rooted, 1)
                act.wait_ge(log_asked, 1)
                nc.scalar.activation(lg[:, :], ratio[:, :], ACT.Ln).then_inc(logged, 1)
                act.wait_ge(tanh_asked, 1)
                nc.scalar.activation(t[5][:, :], t[5][:, :], ACT.Tanh).then_inc(tanhed, 1)
                act.wait_ge(asked, 3)
                nc.scalar.activation(n2[:, :], xsq[:, :], ACT.Sqrt).then_inc(rooted, 1)
                act.wait_ge(log_asked, 2)
                nc.scalar.activation(lg[:, :], ratio[:, :], ACT.Ln).then_inc(logged, 1)

            @block.vector
            def _(v):
                own = Own(v, ch)

                def tt(o, a, b, op):
                    own.link(nc.vector.tensor_tensor(o[:, :], a[:, :], b[:, :], op))

                def ts(o, a, s1, op1, s2=None, op2=ALU.bypass):
                    own.link(nc.vector.tensor_scalar(o[:, :], a[:, :], s1, s2, op1, op2))

                def stt(o, a, s, b, op1, op2):
                    own.link(nc.vector.scalar_tensor_tensor(o[:, :], a[:, :], s, b[:, :], op1, op2))

                def ask(o, a, s1, op1, sem):
                    nc.vector.tensor_scalar(o[:, :], a[:, :], s1, None, op1).then_inc(sem, 1)

                def artanh(o, n, call, a, b, c):
                    ts(a, n, 1.0 - 1e-7, ALU.min)
                    ts(b, a, -1.0, ALU.mult, 1.0, ALU.add)
                    own.link(nc.vector.reciprocal(b[:, :], b[:, :]))
                    stt(ratio, a, 1.0, b, ALU.add, ALU.mult)
                    v.sem_inc(log_asked, 1)
                    tt(b, a, a, ALU.mult)
                    ts(c, b, 1.0 / 15, ALU.mult, 1.0 / 13, ALU.add)
                    for n_ in (11, 9, 7, 5, 3, 1):
                        tt(c, c, b, ALU.mult)
                        ts(c, c, 1.0 / n_, ALU.add)
                    tt(c, c, a, ALU.mult)
                    ts(b, a, 0.3, ALU.is_lt)
                    tt(c, c, b, ALU.mult)
                    ts(b, b, -0.5, ALU.mult, 0.5, ALU.add)
                    v.wait_ge(logged, call)
                    tt(b, b, lg, ALU.mult)
                    tt(o, b, c, ALU.add)

                def newton(r, square, w):
                    own.link(nc.vector.reciprocal(w[:, :], r[:, :]))
                    tt(w, w, square, ALU.mult)
                    tt(w, w, r, ALU.add)
                    ts(r, w, 0.5, ALU.mult)

                ask(t[6], g.sxx, MIN_NORM ** 2, ALU.max, asked)
                ask(t[7], g.smm, MIN_NORM ** 2, ALU.max, asked)
                v.wait_ge(rooted, 1)
                newton(xn, t[6], t[10])
                newton(mn, t[7], t[10])
                arg, rx, rm, c, cm = t[5], t[6], t[7], t[8], t[9]
                artanh(arg, xn, 1, t[10], t[11], t[12])
                own.link(nc.vector.reciprocal(rx[:, :], xn[:, :]))
                own.link(nc.vector.reciprocal(rm[:, :], mn[:, :]))
                tt(rx, rx, mn, ALU.mult)
                tt(arg, arg, rx, ALU.mult)
                v.sem_inc(tanh_asked, 1)
                v.wait_ge(tanhed, 1)
                ts(c, arg, MAX_NORM, ALU.min)
                tt(cm, c, rm, ALU.mult)
                x2, xy2, a, b, den, xy = t[10], t[11], t[12], t[13], t[6], t[7]
                tt(x2, c, c, ALU.mult)
                tt(xy, cm, g.sxy, ALU.mult)
                ts(a, xy, 2.0, ALU.mult, 1.0, ALU.add)
                stt(den, x2, g.y2[:, 0:1], a, ALU.mult, ALU.add)
                ts(den, den, MIN_NORM, ALU.max)
                ts(a, a, g.y2[:, 0:1], ALU.add)
                ts(b, x2, -1.0, ALU.mult, 1.0, ALU.add)
                own.link(nc.vector.reciprocal(den[:, :], den[:, :]))
                tt(a, a, den, ALU.mult)
                tt(b, b, den, ALU.mult)
                tt(xy2, a, xy, ALU.mult)
                ts(xy2, xy2, 2.0, ALU.mult)
                stt(xy2, b, g.y2[:, 0:1], xy2, ALU.mult, ALU.add)
                tt(xy2, xy2, b, ALU.mult)
                tt(x2, x2, a, ALU.mult)
                tt(x2, x2, a, ALU.mult)
                tt(n2, x2, xy2, ALU.add)
                ask(xsq, n2, MIN_NORM ** 2, ALU.max, asked)
                v.wait_ge(rooted, 2)
                newton(n2, xsq, x2)
                tt(cm, cm, a, ALU.mult)
                ts(c, n2, MAX_NORM, ALU.min)
                artanh(rx, c, 2, t[10], t[11], t[12])
                own.link(nc.vector.reciprocal(n2[:, :], n2[:, :]))
                tt(rx, rx, n2, ALU.mult)
                own.mark(nc.vector.tensor_tensor(g.alpha[:, :], rx[:, :], cm[:, :], ALU.mult))
                own.mark(nc.vector.tensor_tensor(g.beta[:, :], rx[:, :], b[:, :], ALU.mult))
                own.wait()


def phase_log(g):
    nc = g.nc
    with ExitStack() as ctx:
        def sb(name, shape, dt=F32):
            return ctx.enter_context(nc.sbuf_tensor(name, shape, dt))

        mx = [sb(f"l_mx{b}", [P, Q, ROW]) for b in range(B)]
        by = [sb(f"l_by{b}", [P, Q, ROW]) for b in range(B)]
        ab = [sb(f"l_ab{b}", [P, 2, Q]) for b in range(B)]
        r = [sb(f"l_r{b}", [P, Q, ROW]) for b in range(B)]
        loaded = [g.sem(f"l_loaded{b}") for b in range(B)]
        factors = g.sem("l_factors")
        scaled = g.sem("l_scaled")
        summed = g.sem("l_summed")
        stored = [g.sem(f"l_stored{b}") for b in range(B)]
        freed = g.sem("l_freed")
        gate = g.sem("l_gate")
        plist = [sb(f"l_plist{h}", [P, 2, KC], I32) for h in range(2)]
        plisted = [g.sem(f"l_plisted{h}") for h in range(2)]
        placed = [g.indirect_sem(f"l_placed{h}") for h in range(2)]
        used = g.sem("l_used")
        pgate = g.sem("l_pgate")
        passes = NCHUNK // G
        g.placed_lists = 1 * (ECHUNK // 2)
        with nc.Block() as block:
            @block.sync
            def _(sp):
                with sp.Fori(0, passes) as i:
                    for b in range(G):
                        sp.wait_ge(summed, nth_node(i, b))
                        sp.dma_start(mx[b % B][:, :, :], rows(g.mx, i * G + b)).then_inc(loaded[b % B], 16)
                        place_list(g, sp, i, b, plist, plisted, used)

            @block.gpsimd
            def _(pool):
                pool.sem_inc(used, 2)
                with pool.Fori(0, passes) as i:
                    for t in range(G + 4):
                        for b in step(t, 4):
                            gated(pool, stored[b % B], turn(i, b) * 32, freed)
                        for b in step(t, 0):
                            place_edges(g, pool, i, b, plist, plisted, placed, used, pgate)

            @block.scalar
            def _(act):
                with act.Fori(0, passes) as i:
                    for t in range(G + 1):
                        for b in step(t, 1):
                            act.wait_ge(summed, nth_node(i, b) + B)
                            act.dma_start(rows(g.t[0], i * G + b), r[b % B][:, :, 0:TROW]).then_inc(stored[b % B], 16)
                            act.dma_start(rows(g.ai[0], i * G + b), r[b % B][:, :, TROW:ROW]).then_inc(stored[b % B], 16)
                        for b in step(t, 0):
                            act.wait_ge(factors, nth_node(i, b))
                            for q in range(Q):
                                last = nc.scalar.activation(by[b % B][:, q, :], g.yrow[:, :], ACT.Copy,
                                                            scale=ab[b % B][:, 1, q:q + 1])
                            last.then_inc(scaled, 1)

            @block.vector
            def _(v):
                v.sem_inc(summed, B)
                v.sem_inc(freed, B)
                with v.Fori(0, passes) as i:
                    for t in range(G + 1):
                        for b in step(t, 1):
                            v.wait_ge(freed, nth_node(i, b))
                            v.wait_ge(loaded[b % B], turn(i, b) * 16)
                            v.wait_ge(scaled, nth_node(i, b))
                            for q in range(Q):
                                last = nc.vector.scalar_tensor_tensor(r[b % B][:, q, :], mx[b % B][:, q, :], ab[b % B][:, 0, q:q + 1],
                                                                      by[b % B][:, q, :], ALU.mult, ALU.add)
                            last.then_inc(summed, 1)
                        for b in step(t, 0):
                            col = bass.ds(i * (G * Q) + b * Q, Q)
                            gated(v, summed, nth_node(i, b), gate)
                            nc.vector.tensor_copy(ab[b % B][:, 0, :], g.alpha[:, col])
                            nc.vector.tensor_copy(ab[b % B][:, 1, :], g.beta[:, col]).then_inc(factors, 1)


def phase_places(g):
    nc = g.nc
    with ExitStack() as ctx:
        row = ctx.enter_context(nc.sbuf_tensor("n_row", [P, 1], F32))
        fix = ctx.enter_context(nc.sbuf_tensor("n_fix", [P, 1], F32))
        loaded = g.sem("n_loaded")
        got = g.indirect_sem("n_got")
        ch = g.sem("n_chain")
        with nc.Block() as block:
            @block.sync
            def _(sp):
                sp.dma_start(g.places[:, 0:NCHUNK * Q].rearrange("p (c q) -> p c q", q=Q),
                             g.place.rearrange("(c p q) o -> p c (q o)", p=P, q=Q)).then_inc(loaded, 16)
                sp.wait_ge(loaded, 16)

            @block.gpsimd
            def _(pool):
                pool.indirect_dma_start(out=g.first_row[:, :], out_offset=None, in_=g.place,
                                        in_offset=bass.IndirectOffsetOnAxis(ap=g.first_i[:, 0:1], axis=0)
                                        ).then_inc(got, 16)

            @block.vector
            def _(v):
                own = Own(v, ch)
                own.mark(nc.vector.memset(g.places[:, NCHUNK * Q:(NCHUNK + B) * Q], EMPTY))
                v.wait_ge(got, 16)
                own.link(nc.vector.tensor_copy(row[:, :], g.first_row[:, :]))
                own.link(nc.vector.scalar_tensor_tensor(fix[:, :], g.goes_on[:, :], float(SKIP), row[:, :],
                                                        ALU.mult, ALU.add))
                own.link(nc.vector.tensor_copy(g.fix_row[:, :], fix[:, :]))


class StateGathers:

    def __init__(self, g, pool, idx, ag, gathered, copied_idx, table):
        self.g, self.pool, self.idx, self.ag, self.gathered, self.table = g, pool, idx, ag, gathered, table
        self.copied_idx = copied_idx
        self.gate = g.sem("gathers_gate")

    def rows(self, i, b, used=None, value=None):
        if used is not None:
            gated(self.pool, used, value, self.copied_idx)
            n = i * (2 * G) + (2 * (b - B) + 2 + B)
        else:
            n = b + 1
        self.pool.tensor_copy(self.idx[b % B][:, :], self.g.places[:, bass.ds(i * (G * Q) + b * Q, Q)]
                              ).then_inc(self.copied_idx, 1)
        if used is None:
            self.pool.wait_ge(self.copied_idx, n)
        else:
            gated(self.pool, self.copied_idx, n, self.gate)

    def gather(self, i, b, q0, q1):
        for q in range(q0, q1):
            self.pool.indirect_dma_start(
                out=self.ag[b % B][:, q, :], out_offset=None, in_=self.table,
                in_offset=bass.IndirectOffsetOnAxis(ap=self.idx[b % B][:, q:q + 1], axis=0)
            ).then_inc(self.gathered[b % B], 16)



def nth(i, b):
    return i * NB + (b + 1)


def edge_streams(g, sp, idx, fac, r, listed, gathered, per_gather, stated, stored, table, more=None):
    passes = ECHUNK // NB
    out = table[0:NPAD].rearrange("(c p k) d -> c p k d", p=P, k=KC)

    def lists(i, b):
        c = bass.ds(i * NB + b, 1)
        sp.dma_start(idx[b][:, :, :], g.edge_idx[c].rearrange("c p n k -> (c p) n k")).then_inc(listed[b], 16)
        sp.dma_start(fac[b][:, :, :], g.edge_fac[c].rearrange("c p n k -> (c p) n k")).then_inc(listed[b], 16)
        if more is not None:
            more(i, b)

    def states(i, b):
        sp.wait_ge(stated, nth(i, b))
        c = bass.ds(i * NB + b, 1)
        sp.dma_start(out[c].rearrange("c p k d -> (c p) k d"), r[b][:, :, :]).then_inc(stored[b], 16)

    for b in range(NB):
        lists(0, b)
    with sp.Fori(0, passes - 1) as i:
        for b in range(NB):
            states(i, b)
            sp.wait_ge(gathered[b], i * (per_gather * KC) + per_gather * KC)
            lists(i + 1, b)
    for b in range(NB):
        states(passes - 1, b)
    for b in range(NB):
        sp.wait_ge(stored[b], 16 * passes)


def edge_gathers(g, pool, gathers, listed, per_list, stated, stored, gate):
    for b in range(NB):
        pool.wait_ge(listed[b], per_list)
        if b == NB - 1:
            pool.wait_ge(stated, 1)
        gathers(b)
    with pool.Fori(1, ECHUNK // NB) as i:
        for b in range(NB):
            gated(pool, listed[b], i * per_list + per_list, gate)
            gated(pool, stored[b], i * 16, gate)
            gated(pool, stated, i * NB + (b + 2 - NB), gate)
            gathers(b)


def phase_attend(g, layer, heads):
    nc = g.nc
    dh = D // heads
    pre = f"a{layer}_"
    with ExitStack() as ctx:
        def sb(name, shape, dt=F32):
            return ctx.enter_context(nc.sbuf_tensor(pre + name, shape, dt))

        idx = [sb(f"idx{b}", [P, 2, KC], I32) for b in range(NB)]
        fac = [sb(f"fac{b}", [P, 2, KC]) for b in range(NB)]
        r = [sb(f"r{b}", [P, KC, ROW]) for b in range(NB)]
        ai = [sb(f"ai{b}", [P, KC, HEADS]) for b in range(NB)]
        s = sb("s", [P, heads, KC])
        mx = sb("mx", [P, heads, KC + 1])
        dn = sb("dn", [P, heads, KC + 1])
        e = sb("e", [P, 2, heads, KC])
        tmp = sb("tmp", [P, D])
        listed = [g.sem(pre + f"listed{b}") for b in range(NB)]
        gathered = [g.indirect_sem(pre + f"gathered{b}") for b in range(NB)]
        stored = [g.sem(pre + f"stored{b}") for b in range(NB)]
        asked = g.sem(pre + "asked")
        raised = g.sem(pre + "raised")
        stated = g.sem(pre + "stated")
        cleared = g.sem(pre + "cleared")
        ch = g.sem(pre + "chain")
        gate = g.sem(pre + "gate")
        passes = ECHUNK // NB
        with nc.Block() as block:
            @block.sync
            def _(sp):
                edge_streams(g, sp, idx, fac, r, listed, gathered, 32, stated, stored, g.states)

            @block.gpsimd
            def _(pool):
                pool.wait_ge(cleared, 1)

                def gathers(b):
                    for k in range(KC):
                        pool.indirect_dma_start(
                            out=r[b][:, k, 0:TROW], out_offset=None, in_=g.t[layer],
                            in_offset=bass.IndirectOffsetOnAxis(ap=idx[b][:, 0, k:k + 1], axis=0)
                        ).then_inc(gathered[b], 16)
                        pool.indirect_dma_start(
                            out=ai[b][:, k, :], out_offset=None, in_=g.ai[layer],
                            in_offset=bass.IndirectOffsetOnAxis(ap=idx[b][:, 1, k:k + 1], axis=0)
                        ).then_inc(gathered[b], 16)

                edge_gathers(g, pool, gathers, listed, 32, stated, stored, gate)

            @block.scalar
            def _(act):
                with act.Fori(0, passes) as i:
                    for b in range(NB):
                        act.wait_ge(asked, nth(i, b))
                        nc.scalar.activation(e[:, :, :, :], e[:, :, :, :], ACT.Exp).then_inc(raised, 1)

            @block.vector
            def _(v):
                for b in range(NB):
                    nc.vector.memset(r[b][:, :, :], 0.0)
                nc.vector.memset(dn[:, :, :], 0.0)
                nc.vector.memset(mx[:, :, :], LOWEST).then_inc(cleared, 1)
                v.wait_ge(cleared, 1)
                per = NB * (7 + 2 * heads + (2 if heads > 1 else 1) * KC)
                with v.Fori(0, passes) as i:
                    own = Own(v, ch, i, per)
                    for b in range(NB):
                        v.wait_ge(gathered[b], i * (32 * KC) + 32 * KC)
                        own.link(nc.vector.tensor_tensor(
                            s[:, :, :], r[b][:, :, D:D + heads].rearrange("p k h -> p h k"),
                            ai[b][:, :, 0:heads].rearrange("p k h -> p h k"), ALU.add))
                        own.link(nc.vector.scalar_tensor_tensor(s[:, :, :], s[:, :, :], SLOPE, s[:, :, :],
                                                                ALU.mult, ALU.max))
                        for h in range(heads):
                            own.mark(nc.vector.tensor_tensor_scan(mx[:, h, 1:KC + 1], fac[b][:, 1, :], s[:, h, :],
                                                                  mx[:, h, 0:1], ALU.add, ALU.max))
                        own.wait()
                        own.mark(nc.vector.tensor_tensor(e[:, 1, :, :], s[:, :, :], mx[:, :, 1:KC + 1], ALU.subtract))
                        own.link(nc.vector.tensor_tensor(e[:, 0, :, :], mx[:, :, 0:KC], mx[:, :, 1:KC + 1],
                                                         ALU.subtract))
                        low = fac[b][:, 1:2, :].to_broadcast([P, heads, KC])
                        nc.vector.tensor_tensor(e[:, 0, :, :], e[:, 0, :, :], low, ALU.add).then_inc(asked, 1)
                        v.wait_ge(raised, nth(i, b))
                        for h in range(heads):
                            own.mark(nc.vector.tensor_tensor_scan(dn[:, h, 1:KC + 1], e[:, 0, h, :], e[:, 1, h, :],
                                                                  dn[:, h, 0:1], ALU.mult, ALU.add))
                        w = e[:, 1, :, :].rearrange("p h k -> p k h").unsqueeze(3).to_broadcast([P, KC, heads, dh])
                        rv = r[b][:, :, 0:D].rearrange("p k (h d) -> p k h d", h=heads)
                        own.link(nc.vector.tensor_tensor(rv, rv, w, ALU.mult))
                        for k in range(KC):
                            prev = r[b][:, k - 1, 0:D] if k else r[(b - 1) % NB][:, KC - 1, 0:D]
                            if heads == 1:
                                own.link(nc.vector.scalar_tensor_tensor(
                                    r[b][:, k, 0:D], prev, e[:, 0, 0, k:k + 1], r[b][:, k, 0:D], ALU.mult, ALU.add))
                            else:
                                f = e[:, 0, :, k:k + 1].to_broadcast([P, heads, dh])
                                own.link(nc.vector.tensor_tensor(
                                    tmp[:, :].rearrange("p (h d) -> p h d", h=heads),
                                    prev.rearrange("p (h d) -> p h d", h=heads), f, ALU.mult))
                                own.link(nc.vector.tensor_tensor(r[b][:, k, 0:D], r[b][:, k, 0:D], tmp[:, :],
                                                                 ALU.add))
                        own.mark(nc.vector.tensor_copy(r[b][:, :, DEN:DEN + heads],
                                                       dn[:, :, 1:KC + 1].rearrange("p h k -> p k h")))
                        own.link(nc.vector.tensor_copy(r[b][:, :, MAXC:MAXC + heads],
                                                       mx[:, :, 1:KC + 1].rearrange("p h k -> p k h")))
                        nc.vector.tensor_copy(dn[:, :, 0:1], dn[:, :, KC:KC + 1])
                        nc.vector.tensor_copy(mx[:, :, 0:1], mx[:, :, KC:KC + 1]).then_inc(stated, 1)
                        v.wait_ge(stated, nth(i, b))
                    own.end()
                nc.vector.tensor_copy(g.last[:, :], r[NB - 1][:, KC - 1, :]).then_inc(cleared, 1)
                v.wait_ge(cleared, 2)


def phase_join(g, tag, heads, table, width=ROW):
    nc = g.nc
    pre = f"j{tag}_"
    nh = max(heads, 1)
    sums = min(width, TROW)
    dh = D // nh
    with ExitStack() as ctx:
        def sb(name, shape, dt=F32):
            return ctx.enter_context(nc.sbuf_tensor(pre + name, shape, dt))

        row = sb("row", [P, width])
        new = sb("new", [P, width])
        dgm = sb("dgm", [P, nh, P])
        w = sb("w", [P, nh, P])
        wt = sb("wt", [P, nh, P])
        mc = sb("mc", [P, nh])
        mn = sb("mn", [P, nh])
        e = sb("e", [P, 2, nh])
        t = sb("t", [P, D])
        pa = ctx.enter_context(nc.psum_tensor(pre + "pa", [P, 512], F32))
        pb = ctx.enter_context(nc.psum_tensor(pre + "pb", [P, 512], F32))
        pc = ctx.enter_context(nc.psum_tensor(pre + "pc", [P, 512], F32))
        got = g.indirect_sem(pre + "got")
        put = g.indirect_sem(pre + "put")
        ready = g.sem(pre + "ready")
        spread = g.sem(pre + "spread")
        raised = g.sem(pre + "raised")
        ch = g.sem(pre + "chain")
        with nc.Block() as block:
            @block.gpsimd
            def _(pool):
                pool.indirect_dma_start(out=row[:, :], out_offset=None, in_=table,
                                        in_offset=bass.IndirectOffsetOnAxis(ap=g.first_row[:, 0:1], axis=0)
                                        ).then_inc(got, 16)
                pool.wait_ge(ready, 4 if heads else 1)
                pool.indirect_dma_start(out=table, out_offset=bass.IndirectOffsetOnAxis(ap=g.fix_row[:, 0:1], axis=0),
                                        in_=new[:, :], in_offset=None, bounds_check=NPAD - 1, oob_is_err=False
                                        ).then_inc(put, 16)
                pool.wait_ge(put, 16)

            if not heads:
                @block.tensor
                def _(pe):
                    nc.tensor.matmul(pc[:, 0:sums], g.cross[:, :], g.last[:, 0:sums], start=True,
                                     stop=True).then_inc(spread, 1)

                @block.vector
                def _(v):
                    own = Own(v, ch)
                    v.wait_ge(got, 16)
                    if width > sums:
                        own.mark(nc.vector.tensor_copy(new[:, sums:width], row[:, sums:width]))
                    v.wait_ge(spread, 1)
                    nc.vector.tensor_tensor(new[:, 0:sums], row[:, 0:sums], pc[:, 0:sums], ALU.add).then_inc(ready, 1)
                return

            @block.tensor
            def _(pe):
                pe.wait_ge(ready, 1)
                nc.tensor.matmul(pa[:, 0:nh * P], g.ones[:, :], dgm[:, :, :].rearrange("p h f -> p (h f)"),
                                 start=True, stop=True).then_inc(spread, 1)
                pe.wait_ge(ready, 3)
                for h in range(nh):
                    last = nc.tensor.transpose(pb[:, h * P:(h + 1) * P], w[:, h, :], g.ident[:, :])
                last.then_inc(spread, 1)
                pe.wait_ge(raised, 3)
                for h in range(nh):
                    nc.tensor.matmul(pc[:, h * dh:(h + 1) * dh], wt[:, h, :], g.last[:, h * dh:(h + 1) * dh],
                                     start=True, stop=True)
                    last = nc.tensor.matmul(pc[:, DEN + h:DEN + h + 1], wt[:, h, :], g.last[:, DEN + h:DEN + h + 1],
                                            start=True, stop=True)
                last.then_inc(spread, 1)

            @block.scalar
            def _(act):
                act.wait_ge(ready, 2)
                nc.scalar.activation(w[:, :, :], w[:, :, :], ACT.Exp).then_inc(raised, 1)
                act.wait_ge(raised, 2)
                nc.scalar.activation(e[:, :, :], e[:, :, :], ACT.Exp)
                act.wait_ge(spread, 2)
                nc.scalar.copy(wt[:, :, :].rearrange("p h f -> p (h f)"), pb[:, 0:nh * P]).then_inc(raised, 1)

            @block.vector
            def _(v):
                own = Own(v, ch)
                for h in range(nh):
                    last = nc.vector.tensor_scalar(dgm[:, h, :], g.ident[:, :], g.last[:, MAXC + h:MAXC + h + 1],
                                                   None, ALU.mult)
                last.then_inc(ready, 1)
                v.wait_ge(spread, 1)
                low = g.low_t[:, :].unsqueeze(1).to_broadcast([P, nh, P])
                own.link(nc.vector.tensor_tensor(w[:, :, :], pa[:, 0:nh * P].rearrange("p (h f) -> p h f", h=nh), low,
                                                 ALU.add))
                own.link(nc.vector.tensor_reduce(mc[:, :], w[:, :, :], AX_X, ALU.max))
                nc.vector.tensor_tensor(w[:, :, :], w[:, :, :], mc[:, :].unsqueeze(2).to_broadcast([P, nh, P]),
                                        ALU.subtract).then_inc(ready, 1)
                v.wait_ge(raised, 1)
                cross = g.cross_t[:, :].unsqueeze(1).to_broadcast([P, nh, P])
                nc.vector.tensor_tensor(w[:, :, :], w[:, :, :], cross, ALU.mult).then_inc(ready, 1)
                v.wait_ge(got, 16)
                own.link(nc.vector.tensor_copy(new[:, :], row[:, :]))
                mr = row[:, MAXC:MAXC + nh]
                own.link(nc.vector.tensor_tensor(mn[:, :], mr, mc[:, :], ALU.max))
                own.mark(nc.vector.tensor_tensor(e[:, 0, :], mr, mn[:, :], ALU.subtract))
                own.mark(nc.vector.tensor_copy(new[:, MAXC:MAXC + nh], mn[:, :]))
                nc.vector.tensor_tensor(e[:, 1, :], mc[:, :], mn[:, :], ALU.subtract).then_inc(raised, 1)
                v.wait_ge(raised, 3)
                v.wait_ge(spread, 3)

                def bc(a):
                    return a.unsqueeze(2).to_broadcast([P, nh, dh])

                def hv(a):
                    return a.rearrange("p (h d) -> p h d", h=nh)

                own.mark(nc.vector.tensor_tensor(hv(new[:, 0:D]), hv(row[:, 0:D]), bc(e[:, 0, :]), ALU.mult))
                own.mark(nc.vector.tensor_tensor(new[:, DEN:DEN + nh], row[:, DEN:DEN + nh], e[:, 0, :], ALU.mult))
                own.mark(nc.vector.tensor_tensor(hv(t[:, :]), hv(pc[:, 0:D]), bc(e[:, 1, :]), ALU.mult))
                own.link(nc.vector.tensor_tensor(mn[:, :], pc[:, DEN:DEN + nh], e[:, 1, :], ALU.mult))
                own.mark(nc.vector.tensor_tensor(new[:, 0:D], new[:, 0:D], t[:, :], ALU.add))
                nc.vector.tensor_tensor(new[:, DEN:DEN + nh], new[:, DEN:DEN + nh], mn[:, :],
                                        ALU.add).then_inc(ready, 1)



def norm_stats(nc, own, gate, src, st, mv, ve):
    for q in range(Q):
        own.mark(nc.vector.bn_stats(st[:, q, :], src[:, q, :]))
    own.wait()
    own.eng.sem_inc(gate, 1)
    for q in range(Q):
        own.mark(nc.vector.bn_aggr(mv[:, q, :], st[:, q, :]))
    own.wait()
    return nc.vector.tensor_scalar(ve[:, :], mv[:, :, 1], EPS, None, ALU.add)


def norm_apply(nc, dst, src, mv, rs):
    for q in range(Q):
        last = nc.vector.tensor_scalar(dst[:, q, :], src[:, q, :], mv[:, q, 0:1], rs[:, q:q + 1],
                                       ALU.subtract, ALU.mult)
    return last


def phase_settle(g, layer, heads):
    nc = g.nc
    dh = D // heads
    pre = f"s{layer}_"
    first = layer == 0
    bias = g.bias0 if first else g.bias1
    with ExitStack() as ctx:
        def sb(name, shape, dt=F32):
            return [ctx.enter_context(nc.sbuf_tensor(f"{pre}{name}{b}", shape, dt)) for b in range(B)]

        x = sb("x", [P, Q, D])
        ag = sb("ag", [P, Q, ROW])
        idx = sb("idx", [P, Q], I32)
        se = sb("se", [P, Q, TROW])
        ai = sb("ai", [P, Q, HEADS])
        s = sb("s", [P, Q, heads])
        m = sb("m", [P, Q, heads])
        e = sb("e", [P, 2, Q, heads])
        den = sb("den", [P, Q, heads])
        o = sb("o", [P, Q, D])
        sq = sb("sq", [P, Q, D])
        nr = sb("nr", [P, 4, Q])
        st = sb("st", [P, Q, 6])
        mv = sb("mv", [P, Q, 2])
        ve = sb("ve", [P, Q])
        rs = sb("rs", [P, Q])
        xn = sb("xn", [P, Q, D])
        xt = sb("xt", [P, CHUNK])
        tr = sb("tr", [P, Q, TROW])
        ao = sb("ao", [P, Q, HEADS])
        hr = sb("hr", [P, Q, D])
        pt = [ctx.enter_context(nc.psum_tensor(f"{pre}pt{b}", [P, 512], F32)) for b in range(R)]
        pm = [ctx.enter_context(nc.psum_tensor(f"{pre}pm{b}", [P, 2, 512], F32)) for b in range(R)]
        pb = [ctx.enter_context(nc.psum_tensor(f"{pre}pb{b}", [P, 512], F32)) for b in range(R)]
        gathered = [g.indirect_sem(f"{pre}gathered{b}") for b in range(B)]
        copied_idx = g.sem(pre + "copied_idx")
        loaded = [g.sem(f"{pre}loaded{b}") for b in range(B)]
        asked = g.sem(pre + "asked")
        raised = g.sem(pre + "raised")
        biased = g.sem(pre + "biased")
        squared = g.sem(pre + "squared")
        normasked = g.sem(pre + "normasked")
        rooted = g.sem(pre + "rooted")
        tanhed = g.sem(pre + "tanhed")
        varasked = g.sem(pre + "varasked")
        scale = g.sem(pre + "scale")
        normed = g.sem(pre + "normed")
        turned = g.sem(pre + "turned")
        copied = g.sem(pre + "copied")
        product = g.sem(pre + "product")
        hidden = g.sem(pre + "hidden")
        back = g.sem(pre + "back")
        moved = g.sem(pre + "moved")
        stored = [g.sem(f"{pre}stored{b}") for b in range(B)]
        freed = g.sem(pre + "freed")
        ch = g.sem(pre + "chain")
        gate = g.sem(pre + "gate")
        passes = NCHUNK // G
        xsrc = g.ins["x"] if first else g.x[1]
        nstores = 3
        L = 3 if first else 2
        with nc.Block() as block:
            @block.sync
            def _(sp):
                with sp.Fori(0, passes) as i:
                    for b in range(G):
                        c = i * G + b
                        sp.wait_ge(normed, nth_node(i, b))
                        for dst, src in ((x, xsrc), (se, g.t[layer]), (ai, g.ai[layer])):
                            sp.dma_start(dst[b % B][:, :, :], rows(src, c)).then_inc(loaded[b % B], 16)

            @block.gpsimd
            def _(pool):
                seq = StateGathers(g, pool, idx, ag, gathered, copied_idx, g.states)
                for b in range(B):
                    seq.rows(0, b)
                    seq.gather(0, b, 0, Q)
                with pool.Fori(0, passes) as i:
                    for t in range(G + 7):
                        for b in step(t, 7):
                            gated(pool, stored[b % B], turn(i, b) * 16 * nstores, freed)
                        for b in step(t, L):
                            pool.wait_ge(varasked, nth_node(i, b))
                            pool.tensor_tensor(rs[b % B][:, :], ve[b % B][:, :], g.mhalf[:, 0:Q], ALU.pow).then_inc(scale, 1)
                            if not first:
                                seq.rows(i, b + B, biased, nth_node(i, b))
                            seq.gather(i, b + B, Q // 2 if first else 0, Q)
                        if first:
                            for b in step(t, 2):
                                pool.wait_ge(normasked, nth_node(i, b))
                                pool.tensor_tensor(nr[b % B][:, 1, :], nr[b % B][:, 0, :], g.half[:, 0:Q],
                                                   ALU.pow).then_inc(rooted, 1)
                                seq.rows(i, b + B, biased, nth_node(i, b))
                                seq.gather(i, b + B, 0, Q // 2)
                for b in range(B):
                    pool.wait_ge(gathered[b % B], (passes * (G // B) + 1) * 16 * Q)

            @block.scalar
            def _(act):
                act.sem_inc(copied, R)
                with act.Fori(0, passes) as i:
                    for t in range(G + (L + 3)):
                        if first:
                            for b in step(t, L + 3):
                                c = i * G + b
                                act.wait_ge(moved, nth_node(i, b) + R)
                                act.dma_start(rows(g.t[1], c), tr[b % B][:, :, :]).then_inc(stored[b % B], 16)
                                act.dma_start(rows(g.ai[1], c), ao[b % B][:, :, :]).then_inc(stored[b % B], 16)
                        if not first:
                            for b in step(t, L + 3):
                                act.wait_ge(hidden, nth_node(i, b) + R)
                                act.dma_start(g.ht[0][bass.ds(i * G + b, 1)].rearrange("c p n -> (c p) n"),
                                              xt[b % B][:, :]).then_inc(stored[b % B], 16)
                                act.wait_ge(moved, nth_node(i, b) + R)
                                act.dma_start(rows(g.hr[0], i * G + b), hr[b % B][:, :, :]).then_inc(stored[b % B], 16)
                        if not first:
                            for b in step(t, L + 2):
                                act.wait_ge(product, nth_node(i, b))
                                nc.scalar.activation(xt[b % B][:, :], pm[b % R][:, 0, :], ACT.Relu,
                                                     bias=g.projb[:, 0:1]).then_inc(hidden, 1)
                        for b in step(t, L + 1):
                            c = i * G + b
                            act.wait_ge(normed, nth_node(i, b) + B)
                            act.dma_start(rows(g.x[layer + 1], c), xn[b % B][:, :, :]).then_inc(stored[b % B], 16)
                            act.wait_ge(turned, nth_node(i, b))
                            nc.scalar.copy(xt[b % B][:, :], pt[b % R][:, :]).then_inc(copied, 1)
                        if first:
                            for b in step(t, 2):
                                act.wait_ge(rooted, nth_node(i, b))
                                nc.scalar.activation(nr[b % B][:, 2, :], nr[b % B][:, 1, :], ACT.Tanh).then_inc(tanhed, 1)
                        if first:
                            for b in step(t, 1):
                                act.wait_ge(biased, nth_node(i, b))
                                nc.scalar.activation(xn[b % B][:, :, :], o[b % B][:, :, :], ACT.Relu).then_inc(squared, 1)
                                act.wait_ge(squared, i * (2 * G) + (2 * b + 1))
                                nc.scalar.activation(sq[b % B][:, :, :], xn[b % B][:, :, :], ACT.Square).then_inc(squared, 1)
                        for b in step(t, 0):
                            act.wait_ge(asked, nth_node(i, b))
                            nc.scalar.activation(e[b % B][:, :, :, :], e[b % B][:, :, :, :], ACT.Exp).then_inc(raised, 1)

            @block.tensor
            def _(pe):
                with pe.Fori(0, passes) as i:
                    for t in range(G + (L + 3)):
                        if not first:
                            for b in step(t, L + 3):
                                pe.wait_ge(hidden, nth_node(i, b) + R)
                                pe.wait_ge(moved, nth_node(i, b))
                                for q in range(Q):
                                    last = nc.tensor.transpose(pb[b % R][:, q * P:(q + 1) * P],
                                                               xt[b % B][:, q * P:(q + 1) * P], g.ident[:, :])
                                last.then_inc(back, 1)
                        for b in step(t, L + 2):
                            pe.wait_ge(copied, nth_node(i, b) + R)
                            pe.wait_ge(moved if first else hidden, nth_node(i, b))
                            if first:
                                for q in range(Q):
                                    w = (q % 2) * (D + 2)
                                    last = nc.tensor.matmul(pm[b % R][:, q // 2, w:w + D + 2], xt[b % B][:, q * P:(q + 1) * P],
                                                            g.w1aug[:, :], start=True, stop=True)
                                last.then_inc(product, 1)
                            else:
                                nc.tensor.matmul(pm[b % R][:, 0, :], g.projw[:, :], xt[b % B][:, :], start=True,
                                                 stop=True).then_inc(product, 1)
                        for b in step(t, L + 1):
                            pe.wait_ge(normed, nth_node(i, b) + B)
                            pe.wait_ge(copied, nth_node(i, b))
                            for q in range(Q):
                                last = nc.tensor.transpose(pt[b % R][:, q * P:(q + 1) * P], xn[b % B][:, q, :], g.ident[:, :])
                            last.then_inc(turned, 1)

            @block.vector
            def _(v):
                for b in range(B):
                    nc.vector.memset(tr[b][:, :, :], 0.0)
                    last = nc.vector.memset(ao[b][:, :, :], 0.0)
                last.then_inc(gate, 1)
                v.wait_ge(gate, 1)
                v.sem_inc(normed, B)
                v.sem_inc(moved, R)
                v.sem_inc(hidden, R)
                v.sem_inc(freed, B)
                per = G * (30 if first else 21)
                with v.Fori(0, passes) as i:
                    own = Own(v, ch, i, per)
                    for t in range(G + (L + 3)):
                        for b in step(t, L + 2 + (not first)):
                            if first:
                                v.wait_ge(product, nth_node(i, b))
                                view = pm[b % R][:, :, 0:2 * (D + 2)].rearrange("p a (s c) -> p a s c", s=2)
                                own.mark(nc.vector.tensor_copy(
                                    tr[b % B][:, :, 0:D + 1].rearrange("p (a s) c -> p a s c", s=2), view[:, :, :, 0:D + 1]))
                                nc.vector.tensor_copy(ao[b % B][:, :, 0:1].rearrange("p (a s) c -> p a s c", s=2),
                                                      view[:, :, :, D + 1:D + 2]).then_inc(moved, 1)
                            else:
                                v.wait_ge(back, nth_node(i, b))
                                nc.vector.tensor_copy(hr[b % B][:, :, :].rearrange("p q d -> p (q d)"),
                                                      pb[b % R][:, :]).then_inc(moved, 1)
                        for b in step(t, L + 1):
                            v.wait_ge(scale, nth_node(i, b))
                            norm_apply(nc, xn[b % B], o[b % B], mv[b % B], rs[b % B]).then_inc(normed, 1)
                        if first:
                            for b in step(t, 3):
                                v.wait_ge(rooted, nth_node(i, b))
                                own.mark(nc.vector.reciprocal(nr[b % B][:, 3, :], nr[b % B][:, 1, :]))
                                v.wait_ge(tanhed, nth_node(i, b))
                                own.mark(nc.vector.tensor_scalar(nr[b % B][:, 2, :], nr[b % B][:, 2, :], MAX_NORM, None, ALU.min))
                                own.wait()
                                own.link(nc.vector.tensor_tensor(nr[b % B][:, 3, :], nr[b % B][:, 3, :], nr[b % B][:, 2, :],
                                                                 ALU.mult))
                                for q in range(Q):
                                    own.mark(nc.vector.scalar_tensor_tensor(
                                        o[b % B][:, q, :], xn[b % B][:, q, :], nr[b % B][:, 3, q:q + 1], x[b % B][:, q, :],
                                        ALU.mult, ALU.add))
                        for b in step(t, L):
                            own.wait()
                            norm_stats(nc, own, gate, o[b % B], st[b % B], mv[b % B], ve[b % B]).then_inc(varasked, 1)
                        if first:
                            for b in step(t, 2):
                                v.wait_ge(squared, i * (2 * G) + (2 * b + 2))
                                own.link(nc.vector.tensor_reduce(nr[b % B][:, 0, :], sq[b % B][:, :, :], AX_X, ALU.add))
                                nc.vector.tensor_scalar(nr[b % B][:, 0, :], nr[b % B][:, 0, :], MIN_NORM ** 2, None,
                                                        ALU.max).then_inc(normasked, 1)
                        for b in step(t, 1):
                            v.wait_ge(raised, nth_node(i, b))
                            own.link(nc.vector.tensor_tensor(den[b % B][:, :, :], ag[b % B][:, :, DEN:DEN + heads],
                                                             e[b % B][:, 0, :, :], ALU.mult))
                            own.link(nc.vector.tensor_tensor(den[b % B][:, :, :], den[b % B][:, :, :], e[b % B][:, 1, :, :], ALU.add))
                            if first:
                                own.link(nc.vector.tensor_scalar(den[b % B][:, :, :], den[b % B][:, :, :], MIN_NORM, None,
                                                                 ALU.max))
                            own.link(nc.vector.reciprocal(den[b % B][:, :, :], den[b % B][:, :, :]))
                            for n in range(2):
                                own.mark(nc.vector.tensor_tensor(e[b % B][:, n, :, :], e[b % B][:, n, :, :], den[b % B][:, :, :],
                                                                 ALU.mult))
                            own.wait()

                            def hv(a):
                                return a.rearrange("p q (h d) -> p q h d", h=heads)

                            def w(n):
                                return e[b % B][:, n, :, :].unsqueeze(3).to_broadcast([P, Q, heads, dh])

                            own.mark(nc.vector.tensor_tensor(hv(ag[b % B][:, :, 0:D]), hv(ag[b % B][:, :, 0:D]), w(0), ALU.mult))
                            own.link(nc.vector.tensor_tensor(hv(se[b % B][:, :, 0:D]), hv(se[b % B][:, :, 0:D]), w(1), ALU.mult))
                            own.link(nc.vector.tensor_tensor(o[b % B][:, :, :], ag[b % B][:, :, 0:D], se[b % B][:, :, 0:D], ALU.add))
                            bb = bias[:, :].unsqueeze(1).to_broadcast([P, Q, D])
                            v.wait_ge(freed, nth_node(i, b))
                            nc.vector.tensor_tensor(o[b % B][:, :, :], o[b % B][:, :, :], bb, ALU.add).then_inc(biased, 1)
                            if not first:
                                v.wait_ge(biased, nth_node(i, b))
                                own.mark(nc.vector.tensor_tensor(o[b % B][:, :, :], o[b % B][:, :, :], x[b % B][:, :, :], ALU.add))
                        for b in step(t, 0):
                            v.wait_ge(loaded[b % B], turn(i, b) * 48)
                            v.wait_ge(gathered[b % B], turn(i, b) * 16 * Q)
                            own.link(nc.vector.tensor_tensor(s[b % B][:, :, :], se[b % B][:, :, D:D + heads],
                                                             ai[b % B][:, :, 0:heads], ALU.add))
                            own.link(nc.vector.scalar_tensor_tensor(s[b % B][:, :, :], s[b % B][:, :, :], SLOPE, s[b % B][:, :, :],
                                                                    ALU.mult, ALU.max))
                            ms = ag[b % B][:, :, MAXC:MAXC + heads]
                            own.link(nc.vector.tensor_tensor(m[b % B][:, :, :], ms, s[b % B][:, :, :], ALU.max))
                            own.link(nc.vector.tensor_tensor(e[b % B][:, 0, :, :], ms, m[b % B][:, :, :], ALU.subtract))
                            nc.vector.tensor_tensor(e[b % B][:, 1, :, :], s[b % B][:, :, :], m[b % B][:, :, :],
                                                    ALU.subtract).then_inc(asked, 1)
                    own.end()



def phase_relate(g, n):
    nc = g.nc
    pre = f"r{n}_"
    with ExitStack() as ctx:
        def sb(name, shape, dt=F32):
            return ctx.enter_context(nc.sbuf_tensor(pre + name, shape, dt))

        idx = [sb(f"idx{b}", [P, 2, KC], I32) for b in range(NB)]
        fac = [sb(f"fac{b}", [P, 2, KC]) for b in range(NB)]
        r = [sb(f"r{b}", [P, KC, D]) for b in range(NB)]
        ty = [sb(f"ty{b}", [P, KC, P]) for b in range(NB)]
        w = sb("w", [P, TYPES, D])
        ht = [sb(f"ht{b}", [P, P]) for b in range(2)]
        hm = [sb(f"hm{b}", [P, TYPES, P]) for b in range(2)]
        pt = [ctx.enter_context(nc.psum_tensor(f"{pre}pt{b}", [P, 512], F32)) for b in range(2)]
        pm = [ctx.enter_context(nc.psum_tensor(f"{pre}pm{b}", [P, 512], F32)) for b in range(2)]
        wloaded = g.sem(pre + "wloaded")
        listed = [g.sem(pre + f"listed{b}") for b in range(NB)]
        gathered = [g.indirect_sem(pre + f"gathered{b}") for b in range(NB)]
        stored = [g.sem(pre + f"stored{b}") for b in range(NB)]
        turned = g.sem(pre + "turned")
        copied = g.sem(pre + "copied")
        masked = g.sem(pre + "masked")
        product = g.sem(pre + "product")
        added = g.sem(pre + "added")
        stated = g.sem(pre + "stated")
        cleared = g.sem(pre + "cleared")
        gate = g.sem(pre + "gate")
        passes = ECHUNK // NB
        per = NB * KC
        assert per % 2 == 0
        with nc.Block() as block:
            @block.sync
            def _(sp):
                sp.dma_start(w[:, :, :], g.ins["edgew"][n]).then_inc(wloaded, 16)

                def types(i, b):
                    k0 = i * (NB * KC) + b * KC
                    src = g.type_rows[bass.ds(k0, KC)].rearrange("k p -> (k p)").unsqueeze(0).to_broadcast([P, KC * P])
                    sp.dma_start(ty[b][:, :, :].rearrange("p k e -> p (k e)"), src).then_inc(listed[b], 16)

                edge_streams(g, sp, idx, fac, r, listed, gathered, 16, stated, stored, g.sums, types)

            @block.gpsimd
            def _(pool):
                pool.wait_ge(cleared, 1)

                def gathers(b):
                    for k in range(KC):
                        pool.indirect_dma_start(
                            out=r[b][:, k, 0:D], out_offset=None, in_=g.hr[n],
                            in_offset=bass.IndirectOffsetOnAxis(ap=idx[b][:, 0, k:k + 1], axis=0)
                        ).then_inc(gathered[b], 16)

                edge_gathers(g, pool, gathers, listed, 48, stated, stored, gate)

            @block.tensor
            def _(pe):
                pe.wait_ge(wloaded, 16)
                with pe.Fori(0, passes) as i:
                    for j in range(per + 1):
                        if j < per:
                            b, k = divmod(j, KC)
                            if k == 0:
                                pe.wait_ge(gathered[b], i * (16 * KC) + 16 * KC)
                            pe.wait_ge(copied, i * per + (j + 1))
                            nc.tensor.transpose(pt[j % 2][:, 0:P], r[b][:, k, 0:D], g.ident[:, :]).then_inc(turned, 1)
                        if j > 0:
                            u = j - 1
                            pe.wait_ge(masked, i * per + (u + 3))
                            pe.wait_ge(added, i * per + (u + 1))
                            for t in range(TYPES):
                                last = nc.tensor.matmul(pm[u % 2][:, 0:D], hm[u % 2][:, t, :], w[:, t, :],
                                                        start=(t == 0), stop=(t == TYPES - 1))
                            last.then_inc(product, 1)

            @block.scalar
            def _(act):
                act.sem_inc(copied, 2)
                with act.Fori(0, passes) as i:
                    for j in range(per):
                        act.wait_ge(turned, i * per + (j + 1))
                        act.wait_ge(masked, i * per + (j + 1))
                        nc.scalar.copy(ht[j % 2][:, :], pt[j % 2][:, 0:P]).then_inc(copied, 1)

            @block.vector
            def _(v):
                for b in range(NB):
                    last = nc.vector.memset(r[b][:, :, :], 0.0)
                last.then_inc(cleared, 1)
                v.wait_ge(cleared, 1)
                v.sem_inc(masked, 2)
                v.sem_inc(added, 2)
                with v.Fori(0, passes) as i:
                    for j in range(per + 1):
                        if j < per:
                            b, k = divmod(j, KC)
                            if k == 0:
                                v.wait_ge(listed[b], i * 48 + 48)
                                v.sem_inc(gate, 1)
                            v.wait_ge(copied, i * per + (j + 3))
                            if j >= 2:
                                v.wait_ge(product, i * per + (j - 1))
                            for t in range(TYPES):
                                last = nc.vector.scalar_tensor_tensor(hm[j % 2][:, t, :], ty[b][:, k, :], float(t),
                                                                      ht[j % 2][:, :], ALU.is_equal, ALU.mult)
                            last.then_inc(masked, 1)
                        if j > 0:
                            b, k = divmod(j - 1, KC)
                            v.wait_ge(product, i * per + j)
                            v.wait_ge(added, i * per + (j + 1))
                            prev = r[b][:, k - 1, 0:D] if k else r[(b - 1) % NB][:, KC - 1, 0:D]
                            nc.vector.scalar_tensor_tensor(r[b][:, k, 0:D], prev, fac[b][:, 0, k:k + 1],
                                                           pm[(j - 1) % 2][:, 0:D], ALU.mult,
                                                           ALU.add).then_inc(added, 1)
                            if k == KC - 1:
                                v.wait_ge(added, i * per + (j + 2))
                                v.sem_inc(stated, 1)
                nc.vector.tensor_copy(g.last[:, 0:D], r[NB - 1][:, KC - 1, :]).then_inc(cleared, 1)
                v.wait_ge(cleared, 2)


def phase_gru(g, n):
    nc = g.nc
    pre = f"g{n}_"
    final = n == 1
    with ExitStack() as ctx:
        def sb(name, shape, dt=F32):
            return [ctx.enter_context(nc.sbuf_tensor(f"{pre}{name}{b}", shape, dt)) for b in range(B)]

        ag = sb("ag", [P, Q, D])
        idx = sb("idx", [P, Q], I32)
        h = sb("h", [P, CHUNK])
        x = sb("x", [P, Q, D])
        at = sb("at", [P, CHUNK])
        trz = sb("trz", [P, 2, CHUNK])
        hn = sb("hn", [P, CHUNK])
        c = sb("c", [P, CHUNK])
        hy = sb("hy", [P, CHUNK])
        hr = sb("hr", [P, Q, D])
        st = sb("st", [P, Q, 6])
        mv = sb("mv", [P, Q, 2])
        ve = sb("ve", [P, Q])
        rs = sb("rs", [P, Q])
        xn = sb("xn", [P, Q, D]) if final else None
        pa = ctx.enter_context(nc.psum_tensor(pre + "pa", [P, 512], F32))
        pg = [ctx.enter_context(nc.psum_tensor(f"{pre}pg{k}", [P, 512], F32)) for k in range(4)]
        pb = ctx.enter_context(nc.psum_tensor(pre + "pb", [P, 512], F32))
        pp = [ctx.enter_context(nc.psum_tensor(f"{pre}pp{k}", [P, 512], F32)) for k in range(2)]
        gathered = [g.indirect_sem(f"{pre}gathered{b}") for b in range(B)]
        copied_idx = g.sem(pre + "copied_idx")
        loaded = [g.sem(f"{pre}loaded{b}") for b in range(B)]
        turned = g.sem(pre + "turned")
        copied = g.sem(pre + "copied")
        gates = g.sem(pre + "gates")
        squashed = g.sem(pre + "squashed")
        casked = g.sem(pre + "casked")
        cand = g.sem(pre + "cand")
        hidden = g.sem(pre + "hidden")
        read = g.sem(pre + "read")
        back = g.sem(pre + "back")
        moved = g.sem(pre + "moved")
        varasked = g.sem(pre + "varasked")
        scale = g.sem(pre + "scale")
        normed = g.sem(pre + "normed")
        turned2 = g.sem(pre + "turned2")
        copied2 = g.sem(pre + "copied2")
        product = g.sem(pre + "product")
        drawn = g.sem(pre + "drawn")
        stored = [g.sem(f"{pre}stored{b}") for b in range(B)]
        freed = g.sem(pre + "freed")
        ch = g.sem(pre + "chain")
        gate = g.sem(pre + "gate")
        passes = NCHUNK // G
        nload = 2 if final else 1
        nstore = 3 if final else 2
        gb = g.gb[n]
        L = 5
        with nc.Block() as block:
            @block.sync
            def _(sp):
                with sp.Fori(0, passes) as i:
                    for b in range(G):
                        sp.wait_ge(moved, nth_node(i, b))
                        ci = i * G + b
                        sp.dma_start(h[b % B][:, :], g.ht[n][bass.ds(ci, 1)].rearrange(
                            "c p n -> (c p) n")).then_inc(loaded[b % B], 16)
                        if final:
                            sp.dma_start(x[b % B][:, :, :], rows(g.x[2], ci)).then_inc(loaded[b % B], 16)

            @block.gpsimd
            def _(pool):
                seq = StateGathers(g, pool, idx, ag, gathered, copied_idx, g.sums)
                for b in range(B):
                    seq.rows(0, b)
                    seq.gather(0, b, 0, Q)
                with pool.Fori(0, passes) as i:
                    for t in range(G + 7):
                        for b in step(t, 7):
                            gated(pool, stored[b % B], turn(i, b) * 16 * nstore, freed)
                        if final:
                            for b in step(t, 3):
                                pool.wait_ge(varasked, nth_node(i, b))
                                pool.tensor_tensor(rs[b % B][:, :], ve[b % B][:, :], g.mhalf[:, 0:Q], ALU.pow).then_inc(scale, 1)
                                seq.rows(i, b + B, copied, nth_node(i, b) + 1)
                                seq.gather(i, b + B, 0, Q)
                        if not final:
                            for b in step(t, 1):
                                seq.rows(i, b + B, copied, nth_node(i, b) + 1)
                                seq.gather(i, b + B, 0, Q)
                for b in range(B):
                    pool.wait_ge(gathered[b % B], (passes * (G // B) + 1) * 16 * Q)

            @block.tensor
            def _(pe):
                with pe.Fori(0, passes) as i:
                    for t in range(G + (L + 1)):
                        if final:
                            for b in step(t, L + 1):
                                pe.wait_ge(copied2, nth_node(i, b) + 1)
                                pe.wait_ge(drawn, nth_node(i, b) + (B - 1))
                                for q in range(Q):
                                    last = nc.tensor.matmul(pp[q // 2][:, (q % 2) * 2 * D:(q % 2 + 1) * 2 * D],
                                                            at[b % B][:, q * P:(q + 1) * P], g.wm1[:, :], start=True,
                                                            stop=True)
                                last.then_inc(product, 1)
                        if final:
                            for b in step(t, L):
                                pe.wait_ge(normed, nth_node(i, b))
                                pe.wait_ge(copied, i * G + (1 + min(b + L, G)))
                                pe.wait_ge(copied2, nth_node(i, b))
                                for q in range(Q):
                                    last = nc.tensor.transpose(pa[:, q * P:(q + 1) * P], xn[b % B][:, q, :], g.ident[:, :])
                                last.then_inc(turned2, 1)
                        for b in step(t, 3):
                            pe.wait_ge(hidden, nth_node(i, b))
                            pe.wait_ge(read, nth_node(i, b))
                            for q in range(Q):
                                hq = hy[b % B][:, q * P:(q + 1) * P]
                                if final:
                                    last = nc.tensor.matmul(pb[:, q * P:(q + 1) * P], hq, g.outw[:, :], start=True,
                                                            stop=True)
                                else:
                                    last = nc.tensor.transpose(pb[:, q * P:(q + 1) * P], hq, g.ident[:, :])
                            last.then_inc(back, 1)
                        for b in step(t, 1):
                            pe.wait_ge(copied, nth_node(i, b) + 1)
                            wi, wh = g.wih[n], g.whh[n]
                            pe.wait_ge(squashed, i * (3 * G) + (3 * b + 1))
                            nc.tensor.matmul(pg[0][:, :], wi[:, 0:D], at[b % B][:, :], start=True, stop=False)
                            nc.tensor.matmul(pg[0][:, :], wh[:, 0:D], h[b % B][:, :], start=False,
                                             stop=True).then_inc(gates, 1)
                            pe.wait_ge(squashed, i * (3 * G) + (3 * b + 2))
                            nc.tensor.matmul(pg[3][:, :], wh[:, 2 * D:3 * D], h[b % B][:, :], start=True,
                                             stop=True).then_inc(gates, 1)
                            pe.wait_ge(casked, nth_node(i, b))
                            nc.tensor.matmul(pg[2][:, :], wi[:, 2 * D:3 * D], at[b % B][:, :], start=True,
                                             stop=True).then_inc(gates, 1)
                            pe.wait_ge(squashed, i * (3 * G) + (3 * b + 3))
                            nc.tensor.matmul(pg[1][:, :], wi[:, D:2 * D], at[b % B][:, :], start=True, stop=False)
                            nc.tensor.matmul(pg[1][:, :], wh[:, D:2 * D], h[b % B][:, :], start=False,
                                             stop=True).then_inc(gates, 1)
                        for b in step(t, 0):
                            pe.wait_ge(loaded[b % B], turn(i, b) * 16 * nload)
                            pe.wait_ge(gathered[b % B], turn(i, b) * 16 * Q)
                            pe.wait_ge(copied, nth_node(i, b))
                            if final:
                                pe.wait_ge(copied2, i * G + (1 + max(0, b + 1 - L)))
                            for q in range(Q):
                                last = nc.tensor.transpose(pa[:, q * P:(q + 1) * P], ag[b % B][:, q, :], g.ident[:, :])
                            last.then_inc(turned, 1)

            @block.scalar
            def _(act):
                act.sem_inc(copied, 1)
                act.sem_inc(copied2, 1)
                act.sem_inc(squashed, 3)
                with act.Fori(0, passes) as i:
                    for t in range(G + (L + 1)):
                        if final:
                            for b in step(t, L + 1):
                                ci = i * G + b
                                act.wait_ge(drawn, nth_node(i, b) + B)
                                for k, tab in enumerate((g.ta, g.tb)):
                                    act.dma_start(rows(tab, ci), trz[b % B][:, k, :].rearrange("p (q d) -> p q d", q=Q)
                                                  ).then_inc(stored[b % B], 16)
                        if final:
                            for b in step(t, L):
                                ci = i * G + b
                                act.wait_ge(normed, nth_node(i, b))
                                act.dma_start(rows(g.x[3], ci), xn[b % B][:, :, :]).then_inc(stored[b % B], 16)
                                act.wait_ge(turned2, nth_node(i, b))
                                nc.scalar.copy(at[b % B][:, :], pa[:, :]).then_inc(copied2, 1)
                        if not final:
                            for b in step(t, 4):
                                ci = i * G + b
                                act.wait_ge(hidden, nth_node(i, b))
                                act.dma_start(g.ht[1][bass.ds(ci, 1)].rearrange("c p n -> (c p) n"),
                                              hy[b % B][:, :]).then_inc(stored[b % B], 16)
                                act.wait_ge(moved, nth_node(i, b) + B)
                                act.dma_start(rows(g.hr[1], ci), hr[b % B][:, :, :]).then_inc(stored[b % B], 16)
                        for b in step(t, 2):
                            act.wait_ge(casked, nth_node(i, b) + 1)
                            nc.scalar.activation(c[b % B][:, :], c[b % B][:, :], ACT.Tanh, bias=gb[:, 2:3]).then_inc(cand, 1)
                        for b in step(t, 1):
                            act.wait_ge(freed, nth_node(i, b))
                            act.wait_ge(gates, i * (4 * G) + (4 * b + 1))
                            nc.scalar.activation(trz[b % B][:, 0, :], pg[0][:, :], ACT.Tanh, bias=gb[:, 0:1],
                                                 scale=0.5).then_inc(squashed, 1)
                            act.wait_ge(gates, i * (4 * G) + (4 * b + 2))
                            nc.scalar.activation(hn[b % B][:, :], pg[3][:, :], ACT.Identity,
                                                 bias=gb[:, 3:4]).then_inc(squashed, 1)
                            act.wait_ge(gates, i * (4 * G) + (4 * b + 4))
                            nc.scalar.activation(trz[b % B][:, 1, :], pg[1][:, :], ACT.Tanh, bias=gb[:, 1:2],
                                                 scale=0.5).then_inc(squashed, 1)
                        for b in step(t, 0):
                            act.wait_ge(turned, nth_node(i, b))
                            act.wait_ge(drawn if final else moved, nth_node(i, b))
                            nc.scalar.copy(at[b % B][:, :], pa[:, :]).then_inc(copied, 1)

            @block.vector
            def _(v):
                v.sem_inc(casked, 1)
                v.sem_inc(read, 1)
                v.sem_inc(moved, B)
                v.sem_inc(freed, B)
                v.sem_inc(drawn, B)
                per = G * (15 if final else 4)
                with v.Fori(0, passes) as i:
                    own = Own(v, ch, i, per)
                    ob = g.outb[:, :].unsqueeze(1).to_broadcast([P, Q, D])
                    for t in range(G + (L + 1)):
                        if final:
                            for b in step(t, L + 1):
                                v.wait_ge(product, nth_node(i, b))
                                for k in range(2):
                                    view = pp[k][:, :].rearrange("p (q a d) -> p a q d", q=2, a=2)
                                    last = nc.vector.tensor_tensor(
                                        trz[b % B][:, :, :].rearrange("p a (q d) -> p a q d", q=Q)[:, :, 2 * k:2 * k + 2, :],
                                        view,
                                        g.bab[:, :, :].unsqueeze(2).to_broadcast([P, 2, 2, D]), ALU.add)
                                last.then_inc(drawn, 1)
                        if final:
                            for b in step(t, 4):
                                v.wait_ge(scale, nth_node(i, b))
                                own.mark(norm_apply(nc, xn[b % B], hr[b % B], mv[b % B], rs[b % B]))
                                own.wait()
                                v.sem_inc(normed, 1)
                                v.sem_inc(moved, 1)
                        if not final:
                            for b in step(t, 3):
                                v.wait_ge(back, nth_node(i, b))
                                nc.vector.tensor_copy(hr[b % B][:, :, :].rearrange("p q d -> p (q d)"),
                                                      pb[:, :]).then_inc(read, 1)
                                v.wait_ge(read, nth_node(i, b) + 1)
                                v.sem_inc(moved, 1)
                        if final:
                            for b in step(t, 3):
                                v.wait_ge(back, nth_node(i, b))
                                own.link(nc.vector.tensor_tensor(hr[b % B][:, :, :],
                                                                 pb[:, :].rearrange("p (q d) -> p q d", q=Q),
                                                                 x[b % B][:, :, :], ALU.add))
                                v.sem_inc(read, 1)
                                own.link(nc.vector.tensor_tensor(hr[b % B][:, :, :], hr[b % B][:, :, :], ob, ALU.add))
                                norm_stats(nc, own, gate, hr[b % B], st[b % B], mv[b % B], ve[b % B]).then_inc(varasked, 1)
                        for b in step(t, 2):
                            v.wait_ge(cand, nth_node(i, b))
                            v.wait_ge(freed, nth_node(i, b))
                            own.link(nc.vector.tensor_tensor(h[b % B][:, :], h[b % B][:, :], c[b % B][:, :], ALU.subtract))
                            own.link(nc.vector.scalar_tensor_tensor(h[b % B][:, :], trz[b % B][:, 1, :], 1.0, h[b % B][:, :],
                                                                    ALU.add, ALU.mult))
                            own.link(nc.vector.scalar_tensor_tensor(h[b % B][:, :], h[b % B][:, :], 0.5, c[b % B][:, :],
                                                                    ALU.mult, ALU.add))
                            nc.vector.tensor_scalar(hy[b % B][:, :], h[b % B][:, :], 0.0, None, ALU.max).then_inc(hidden, 1)
                        for b in step(t, 1):
                            v.wait_ge(squashed, i * (3 * G) + (3 * b + 5))
                            own.link(nc.vector.scalar_tensor_tensor(hn[b % B][:, :], trz[b % B][:, 0, :], 1.0, hn[b % B][:, :],
                                                                    ALU.add, ALU.mult))
                            v.wait_ge(gates, i * (4 * G) + (4 * b + 3))
                            nc.vector.scalar_tensor_tensor(c[b % B][:, :], hn[b % B][:, :], 0.5, pg[2][:, :],
                                                           ALU.mult, ALU.add).then_inc(casked, 1)
                    own.end()



def phase_filter(g):
    nc = g.nc
    pre = "f_"
    with ExitStack() as ctx:
        def sb(name, shape, dt=F32):
            return ctx.enter_context(nc.sbuf_tensor(pre + name, shape, dt))

        idx = [sb(f"idx{b}", [P, 2, KC], I32) for b in range(NB)]
        fac = [sb(f"fac{b}", [P, 2, KC]) for b in range(NB)]
        r = [sb(f"r{b}", [P, KC, ROW]) for b in range(NB)]
        bd = [sb(f"bd{b}", [P, KC, D]) for b in range(NB)]
        ra = [sb(f"ra{b}", [RADIAL, KC, P]) for b in range(NB)]
        dg = sb("dg", [P, KC + 1])
        t1 = [sb(f"t1{b}", [P, P]) for b in range(2)]
        h1 = [sb(f"h1{b}", [P, P]) for b in range(2)]
        t2 = [sb(f"t2{b}", [P, P]) for b in range(2)]
        h2 = [sb(f"h2{b}", [P, P]) for b in range(2)]
        p1 = [ctx.enter_context(nc.psum_tensor(f"{pre}p1{b}", [P, 512], F32)) for b in range(2)]
        p2 = [ctx.enter_context(nc.psum_tensor(f"{pre}p2{b}", [P, 512], F32)) for b in range(2)]
        listed = [g.sem(pre + f"listed{b}") for b in range(NB)]
        gathered = [g.indirect_sem(pre + f"gathered{b}") for b in range(NB)]
        stored = [g.sem(pre + f"stored{b}") for b in range(NB)]
        radial = g.sem(pre + "radial")
        sqd = g.sem(pre + "sqd")
        summed = g.sem(pre + "summed")
        tanh1 = g.sem(pre + "tanh1")
        silu1 = g.sem(pre + "silu1")
        summed2 = g.sem(pre + "summed2")
        tanh2 = g.sem(pre + "tanh2")
        silu2 = g.sem(pre + "silu2")
        added = g.sem(pre + "added")
        stated = g.sem(pre + "stated")
        degrees = g.sem(pre + "degrees")
        cleared = g.sem(pre + "cleared")
        gate = g.sem(pre + "gate")
        passes = ECHUNK // NB
        per = NB * KC
        coeff = -0.5 / (CUTOFF / (RADIAL - 1)) ** 2
        with nc.Block() as block:
            @block.sync
            def _(sp):
                def distances(i, b):
                    k0 = i * (NB * KC) + b * KC
                    src = g.dist_rows[bass.ds(k0, KC)].rearrange("k p -> (k p)").unsqueeze(0)
                    sp.dma_start(ra[b][:, :, :].rearrange("p k e -> p (k e)"),
                                 src.to_broadcast([RADIAL, KC * P])).then_inc(listed[b], 16)

                edge_streams(g, sp, idx, fac, r, listed, gathered, 32, stated, stored, g.states, distances)

            @block.gpsimd
            def _(pool):
                pool.wait_ge(cleared, 1)

                def gathers(b):
                    for k in range(KC):
                        pool.indirect_dma_start(
                            out=r[b][:, k, 0:D], out_offset=None, in_=g.ta,
                            in_offset=bass.IndirectOffsetOnAxis(ap=idx[b][:, 0, k:k + 1], axis=0)
                        ).then_inc(gathered[b], 16)
                        pool.indirect_dma_start(
                            out=bd[b][:, k, :], out_offset=None, in_=g.tb,
                            in_offset=bass.IndirectOffsetOnAxis(ap=idx[b][:, 1, k:k + 1], axis=0)
                        ).then_inc(gathered[b], 16)

                edge_gathers(g, pool, gathers, listed, 48, stated, stored, gate)

            @block.tensor
            def _(pe):
                with pe.Fori(0, passes) as i:
                    for j in range(per + 1):
                        if j < per:
                            b, k = divmod(j, KC)
                            if k == 0:
                                pe.wait_ge(gathered[b], i * (32 * KC) + 32 * KC)
                                pe.wait_ge(radial, nth(i, b))
                            pe.wait_ge(silu1, i * per + (j + 1))
                            o = p1[j % 2][:, 0:P]
                            nc.tensor.matmul(o, r[b][:, k, 0:D], g.ident[:, :], start=True, stop=False)
                            nc.tensor.matmul(o, bd[b][:, k, :], g.ident[:, :], start=False, stop=False)
                            nc.tensor.matmul(o, g.wr[:, :], ra[b][:, k, :], start=False,
                                             stop=True).then_inc(summed, 1)
                        if j > 0:
                            u = j - 1
                            pe.wait_ge(silu1, i * per + (u + 3))
                            pe.wait_ge(added, i * per + (u + 1))
                            o = p2[u % 2][:, 0:D]
                            nc.tensor.matmul(o, h1[u % 2][:, :], g.wm2[:, :], start=True, stop=False)
                            nc.tensor.matmul(o, g.ones[0:1, :], g.bm2[0:1, :], start=False,
                                             stop=True).then_inc(summed2, 1)

            @block.scalar
            def _(act):
                with act.Fori(0, passes) as i:
                    for j in range(per + 2):
                        if j < per:
                            b, k = divmod(j, KC)
                            if k == 0:
                                act.wait_ge(listed[b], i * 48 + 48)
                                nc.scalar.activation(ra[b][:, :, :], ra[b][:, :, :], ACT.Square,
                                                     bias=g.noff[:, 0:1]).then_inc(sqd, 1)
                                act.wait_ge(sqd, nth(i, b))
                                nc.scalar.activation(ra[b][:, :, :], ra[b][:, :, :], ACT.Exp,
                                                     scale=coeff).then_inc(radial, 1)
                            act.wait_ge(summed, i * per + (j + 1))
                            nc.scalar.activation(t1[j % 2][:, :], p1[j % 2][:, 0:P], ACT.Tanh,
                                                 scale=0.5).then_inc(tanh1, 1)
                        if 1 <= j <= per:
                            u = j - 1
                            act.wait_ge(summed2, i * per + (u + 1))
                            nc.scalar.activation(t2[u % 2][:, :], p2[u % 2][:, 0:D], ACT.Tanh,
                                                 scale=0.5).then_inc(tanh2, 1)

            @block.vector
            def _(v):
                for b in range(NB):
                    nc.vector.memset(r[b][:, :, :], 0.0)
                nc.vector.memset(dg[:, :], 0.0).then_inc(cleared, 1)
                v.wait_ge(cleared, 1)
                v.sem_inc(silu1, 2)
                v.sem_inc(added, 2)
                with v.Fori(0, passes) as i:
                    for j in range(per + 1):
                        if j < per:
                            v.wait_ge(tanh1, i * per + (j + 1))
                            nc.vector.scalar_tensor_tensor(h1[j % 2][:, :], t1[j % 2][:, :], 1.0,
                                                           p1[j % 2][:, 0:P], ALU.add, ALU.mult).then_inc(silu1, 1)
                        if j > 0:
                            u = j - 1
                            b, k = divmod(u, KC)
                            v.wait_ge(tanh2, i * per + (u + 1))
                            v.wait_ge(added, i * per + (u + 2))
                            nc.vector.scalar_tensor_tensor(h2[u % 2][:, :], t2[u % 2][:, :], 1.0,
                                                           p2[u % 2][:, 0:D], ALU.add, ALU.mult).then_inc(silu2, 1)
                            v.wait_ge(silu2, i * per + (u + 1))
                            prev = r[b][:, k - 1, 0:D] if k else r[(b - 1) % NB][:, KC - 1, 0:D]
                            nc.vector.scalar_tensor_tensor(r[b][:, k, 0:D], prev, fac[b][:, 0, k:k + 1],
                                                           h2[u % 2][:, :], ALU.mult, ALU.add).then_inc(added, 1)
                            if k == KC - 1:
                                nc.vector.tensor_tensor_scan(dg[:, 1:KC + 1], fac[b][:, 0, :],
                                                             g.ones[:, 0:KC], dg[:, 0:1], ALU.mult,
                                                             ALU.add).then_inc(degrees, 1)
                                v.wait_ge(degrees, i * (2 * NB) + (2 * b + 1))
                                nc.vector.tensor_copy(r[b][:, :, DEN], dg[:, 1:KC + 1])
                                nc.vector.tensor_copy(dg[:, 0:1], dg[:, KC:KC + 1]).then_inc(degrees, 1)
                                v.wait_ge(degrees, i * (2 * NB) + (2 * b + 2))
                                v.wait_ge(added, i * per + (u + 3))
                                v.sem_inc(stated, 1)
                nc.vector.tensor_copy(g.last[:, :], r[NB - 1][:, KC - 1, :]).then_inc(cleared, 1)
                v.wait_ge(cleared, 2)


def phase_update(g):
    nc = g.nc
    pre = "u_"
    with ExitStack() as ctx:
        def sb(name, shape, dt=F32):
            return [ctx.enter_context(nc.sbuf_tensor(f"{pre}{name}{b}", shape, dt)) for b in range(B)]

        x = sb("x", [P, Q, D])
        ag = sb("ag", [P, Q, ROW])
        idx = sb("idx", [P, Q], I32)
        xt = sb("xt", [P, CHUNK])
        at = sb("at", [P, CHUNK])
        dt = sb("dt", [2 * HEADS, CHUNK])
        th = sb("th", [P, CHUNK])
        u = sb("u", [P, CHUNK])
        th2 = sb("th2", [P, CHUNK])
        u2 = sb("u2", [P, CHUNK])
        y = sb("y", [P, Q, D])
        st = sb("st", [P, Q, 6])
        mv = sb("mv", [P, Q, 2])
        ve = sb("ve", [P, Q])
        rs = sb("rs", [P, Q])
        xn = sb("xn", [P, Q, D])
        px = ctx.enter_context(nc.psum_tensor(pre + "px", [P, 512], F32))
        pa = ctx.enter_context(nc.psum_tensor(pre + "pa", [P, 512], F32))
        pd = ctx.enter_context(nc.psum_tensor(pre + "pd", [P, 512], F32))
        pu = [ctx.enter_context(nc.psum_tensor(f"{pre}pu{b}", [P, 512], F32)) for b in range(R)]
        pv = [ctx.enter_context(nc.psum_tensor(f"{pre}pv{b}", [P, 512], F32)) for b in range(R)]
        py = ctx.enter_context(nc.psum_tensor(pre + "py", [P, 512], F32))
        gathered = [g.indirect_sem(f"{pre}gathered{b}") for b in range(B)]
        copied_idx = g.sem(pre + "copied_idx")
        loaded = [g.sem(f"{pre}loaded{b}") for b in range(B)]
        turned = g.sem(pre + "turned")
        copied = g.sem(pre + "copied")
        sum1 = g.sem(pre + "sum1")
        tanh1 = g.sem(pre + "tanh1")
        silu1 = g.sem(pre + "silu1")
        sum2 = g.sem(pre + "sum2")
        tanh2 = g.sem(pre + "tanh2")
        silu2 = g.sem(pre + "silu2")
        sum3 = g.sem(pre + "sum3")
        read3 = g.sem(pre + "read3")
        varasked = g.sem(pre + "varasked")
        scale = g.sem(pre + "scale")
        normed = g.sem(pre + "normed")
        stored = [g.sem(f"{pre}stored{b}") for b in range(B)]
        freed = g.sem(pre + "freed")
        ch = g.sem(pre + "chain")
        gate = g.sem(pre + "gate")
        passes = NCHUNK // G
        with nc.Block() as block:
            @block.sync
            def _(sp):
                with sp.Fori(0, passes) as i:
                    for b in range(G):
                        sp.wait_ge(normed, nth_node(i, b))
                        sp.dma_start(x[b % B][:, :, :], rows(g.x[3], i * G + b)).then_inc(loaded[b % B], 16)

            @block.gpsimd
            def _(pool):
                seq = StateGathers(g, pool, idx, ag, gathered, copied_idx, g.states)
                for b in range(B):
                    seq.rows(0, b)
                    seq.gather(0, b, 0, Q)
                with pool.Fori(0, passes) as i:
                    for t in range(G + 6):
                        for b in step(t, 6):
                            gated(pool, stored[b % B], turn(i, b) * 16, freed)
                        for b in step(t, 3):
                            pool.wait_ge(varasked, nth_node(i, b))
                            pool.tensor_tensor(rs[b % B][:, :], ve[b % B][:, :], g.mhalf[:, 0:Q], ALU.pow).then_inc(scale, 1)
                            seq.rows(i, b + B, copied, nth_node(i, b) + 1)
                            seq.gather(i, b + B, 0, Q)
                for b in range(B):
                    pool.wait_ge(gathered[b % B], (passes * (G // B) + 1) * 16 * Q)

            @block.tensor
            def _(pe):
                mm = nc.tensor.matmul
                with pe.Fori(0, passes) as i:
                    for t in range(G + 3):
                        for b in step(t, 3):
                            pe.wait_ge(silu2, nth_node(i, b) + R)
                            pe.wait_ge(read3, nth_node(i, b))
                            for q in range(Q):
                                last = mm(py[:, q * P:(q + 1) * P], u2[b % B][:, q * P:(q + 1) * P], g.wi2[:, :], start=True,
                                          stop=True)
                            last.then_inc(sum3, 1)
                        for b in step(t, 2):
                            pe.wait_ge(silu1, nth_node(i, b) + R)
                            pe.wait_ge(silu2, nth_node(i, b))
                            mm(pv[b % R][:, :], g.wd[:, :], u[b % B][:, :], start=True, stop=True).then_inc(sum2, 1)
                        for b in step(t, 1):
                            pe.wait_ge(copied, nth_node(i, b) + 1)
                            pe.wait_ge(silu1, nth_node(i, b))
                            mm(pu[b % R][:, :], g.wu1a[:, :], xt[b % B][:, :], start=True, stop=False)
                            mm(pu[b % R][:, :], g.wc[:, :], at[b % B][:, :], start=False, stop=False)
                            mm(pu[b % R][:, :], g.bc[:, :], dt[b % B][:, :], start=False, stop=True).then_inc(sum1, 1)
                        for b in step(t, 0):
                            pe.wait_ge(loaded[b % B], turn(i, b) * 16)
                            pe.wait_ge(gathered[b % B], turn(i, b) * 16 * Q)
                            pe.wait_ge(copied, nth_node(i, b))
                            for q in range(Q):
                                qs = slice(q * P, (q + 1) * P)
                                nc.tensor.transpose(px[:, qs], x[b % B][:, q, :], g.ident[:, :])
                                nc.tensor.transpose(pa[:, qs], ag[b % B][:, q, 0:D], g.ident[:, :])
                                last = nc.tensor.transpose(pd[0:2 * HEADS, qs], ag[b % B][:, q, D:ROW], g.ident[:, :])
                            last.then_inc(turned, 1)

            @block.scalar
            def _(act):
                act.sem_inc(copied, 1)
                with act.Fori(0, passes) as i:
                    for t in range(G + 4):
                        for b in step(t, 4):
                            act.wait_ge(normed, nth_node(i, b) + B)
                            act.dma_start(rows(g.out, i * G + b), xn[b % B][:, :, :]).then_inc(stored[b % B], 16)
                        for b in step(t, 2):
                            act.wait_ge(sum2, nth_node(i, b))
                            nc.scalar.activation(th2[b % B][:, :], pv[b % R][:, :], ACT.Tanh, bias=g.bd[:, 1:2],
                                                 scale=0.5).then_inc(tanh2, 1)
                        for b in step(t, 1):
                            act.wait_ge(sum1, nth_node(i, b))
                            nc.scalar.activation(th[b % B][:, :], pu[b % R][:, :], ACT.Tanh, bias=g.bu1[:, 1:2],
                                                 scale=0.5).then_inc(tanh1, 1)
                        for b in step(t, 0):
                            act.wait_ge(turned, nth_node(i, b))
                            nc.scalar.copy(xt[b % B][:, :], px[:, :])
                            nc.scalar.copy(at[b % B][:, :], pa[:, :])
                            nc.scalar.copy(dt[b % B][:, :], pd[0:2 * HEADS, :]).then_inc(copied, 1)

            @block.vector
            def _(v):
                v.sem_inc(read3, 1)
                v.sem_inc(silu1, R)
                v.sem_inc(silu2, R)
                v.sem_inc(normed, B)
                v.sem_inc(freed, B)
                per = G * (11)
                bb = g.bi2[:, :].unsqueeze(1).to_broadcast([P, Q, D])
                with v.Fori(0, passes) as i:
                    own = Own(v, ch, i, per)

                    def silu(b, o, t, p, bias, done):
                        own.link(nc.vector.tensor_scalar(o[b % B][:, :], p[b % R][:, :], bias, None, ALU.add))
                        nc.vector.scalar_tensor_tensor(o[b % B][:, :], t[b % B][:, :], 1.0, o[b % B][:, :], ALU.add,
                                                       ALU.mult).then_inc(done, 1)

                    for t in range(G + 4):
                        for b in step(t, 4):
                            v.wait_ge(scale, nth_node(i, b))
                            v.wait_ge(freed, nth_node(i, b))
                            norm_apply(nc, xn[b % B], y[b % B], mv[b % B], rs[b % B]).then_inc(normed, 1)
                        for b in step(t, 3):
                            v.wait_ge(sum3, nth_node(i, b))
                            nc.vector.tensor_tensor(y[b % B][:, :, :], py[:, :].rearrange("p (q d) -> p q d", q=Q),
                                                    x[b % B][:, :, :], ALU.add).then_inc(read3, 1)
                            v.wait_ge(read3, nth_node(i, b) + 1)
                            own.link(nc.vector.tensor_tensor(y[b % B][:, :, :], y[b % B][:, :, :], bb, ALU.add))
                            norm_stats(nc, own, gate, y[b % B], st[b % B], mv[b % B], ve[b % B]).then_inc(varasked, 1)
                        for b in step(t, 2):
                            v.wait_ge(tanh2, nth_node(i, b))
                            silu(b, u2, th2, pv, g.bd[:, 0:1], silu2)
                        for b in step(t, 1):
                            v.wait_ge(tanh1, nth_node(i, b))
                            silu(b, u, th, pu, g.bu1[:, 0:1], silu1)
                    own.end()



PHASES = [
    phase_weights, phase_edges,
    phase_product, phase_map, phase_log, phase_places,
    lambda g: phase_attend(g, 0, HEADS), lambda g: phase_join(g, 0, HEADS, g.states),
    lambda g: phase_settle(g, 0, HEADS),
    lambda g: phase_attend(g, 1, 1), lambda g: phase_join(g, 1, 1, g.states), lambda g: phase_settle(g, 1, 1),
    lambda g: phase_relate(g, 0), lambda g: phase_join(g, 2, 0, g.sums, D), lambda g: phase_gru(g, 0),
    lambda g: phase_relate(g, 1), lambda g: phase_join(g, 3, 0, g.sums, D), lambda g: phase_gru(g, 1),
    phase_filter, lambda g: phase_join(g, 4, 0, g.states), phase_update,
]


def gnn_kernel(nc, ins, out):
    with ExitStack() as ctx:
        g = Program(nc, ins, out, ctx)
        for phase in PHASES:
            g.sems = []
            with ExitStack() as g.sem_ctx:
                phase(g)
                with nc.Block() as block:
                    @block.gpsimd
                    def _(pool):
                        for sem in g.sems:
                            pool.sem_clear(sem)



def kernel(**inputs):
    import numpy as np
    import concourse.bacc as bacc
    from concourse.bass_utils import run_bass_kernel_spmd

    a = {k: np.asarray(v) for k, v in inputs.items()}

    def padded(v, n, fill=0):
        out = np.full((n,) + v.shape[1:], fill, v.dtype)
        out[:v.shape[0]] = v
        return out

    def col(v):
        return v.reshape(-1, 1)

    def row(v):
        return v.reshape(1, -1)

    att = a["L0_gnn_att"][0]
    dh = D // HEADS
    attm = np.zeros((HEADS, dh, 2 * HEADS), att.dtype)
    for h in range(HEADS):
        attm[h, :, h] = att[h, dh:]
        attm[h, :, HEADS + h] = att[h, :dh]
    lay = {
        "x": padded(a["x"], NPAD),
        "src": padded(a["src"], P * KE).reshape(P, KE),
        "dst": padded(a["dst"], P * KE, N).reshape(P, KE),
        "etype": padded(a["edge_type_8"], P * KE).reshape(P, KE),
        "dist": padded(a["edge_weight"], P * KE).reshape(P, KE),
        "w0": a["L0_gnn_W"], "w0t": a["L0_gnn_W"].T, "attm": attm.reshape(D, 2 * HEADS),
        "lin_bias": col(a["L0_gnn_lin_bias"]), "conv_bias": row(a["L0_gnn_conv_bias"]),
        "w1": a["L1_gnn_W"], "w1t": a["L1_gnn_W"].T,
        "att1": np.stack([a["L1_gnn_att_src"], a["L1_gnn_att_dst"]], 1), "bias1": row(a["L1_gnn_bias"]),
        "projwt": a["L2_gnn_node_proj_w"].T, "projb": col(a["L2_gnn_node_proj_b"]),
        "edgew": a["L2_gnn_edge_W"].transpose(0, 3, 1, 2),
        "wiht": a["L2_gnn_gru_wih"].transpose(0, 2, 1), "whht": a["L2_gnn_gru_whh"].transpose(0, 2, 1),
        "biht": a["L2_gnn_gru_bih"].reshape(2, 3, D).transpose(0, 2, 1),
        "bhht": a["L2_gnn_gru_bhh"].reshape(2, 3, D).transpose(0, 2, 1),
        "outwt": a["L2_gnn_out_w"].T, "out_b": row(a["L2_gnn_out_b"]),
        "wm1": a["L3_gnn_Wm1"], "bm1": row(a["L3_gnn_bm1"]), "wm2": a["L3_gnn_Wm2"],
        "bm2": row(a["L3_gnn_bm2"]), "wm3t": a["L3_gnn_Wm3"].T, "bm3": col(a["L3_gnn_bm3"]),
        "wu1": a["L3_gnn_Wu1"], "bu1": col(a["L3_gnn_bu1"]), "wu2t": a["L3_gnn_Wu2"].T,
        "bu2": col(a["L3_gnn_bu2"]), "wi1": a["L3_gnn_Wi1"], "bi1": col(a["L3_gnn_bi1"]),
        "wi2": a["L3_gnn_Wi2"], "bi2": row(a["L3_gnn_bi2"]),
    }
    lay = {k: np.ascontiguousarray(v) for k, v in lay.items()}
    nc = bacc.Bacc("TRN2", target_bir_lowering=False, num_devices=1)
    ins = {k: nc.dram_tensor(f"in_{k}", v.shape, mybir.dt.from_np(v.dtype), kind="ExternalInput").ap()
           for k, v in lay.items()}
    out = nc.dram_tensor("out", [NPAD, D], F32, kind="ExternalOutput").ap()
    gnn_kernel(nc, ins, out)
    r = run_bass_kernel_spmd(nc, [{f"in_{k}": v for k, v in lay.items()}], core_ids=[0])
    return r.results[0]["out"][:N]
```

```python
from contextlib import ExitStack

import concourse.bass as bass
from concourse import mybir

F32 = mybir.dt.float32
I32 = mybir.dt.int32
ALU = mybir.AluOpType
ACT = mybir.ActivationFunctionType
AX_X = mybir.AxisListType.X

P = 128
D = 128
N = 50000
E = 50000
HEADS = 4
TYPES = 8
RADIAL = 50
CUTOFF = 10.0

Q = 4
CHUNK = P * Q
G = 14
B = 7
R = 2
NCHUNK = -(-N // CHUNK)
NPAD = NCHUNK * CHUNK
COLS = NCHUNK * Q
KC = 14
NB = 4
ECHUNK = -(-E // (P * KC))
KE = ECHUNK * KC
assert ECHUNK % NB == 0 and NCHUNK % G == 0 and NPAD == P * KE
assert ECHUNK == 4 * (NCHUNK // G) and G == 2 * B and KC % B == 0
ROW = D + 2 * HEADS
TROW = D + HEADS
DEN = D
MAXC = D + HEADS
LOWEST = -1.0e30
EMPTY = NPAD
SKIP = 1 << 20
EPS = 1e-5
MIN_NORM = 1e-15
MAX_NORM = 1.0 - 0.004
SLOPE = 0.2


def nth_node(i, b):
    return i * G + (b + 1)


def turn(i, b):
    return i * (G // B) + (b // B + 1)


FILL, RUN, DRAIN = range(3)


def laps(eng):
    yield 0, FILL
    with eng.Fori(1, NCHUNK // G) as i:
        yield i, RUN
    yield NCHUNK // G, DRAIN


def steps(part, last):
    return range(last) if part == DRAIN else range(G)


def step(part, t, lag):
    b = t - lag
    there = {FILL: b >= 0, RUN: True, DRAIN: b < 0}[part]
    return [b] if there else []


class Own:

    def __init__(self, eng, sem, i=None, per=0):
        self.eng, self.sem, self.per, self.n, self.waited = eng, sem, per, 0, None
        self.base = None if i is None else eng.snap(i * per)

    def mark(self, ins):
        self.n += 1
        ins.then_inc(self.sem, 1)
        return self.n

    def wait(self, n=None):
        n = self.n if n is None else n
        self.eng.wait_ge(self.sem, n if self.base is None else self.base + n)

    def wait_new(self):
        if self.n != self.waited:
            self.wait()
        self.waited = self.n

    def link(self, ins):
        self.mark(ins)
        self.wait()

    def lap(self, part, i, per):
        self.base = self.eng.snap((i - 1) * per) if part == RUN else None
        self.before, self.per = self.n, per

    def end(self, part=None):
        if part is None:
            assert self.base is None or self.n == self.per, (self.sem, self.n, self.per)
        elif part == RUN:
            assert self.n == self.before + self.per, (self.sem, self.n - self.before, self.per)
            self.n = self.before + (NCHUNK // G - 1) * self.per


def gated(eng, sem, value, gate):
    eng.wait_ge(sem, value)
    eng.sem_inc(gate, 1)


class Program:

    def __init__(self, nc, ins, out, ctx):
        self.nc, self.ins, self.out, self.ctx = nc, ins, out, ctx

        def table(name, shape, dt=F32):
            return nc.dram_tensor(name, shape, dt, kind="Internal").ap()

        self.edge_idx = table("edge_idx", [ECHUNK, P, 2, KC], I32)
        self.place_idx = table("place_idx", [ECHUNK, P, 2, KC], I32)
        self.place = table("place", [NPAD, 1], I32)
        self.edge_fac = table("edge_fac", [ECHUNK, P, 2, KC])
        self.records = [table(f"records{n}", [NPAD, 4], I32) for n in range(2)]
        self.type_rows = table("type_rows", [KE, P])
        self.dist_rows = table("dist_rows", [KE, P])
        self.mx = table("mx", [NPAD, ROW])
        self.states = table("states", [EMPTY + P, ROW])
        self.sums = table("sums", [EMPTY + P, D])
        self.t = [table(f"t{n}", [NPAD, TROW]) for n in range(2)]
        self.ai = [table(f"ai{n}", [NPAD, HEADS]) for n in range(2)]
        self.x = [None] + [table(f"x{n}", [NPAD, D]) for n in (1, 2, 3)]
        self.ht = [table(f"ht{n}", [NCHUNK, P, CHUNK]) for n in range(2)]
        self.hr = [table(f"hr{n}", [NPAD, D]) for n in range(2)]
        self.ta = table("ta", [NPAD, D])
        self.tb = table("tb", [NPAD, D])

        self.ident = self.sb("ident", [P, P])
        self.ones = self.sb("ones", [P, P])
        self.half = self.sb("half", [P, 2 * Q])
        self.mhalf = self.sb("mhalf", [P, 2 * Q])
        self.w0aug = self.sb("w0aug", [P, ROW + 1])
        self.yrow = self.sb("yrow", [P, ROW])
        self.y2 = self.sb("y2", [P, 1])
        self.w1aug = self.sb("w1aug", [P, D + 2])
        self.bias0 = self.sb("bias0", [P, D])
        self.bias1 = self.sb("bias1", [P, D])
        self.outb = self.sb("outb", [P, D])
        self.sxx = self.sb("sxx", [P, COLS])
        self.smm = self.sb("smm", [P, COLS])
        self.sxy = self.sb("sxy", [P, COLS])
        self.alpha = self.sb("alpha", [P, COLS])
        self.beta = self.sb("beta", [P, COLS])
        self.bi2 = self.sb("bi2", [P, D])
        self.bab = self.sb("bab", [P, 2, D])
        self.bm2 = self.sb("bm2", [P, D])
        self.projw = self.sb("projw", [P, D])
        self.projb = self.sb("projb", [P, 1])
        self.wih = [self.sb(f"wih{n}", [P, 3 * D]) for n in range(2)]
        self.whh = [self.sb(f"whh{n}", [P, 3 * D]) for n in range(2)]
        self.gb = [self.sb(f"gb{n}", [P, 4]) for n in range(2)]
        self.outw = self.sb("outw", [P, D])
        self.wm1 = self.sb("wm1", [P, 2 * D])
        self.wr = self.sb("wr", [RADIAL, D])
        self.wm2 = self.sb("wm2", [P, D])
        self.wu1a = self.sb("wu1a", [P, D])
        self.wc = self.sb("wc", [P, D])
        self.bc = self.sb("bc", [2 * HEADS, D])
        self.bu1 = self.sb("bu1", [P, 2])
        self.wd = self.sb("wd", [P, D])
        self.bd = self.sb("bd", [P, 2])
        self.wi2 = self.sb("wi2", [P, D])
        self.noff = self.sb("noff", [RADIAL, 1])
        self.cross = self.sb("cross", [P, P])
        self.cross_t = self.sb("cross_t", [P, P])
        self.low_t = self.sb("low_t", [P, P])
        self.last = self.sb("last", [P, ROW])
        self.goes_on = self.sb("goes_on", [P, 1])
        self.first_i = self.sb("first_i", [P, 1], I32)
        self.first_row = self.sb("first_row", [P, 1], I32)
        self.fix_row = self.sb("fix_row", [P, 1], I32)
        self.places = self.sb("places", [P, (NCHUNK + B) * Q], I32)

    def sb(self, name, shape, dt=F32):
        return self.ctx.enter_context(self.nc.sbuf_tensor(name, shape, dt))

    def indirect_sem(self, name):
        return self.ctx.enter_context(self.nc.semaphore(name))

    def sem(self, name):
        s = self.sem_ctx.enter_context(self.nc.semaphore(name))
        self.sems.append(s)
        return s


def rows(table, c, q=Q):
    r = table.rearrange("(c p q) d -> c p q d", p=P, q=q)
    return r[bass.ds(c, 1)].rearrange("c p q d -> (c p) q d")



def phase_weights(g):
    nc, ins = g.nc, g.ins
    with ExitStack() as ctx:
        def sb(name, shape, dt=F32):
            return ctx.enter_context(nc.sbuf_tensor(name, shape, dt))

        w0 = sb("w_w0", [P, D])
        attm = sb("w_attm", [P, 2 * HEADS])
        linb = sb("w_linb", [P, 1])
        w1t = sb("w_w1t", [P, D])
        att1 = sb("w_att1", [P, 2])
        bih = [sb(f"w_bih{n}", [P, 3]) for n in range(2)]
        bhh = [sb(f"w_bhh{n}", [P, 3]) for n in range(2)]
        wm2 = sb("w_wm2", [P, D])
        wm3t = sb("w_wm3t", [P, D])
        wu1b = sb("w_wu1b", [P, D])
        bm3 = sb("w_bm3", [P, 1])
        bu1 = sb("w_bu1", [P, 1])
        wu2t = sb("w_wu2t", [P, D])
        wi1 = sb("w_wi1", [P, D])
        bu2 = sb("w_bu2", [P, 1])
        bi1 = sb("w_bi1", [P, 1])
        wi2 = sb("w_wi2", [P, D])
        rim = sb("w_rim", [P, ROW])
        b2 = sb("w_b2", [P, 1])
        sc = sb("w_sc", [P, 8])
        y = sb("w_y", [P, 1])
        ybc = sb("w_ybc", [P, P])
        offi = sb("w_offi", [RADIAL, 1], I32)
        offf = sb("w_offf", [RADIAL, 1])
        empty = sb("w_empty", [P, ROW])
        nowhere = sb("w_nowhere", [P, NPAD // P], I32)
        pw = ctx.enter_context(nc.psum_tensor("w_pw", [P, 8, 512], F32))

        loaded = g.sem("w_loaded")
        made = g.sem("w_made")
        norm2 = g.sem("w_norm2")
        root = g.sem("w_root")
        tanh = g.sem("w_tanh")
        yready = g.sem("w_yready")
        folded = g.sem("w_folded")
        ch = g.sem("w_chain")
        chp = g.sem("w_chain_pool")
        zeroed = g.sem("w_zeroed")
        zrow = g.sem("w_zrow")
        done = g.sem("w_done")

        loads = [
            (g.w0aug[:, 0:D], ins["w0t"]), (w0[:, :], ins["w0"]), (attm[:, :], ins["attm"]),
            (linb[:, :], ins["lin_bias"]), (g.w1aug[:, 0:D], ins["w1"]), (w1t[:, :], ins["w1t"]),
            (att1[:, :], ins["att1"]), (g.projw[:, :], ins["projwt"]), (g.projb[:, :], ins["projb"]),
            (g.wih[0][:, :], ins["wiht"][0]), (g.wih[1][:, :], ins["wiht"][1]),
            (g.whh[0][:, :], ins["whht"][0]), (g.whh[1][:, :], ins["whht"][1]),
            (bih[0][:, :], ins["biht"][0]), (bih[1][:, :], ins["biht"][1]),
            (bhh[0][:, :], ins["bhht"][0]), (bhh[1][:, :], ins["bhht"][1]),
            (g.outw[:, :], ins["outwt"]), (g.wm1[:, 0:D], ins["wm1"][0:D]),
            (g.wm1[:, D:2 * D], ins["wm1"][D:2 * D]), (g.wr[:, :], ins["wm1"][2 * D:2 * D + RADIAL]),
            (wm2[:, :], ins["wm2"]), (wm3t[:, :], ins["wm3t"]), (g.wu1a[:, :], ins["wu1"][0:D]),
            (wu1b[:, :], ins["wu1"][D:2 * D]), (bm3[:, :], ins["bm3"]), (bu1[:, :], ins["bu1"]),
            (wu2t[:, :], ins["wu2t"]), (wi1[:, :], ins["wi1"]), (bu2[:, :], ins["bu2"]),
            (bi1[:, :], ins["bi1"]), (wi2[:, :], ins["wi2"]),
        ]
        for tile, name in ((g.bias0, "conv_bias"), (g.bias1, "bias1"), (g.outb, "out_b"),
                           (g.bi2, "bi2"), (g.bab[:, 1, :], "bm1"), (g.bm2, "bm2")):
            loads.append((tile if name == "bm1" else tile[:, :], ins[name].to_broadcast([P, D])))

        with nc.Block() as block:
            @block.sync
            def _(sp):
                for dst, src in loads:
                    sp.dma_start(dst, src).then_inc(loaded, 16)
                sp.wait_ge(loaded, 16 * len(loads))

            @block.gpsimd
            def _(pool):
                own = Own(pool, chp)
                pool.memset(g.ones[:, :], 1.0).then_inc(made, 1)
                pool.memset(g.half[:, :], 0.5).then_inc(made, 1)
                pool.memset(g.mhalf[:, :], -0.5).then_inc(made, 1)
                pool.iota(offi[:, :], pattern=[[0, 1]], base=0, channel_multiplier=1).then_inc(made, 1)
                own.link(pool.memset(g.ident[:, :], 0.0))
                pool.affine_select(out=g.ident[:, :], in_=g.ident[:, :], compare_op=ALU.not_equal,
                                   fill=1.0, base=0, pattern=[[-1, P]], channel_multiplier=1).then_inc(made, 1)
                pool.wait_ge(norm2, 2)
                pool.wait_ge(made, 5)
                pool.tensor_tensor(sc[:, 1:2], sc[:, 0:1], g.half[:, 0:1], ALU.pow).then_inc(root, 1)

            @block.scalar
            def _(act):
                act.wait_ge(zrow, 1)
                act.dma_start(g.states[EMPTY:EMPTY + P, :], empty[:, :]).then_inc(zeroed, 16)
                act.dma_start(g.sums[EMPTY:EMPTY + P, :], empty[:, 0:D]).then_inc(zeroed, 16)
                act.dma_start(g.place.rearrange("(p n) o -> p (n o)", p=P), nowhere[:, :]).then_inc(zeroed, 16)
                act.wait_ge(root, 1)
                nc.scalar.activation(sc[:, 2:3], sc[:, 1:2], ACT.Tanh).then_inc(tanh, 1)
                act.wait_ge(zeroed, 16 * 3)

            @block.tensor
            def _(pe):
                pe.wait_ge(ch, 1)
                pe.wait_ge(made, 5)
                nc.tensor.matmul(pw[:, 0, 0:1], g.ones[:, :], b2[:, :], start=True, stop=True).then_inc(norm2, 1)
                pe.wait_ge(loaded, 16 * len(loads))
                mm = nc.tensor.matmul
                mm(pw[:, 1, 0:8], w0[:, :], attm[:, :], start=True, stop=True)
                mm(pw[:, 2, 0:2], w1t[:, :], att1[:, :], start=True, stop=True)
                mm(pw[:, 3, 0:D], wm3t[:, :], wu1b[:, :], start=True, stop=True)
                mm(pw[0:1, 4, 0:D], bm3[:, :], wu1b[:, :], start=True, stop=True)
                mm(pw[:, 5, 0:D], wu2t[:, :], wi1[:, :], start=True, stop=True)
                mm(pw[:, 6, 0:1], wi1[:, :], bu2[:, :], start=True, stop=True).then_inc(folded, 1)
                pe.wait_ge(yready, 1)
                mm(pw[:, 7, 0:1], w0[:, :], y[:, :], start=True, stop=True).then_inc(folded, 1)
                mm(pw[:, 0, 0:ROW], ybc[:, :], rim[:, :], start=True, stop=True)
                mm(pw[:, 0, 256:257], ybc[:, :], y[:, :], start=True, stop=True).then_inc(folded, 1)

            @block.vector
            def _(v):
                own = Own(v, ch)
                v.wait_ge(loaded, 16 * len(loads))
                own.mark(nc.vector.tensor_tensor(b2[:, :], linb[:, :], linb[:, :], ALU.mult))
                nc.vector.memset(nowhere[:, :], EMPTY)
                nc.vector.memset(empty[:, 0:MAXC], 0.0)
                nc.vector.memset(empty[:, MAXC:ROW], LOWEST).then_inc(zrow, 1)
                v.wait_ge(made, 5)
                own.mark(nc.vector.tensor_copy(offf[:, :], offi[:, :]))
                own.mark(nc.vector.tensor_copy(rim[:, 0:D], g.ident[:, :]))
                own.mark(nc.vector.tensor_copy(rim[:, D:ROW], attm[:, :]))
                own.wait()
                own.mark(nc.vector.tensor_scalar(g.noff[:, :], offf[:, :], -CUTOFF / (RADIAL - 1), None, ALU.mult))
                for n in range(2):
                    own.link(nc.vector.tensor_tensor(sc[:, 3:5], bih[n][:, 0:2], bhh[n][:, 0:2], ALU.add))
                    own.mark(nc.vector.tensor_scalar(g.gb[n][:, 0:2], sc[:, 3:5], 0.5, None, ALU.mult))
                    own.mark(nc.vector.tensor_copy(g.gb[n][:, 2:3], bih[n][:, 2:3]))
                    own.mark(nc.vector.tensor_copy(g.gb[n][:, 3:4], bhh[n][:, 2:3]))
                    own.wait()
                own.mark(nc.vector.tensor_scalar(g.wm2[:, :], wm2[:, :], 0.5, None, ALU.mult))
                own.mark(nc.vector.tensor_scalar(g.wi2[:, :], wi2[:, :], 0.5, None, ALU.mult))
                own.mark(nc.vector.tensor_copy(g.bu1[:, 0:1], bu1[:, :]))
                own.mark(nc.vector.tensor_scalar(g.bu1[:, 1:2], bu1[:, :], 0.5, None, ALU.mult))
                own.mark(nc.vector.memset(g.bc[:, :], 0.0))
                own.mark(nc.vector.memset(g.bab[:, 0, :], 0.0))
                own.wait()
                v.wait_ge(norm2, 1)
                nc.vector.tensor_scalar(sc[:, 0:1], pw[:, 0, 0:1], MIN_NORM ** 2, None, ALU.max).then_inc(norm2, 1)
                v.wait_ge(folded, 1)
                own.mark(nc.vector.tensor_copy(g.w0aug[:, D:ROW], pw[:, 1, 0:8]))
                own.mark(nc.vector.tensor_copy(g.w1aug[:, D:D + 2], pw[:, 2, 0:2]))
                own.mark(nc.vector.tensor_scalar(g.wc[:, :], pw[:, 3, 0:D], 0.5, None, ALU.mult))
                own.mark(nc.vector.tensor_copy(g.bc[0:1, :], pw[0:1, 4, 0:D]))
                own.mark(nc.vector.tensor_scalar(g.wd[:, :], pw[:, 5, 0:D], 0.5, None, ALU.mult))
                own.link(nc.vector.tensor_tensor(g.bd[:, 0:1], pw[:, 6, 0:1], bi1[:, :], ALU.add))
                own.mark(nc.vector.tensor_scalar(g.bd[:, 1:2], g.bd[:, 0:1], 0.5, None, ALU.mult))
                v.wait_ge(tanh, 1)
                own.mark(nc.vector.tensor_scalar(sc[:, 5:6], sc[:, 2:3], MAX_NORM, None, ALU.min))
                own.link(nc.vector.reciprocal(sc[:, 6:7], sc[:, 1:2]))
                own.link(nc.vector.tensor_tensor(sc[:, 7:8], sc[:, 5:6], sc[:, 6:7], ALU.mult))
                own.link(nc.vector.tensor_tensor(y[:, :], sc[:, 7:8], linb[:, :], ALU.mult))
                nc.vector.tensor_scalar(ybc[:, :], g.ones[:, :], y[:, 0:1], None, ALU.mult).then_inc(yready, 1)
                v.wait_ge(folded, 3)
                own.mark(nc.vector.tensor_copy(g.w0aug[:, ROW:ROW + 1], pw[:, 7, 0:1]))
                own.mark(nc.vector.tensor_copy(g.yrow[:, :], pw[:, 0, 0:ROW]))
                own.mark(nc.vector.tensor_copy(g.y2[:, :], pw[:, 0, 256:257]))
                own.wait()



def sort_edges(g, flag, src_i, dst_i, typ_i, dist, next_i):
    nc = g.nc
    digits = 256
    assert NPAD < digits * digits
    with ExitStack() as ctx:
        def sb(name, shape, dt=F32):
            return ctx.enter_context(nc.sbuf_tensor("o_" + name, shape, dt))

        rec = sb("rec", [P, KE, 4], I32)
        digit_i = sb("digit_i", [P, KE], I32)
        digit = sb("digit", [P, KE])
        ramp = sb("ramp", [P, digits])
        tri = sb("tri", [P, P])
        hot = sb("hot", [P, digits])
        seen = sb("seen", [P, digits])
        base = sb("base", [P, digits])
        upto = sb("upto", [P, digits])
        place = sb("place", [P, 1])
        place_i = sb("place_i", [P, 1], I32)
        moved = sb("moved", [P, 4], I32)
        pc = ctx.enter_context(nc.psum_tensor("o_pc", [P, 512], F32))
        pr = ctx.enter_context(nc.psum_tensor("o_pr", [P, 512], F32))
        ramped = g.sem("o_ramped")
        ch = g.sem("o_chain")
        hotch = [g.sem(f"o_count_chain{n}") for n in range(2)]
        placech = [g.sem(f"o_place_chain{n}") for n in range(2)]
        gate = g.sem("o_gate")
        gatev = g.sem("o_gatev")
        counted = g.sem("o_counted")
        totalled = g.sem("o_totalled")
        hotted = [g.sem(f"o_hotted{n}") for n in range(2)]
        ranked = [g.sem(f"o_ranked{n}") for n in range(2)]
        placed = [g.sem(f"o_placed{n}") for n in range(2)]
        put = [g.indirect_sem(f"o_put{n}") for n in range(2)]
        room = [g.sem(f"o_room{n}") for n in range(2)]
        loaded = g.sem("o_loaded")
        with nc.Block() as block:
            @block.gpsimd
            def _(pool):
                with pool.If(pool.value_load(flag[0:1, 0:1], min_val=0, max_val=1)):
                    own = Own(pool, ramped)
                    own.mark(pool.iota(ramp[:, :], pattern=[[1, digits]], base=0, channel_multiplier=0,
                                       allow_small_or_imprecise_dtypes=True))
                    own.link(pool.memset(tri[:, :], 1.0))
                    own.mark(pool.affine_select(out=tri[:, :], in_=tri[:, :], compare_op=ALU.is_gt, fill=0.0, base=0,
                                                pattern=[[1, P]], channel_multiplier=-1))
                    for n in range(2):
                        pool.sem_inc(room[n], 1)
                        with pool.Fori(0, KE) as j:
                            gated(pool, placed[n], j + 1, gate)
                            pool.indirect_dma_start(
                                out=g.records[n], out_offset=bass.IndirectOffsetOnAxis(ap=place_i[:, 0:1], axis=0),
                                in_=moved[:, :], in_offset=None, bounds_check=NPAD - 1, oob_is_err=False
                            ).then_inc(put[n], 16)
                            gated(pool, put[n], j * 16 + 16, room[n])

            @block.sync
            def _(sp):
                with sp.If(sp.value_load(flag[0:1, 0:1], min_val=0, max_val=1)):
                    sp.wait_ge(room[0], KE + 1)
                    parts = 8
                    step = KE // parts
                    by = g.records[0].rearrange("(j p) c -> p j c", p=P)
                    for a in range(parts):
                        sp.dma_start(rec[:, a * step:(a + 1) * step, :],
                                     by[:, a * step:(a + 1) * step, :]).then_inc(loaded, 16)
                    sp.wait_ge(room[1], KE + 1)
                    sp.dma_start(rec[:, :, :], g.records[1].rearrange("(p k) c -> p k c", p=P)).then_inc(loaded, 16)
                    with nc.allow_non_contiguous_dma(reason="one word of each partition"):
                        sp.dma_start(next_i[0:P - 1, :], g.records[1].rearrange("(p k) c -> p k c", p=P)[1:P, 0, 1:2]
                                     ).then_inc(loaded, 16)

            @block.tensor
            def _(pe):
                with pe.If(pe.value_load(flag[0:1, 0:1], min_val=0, max_val=1)):
                    pe.wait_ge(ramped, 3)
                    for n in range(2):
                        pe.wait_ge(counted, n + 1)
                        nc.tensor.matmul(pc[:, 0:digits], g.ones[:, :], seen[:, :], start=True,
                                         stop=True).then_inc(totalled, 1)
                        with pe.Fori(0, KE) as j:
                            pe.wait_ge(hotted[n], j + 1)
                            nc.tensor.matmul(pr[:, 0:digits], tri[:, :], hot[:, :], start=True, stop=True)
                            nc.tensor.matmul(pc[:, 0:digits], g.ones[:, :], hot[:, :], start=True,
                                             stop=True).then_inc(ranked[n], 1)

            @block.vector
            def _(v):
                with v.If(v.value_load(flag[0:1, 0:1], min_val=0, max_val=1)):
                    own = Own(v, ch)
                    own.mark(nc.vector.tensor_copy(rec[:, :, 0], src_i[:, :]))
                    own.mark(nc.vector.tensor_copy(rec[:, :, 1], dst_i[:, :]))
                    own.mark(nc.vector.tensor_copy(rec[:, :, 2], typ_i[:, :]))
                    own.link(nc.vector.tensor_copy(rec[:, :, 3], dist[:, :].bitcast(I32)))
                    v.wait_ge(ramped, 3)
                    for n in range(2):
                        if n:
                            v.wait_ge(loaded, 16 * 8)
                            own.link(nc.vector.tensor_single_scalar(digit_i[:, :], rec[:, :, 1], 8,
                                                                    op=ALU.logical_shift_right))
                        else:
                            own.link(nc.vector.tensor_single_scalar(digit_i[:, :], rec[:, :, 1], digits - 1,
                                                                    op=ALU.bitwise_and))
                        own.mark(nc.vector.tensor_copy(digit[:, :], digit_i[:, :]))
                        own.link(nc.vector.memset(seen[:, :], 0.0))
                        with v.Fori(0, KE) as j:
                            o = Own(v, hotch[n], j, 1)
                            o.mark(nc.vector.scalar_tensor_tensor(seen[:, :], ramp[:, :], digit[:, bass.ds(j, 1)],
                                                                  seen[:, :], ALU.is_equal, ALU.add))
                            o.wait()
                            o.end()
                        v.sem_inc(counted, 1)
                        v.wait_ge(totalled, n + 1)
                        own.link(nc.vector.tensor_copy(seen[:, :], pc[:, 0:digits]))
                        own.link(nc.vector.tensor_tensor_scan(upto[:, :], g.ones[:, 0:1].to_broadcast([P, digits]),
                                                              seen[:, :], 0.0, ALU.mult, ALU.add))
                        own.link(nc.vector.tensor_tensor(base[:, :], upto[:, :], seen[:, :], ALU.subtract))
                        with v.Fori(0, KE) as j:
                            o = Own(v, placech[n], j, 6)
                            o.mark(nc.vector.tensor_scalar(hot[:, :], ramp[:, :], digit[:, bass.ds(j, 1)], None,
                                                           ALU.is_equal))
                            o.wait()
                            v.sem_inc(hotted[n], 1)
                            v.wait_ge(ranked[n], j + 1)
                            o.link(nc.vector.tensor_tensor(upto[:, :], pr[:, 0:digits], base[:, :], ALU.add))
                            o.link(nc.vector.tensor_tensor(upto[:, :], upto[:, :], hot[:, :], ALU.mult))
                            o.mark(nc.vector.tensor_tensor(base[:, :], base[:, :], pc[:, 0:digits], ALU.add))
                            o.link(nc.vector.tensor_reduce(place[:, :], upto[:, :], AX_X, ALU.add))
                            gated(v, room[n], j + 1, gatev)
                            o.mark(nc.vector.tensor_copy(place_i[:, :], place[:, :]))
                            nc.vector.tensor_copy(moved[:, :].unsqueeze(1), rec[:, bass.ds(j, 1), :]).then_inc(placed[n], 1)
                            v.wait_ge(placed[n], j + 1)
                            o.end()
                    v.wait_ge(loaded, 16 * 10)
                    own.mark(nc.vector.tensor_copy(src_i[:, :], rec[:, :, 0]))
                    own.mark(nc.vector.tensor_copy(dst_i[:, :], rec[:, :, 1]))
                    own.mark(nc.vector.tensor_copy(typ_i[:, :], rec[:, :, 2]))
                    own.link(nc.vector.tensor_copy(dist[:, :].bitcast(I32), rec[:, :, 3]))


def phase_edges(g):
    nc, ins = g.nc, g.ins
    with ExitStack() as ctx:
        def sb(name, shape, dt=F32):
            return ctx.enter_context(nc.sbuf_tensor(name, shape, dt))

        src_i = sb("e_src", [P, KE], I32)
        dst_i = sb("e_dst", [P, KE], I32)
        typ_i = sb("e_typ", [P, KE], I32)
        next_i = sb("e_nexti", [P, 1], I32)
        dist = sb("e_dist", [P, KE])
        dst = sb("e_dstf", [P, KE + 1])
        typ = sb("e_typf", [P, KE])
        same = sb("e_same", [P, KE])
        fac = sb("e_fac", [P, 2, KE])
        sct = sb("e_sct", [P, KE])
        sct_i = sb("e_scti", [P, KE], I32)
        own_row = sb("e_own_row", [P, ECHUNK, KC], I32)
        dg = sb("e_dg", [P, P])
        firstb = sb("e_firstb", [P, P])
        tri = sb("e_tri", [P, P])
        rowsb = sb("e_rows", [KE // 4, 2, 4, P])
        pt = ctx.enter_context(nc.psum_tensor("e_pt", [P, 4, 512], F32))
        loaded = g.sem("e_loaded")
        pre = g.sem("e_pre")
        cast = g.sem("e_cast")
        trid = g.sem("e_trid")
        numbered = g.sem("e_numbered")
        turned = g.sem("e_turned")
        ch = g.sem("e_chain")
        ready = g.sem("e_ready")
        stored = g.sem("e_stored")
        flag = sb("e_flag", [1, 1], I32)
        disorder = sb("e_disorder", [P, 2])
        read = g.sem("e_read")
        compared = g.sem("e_compared")
        summed = g.sem("e_summed")
        och = g.sem("e_order_chain")
        K4 = KE // 4
        with nc.Block() as block:
            @block.sync
            def _(sp):
                sp.dma_start(src_i[:, :], ins["src"]).then_inc(loaded, 16)
                sp.dma_start(dst_i[:, :], ins["dst"]).then_inc(loaded, 16)
                sp.dma_start(typ_i[:, :], ins["etype"]).then_inc(loaded, 16)
                sp.dma_start(dist[:, :], ins["dist"]).then_inc(loaded, 16)
                sp.wait_ge(pre, 1)
                with nc.allow_non_contiguous_dma(reason="one word of each partition"):
                    sp.dma_start(next_i[0:P - 1, :], ins["dst"][1:P, 0:1]).then_inc(loaded, 16)

            @block.vector
            def _(v):
                own = Own(v, och)
                nc.vector.memset(next_i[:, :], NPAD).then_inc(pre, 1)
                v.wait_ge(loaded, 16 * 5)
                own.mark(nc.vector.tensor_copy(dst[:, 0:KE], dst_i[:, :]))
                own.link(nc.vector.tensor_copy(dst[:, KE:KE + 1], next_i[:, :]))
                own.link(nc.vector.tensor_tensor(same[:, :], dst[:, 0:KE], dst[:, 1:KE + 1], ALU.is_gt))
                nc.vector.tensor_reduce(disorder[:, 0:1], same[:, :], AX_X, ALU.add).then_inc(compared, 1)
                v.wait_ge(summed, 1)
                own.link(nc.vector.tensor_scalar(disorder[0:1, 1:2], pt[0:1, 0, 0:1], 0.0, None, ALU.is_gt))
                own.link(nc.vector.tensor_copy(flag[:, :], disorder[0:1, 1:2]))

            @block.tensor
            def _(pe):
                pe.wait_ge(compared, 1)
                nc.tensor.matmul(pt[0:1, 0, 0:1], g.ones[:, 0:1], disorder[:, 0:1], start=True,
                                 stop=True).then_inc(summed, 1)

        sort_edges(g, flag, src_i, dst_i, typ_i, dist, next_i)

        with nc.Block() as block:
            @block.sync
            def _(sp):
                sp.wait_ge(ready, 2)
                sp.wait_ge(numbered, 1)
                for table, n, values in ((g.edge_idx, 0, src_i[:, :]), (g.edge_idx, 1, dst_i[:, :]),
                                         (g.place_idx, 0, sct_i[:, :]),
                                         (g.place_idx, 1, own_row[:, :, :].rearrange("p c k -> p (c k)")),
                                         (g.edge_fac, 0, fac[:, 0, :]), (g.edge_fac, 1, fac[:, 1, :])):
                    sp.dma_start(table[:, :, n, :].rearrange("c p k -> p c k"),
                                 values.rearrange("p (c k) -> p c k", k=KC)).then_inc(stored, 16)
                sp.wait_ge(ready, 3)
                for n, t in enumerate((g.type_rows, g.dist_rows)):
                    sp.dma_start(t.rearrange("(a k) p -> k a p", a=4), rowsb[:, n, :, :]).then_inc(stored, 16)
                sp.wait_ge(stored, 16 * (6 + 2))

            @block.gpsimd
            def _(pool):
                own = Own(pool, cast)
                pool.iota(own_row[:, :, :], pattern=[[P * KC, ECHUNK], [1, KC]], base=0,
                          channel_multiplier=KC).then_inc(numbered, 1)
                own.link(pool.memset(tri[:, :], 1.0))
                pool.affine_select(out=tri[:, :], in_=tri[:, :], compare_op=ALU.is_gt, fill=0.0, base=0,
                                   pattern=[[1, P]], channel_multiplier=-1).then_inc(trid, 1)

            @block.tensor
            def _(pe):
                pe.wait_ge(ready, 1)
                for n, t in enumerate((typ, dist)):
                    for a in range(4):
                        last = nc.tensor.transpose(pt[0:K4, n, a * P:(a + 1) * P], t[:, a * K4:(a + 1) * K4],
                                                   g.ident[:, :])
                last.then_inc(turned, 1)
                nc.tensor.matmul(pt[:, 2, 0:P], g.ones[:, :], dg[:, :], start=True, stop=True).then_inc(turned, 1)
                pe.wait_ge(ready, 4)
                nc.tensor.transpose(pt[:, 3, 0:P], g.cross[:, :], g.ident[:, :]).then_inc(turned, 1)

            @block.vector
            def _(v):
                own = Own(v, ch)
                own.mark(nc.vector.tensor_copy(typ[:, :], typ_i[:, :]))
                own.mark(nc.vector.tensor_copy(dst[:, 0:KE], dst_i[:, :]))
                own.mark(nc.vector.tensor_copy(dst[:, KE:KE + 1], next_i[:, :]))
                own.mark(nc.vector.tensor_copy(g.first_i[:, :], dst_i[:, 0:1]))
                own.wait()
                nc.vector.tensor_scalar(dg[:, :], g.ident[:, :], dst[:, 0:1], None, ALU.mult).then_inc(ready, 1)
                own.link(nc.vector.tensor_tensor(same[:, :], dst[:, 0:KE], dst[:, 1:KE + 1], ALU.is_equal))
                own.link(nc.vector.scalar_tensor_tensor(sct[:, :], same[:, :], float(SKIP), dst[:, 0:KE],
                                                        ALU.mult, ALU.add))
                own.mark(nc.vector.tensor_copy(sct_i[:, :], sct[:, :]))
                own.mark(nc.vector.memset(fac[:, 0, 0:1], 0.0))
                own.link(nc.vector.tensor_copy(fac[:, 0, 1:KE], same[:, 0:KE - 1]))
                nc.vector.tensor_scalar(fac[:, 1, :], fac[:, 0, :], -LOWEST, LOWEST, ALU.mult,
                                        ALU.add).then_inc(ready, 1)
                v.wait_ge(turned, 1)
                own.mark(nc.vector.tensor_copy(rowsb[:, 0, :, :], pt[0:K4, 0, :].rearrange("k (a p) -> k a p", a=4)))
                nc.vector.tensor_copy(rowsb[:, 1, :, :],
                                      pt[0:K4, 1, :].rearrange("k (a p) -> k a p", a=4)).then_inc(ready, 1)
                v.wait_ge(turned, 2)
                v.wait_ge(trid, 1)
                own.link(nc.vector.tensor_copy(firstb[:, :], pt[:, 2, 0:P]))
                nc.vector.scalar_tensor_tensor(g.cross[:, :], firstb[:, :], dst[:, KE - 1:KE], tri[:, :],
                                               ALU.is_equal, ALU.mult).then_inc(ready, 1)
                v.wait_ge(turned, 3)
                own.link(nc.vector.tensor_copy(g.cross_t[:, :], pt[:, 3, 0:P]))
                own.mark(nc.vector.tensor_scalar(g.low_t[:, :], g.cross_t[:, :], -LOWEST, LOWEST, ALU.mult, ALU.add))
                own.link(nc.vector.tensor_tensor(g.goes_on[:, :], dst[:, 0:1], dst[:, KE:KE + 1], ALU.is_equal))



def place_list(g, sp, i, b, plist, plisted, used):
    if b % B == 0:
        h = b // B
        sp.wait_ge(used, i * 2 + (h + 1))
        sp.dma_start(plist[h][:, :, :], g.place_idx[bass.ds(i * 2 + h + g.placed_lists, 1)].rearrange(
            "c p n k -> (c p) n k")).then_inc(plisted[h], 16)


def place_edges(g, pool, i, b, plist, plisted, placed, used, gate):
    h, part = divmod(b, B)
    if part == 0:
        gated(pool, plisted[h], i * 16 + 16, gate)
    for k in range(part * (KC // B), (part + 1) * (KC // B)):
        pool.indirect_dma_start(
            out=g.place, out_offset=bass.IndirectOffsetOnAxis(ap=plist[h][:, 0, k:k + 1], axis=0),
            in_=plist[h][:, 1, k:k + 1], in_offset=None, bounds_check=NPAD - 1, oob_is_err=False
        ).then_inc(placed[h], 16)
    if part == B - 1:
        gated(pool, placed[h], i * (16 * KC) + 16 * KC, used)


def phase_product(g):
    nc = g.nc
    with ExitStack() as ctx:
        def sb(name, shape, dt=F32):
            return ctx.enter_context(nc.sbuf_tensor(name, shape, dt))

        x = [sb(f"p_x{b}", [P, Q, D]) for b in range(B)]
        xt = [sb(f"p_xt{b}", [P, CHUNK]) for b in range(B)]
        mx = [sb(f"p_mx{b}", [P, Q, ROW]) for b in range(B)]
        x2 = [sb(f"p_x2{b}", [P, Q, D]) for b in range(B)]
        m2 = [sb(f"p_m2{b}", [P, Q, D]) for b in range(B)]
        pt = [ctx.enter_context(nc.psum_tensor(f"p_pt{b}", [P, 512], F32)) for b in range(R)]
        pm = [ctx.enter_context(nc.psum_tensor(f"p_pm{b}", [P, 2, 512], F32)) for b in range(R)]
        loaded = [g.sem(f"p_loaded{b}") for b in range(B)]
        turned = g.sem("p_turned")
        copied = g.sem("p_copied")
        product = g.sem("p_product")
        squared = g.sem("p_squared")
        moved = g.sem("p_moved")
        summed = g.sem("p_summed")
        stored = [g.sem(f"p_stored{b}") for b in range(B)]
        freed = g.sem("p_freed")
        gate = g.sem("p_gate")
        plist = [sb(f"p_plist{h}", [P, 2, KC], I32) for h in range(2)]
        plisted = [g.sem(f"p_plisted{h}") for h in range(2)]
        placed = [g.indirect_sem(f"p_placed{h}") for h in range(2)]
        used = g.sem("p_used")
        pgate = g.sem("p_pgate")
        passes = NCHUNK // G
        g.placed_lists = 0 * (ECHUNK // 2)
        with nc.Block() as block:
            @block.sync
            def _(sp):
                with sp.Fori(0, passes) as i:
                    for b in range(G):
                        sp.wait_ge(summed, nth_node(i, b))
                        sp.dma_start(x[b % B][:, :, :], rows(g.ins["x"], i * G + b)).then_inc(loaded[b % B], 16)
                        place_list(g, sp, i, b, plist, plisted, used)

            @block.gpsimd
            def _(pool):
                pool.sem_inc(used, 2)
                for i, part in laps(pool):
                    for t in steps(part, 5):
                        for b in step(part, t, 5):
                            gated(pool, stored[b % B], turn(i, b) * 16, freed)
                        for b in step(part, t, 0):
                            place_edges(g, pool, i, b, plist, plisted, placed, used, pgate)

            @block.tensor
            def _(pe):
                for i, part in laps(pe):
                    for t in steps(part, 1):
                        for b in step(part, t, 1):
                            pe.wait_ge(copied, nth_node(i, b) + R)
                            pe.wait_ge(moved, nth_node(i, b))
                            for q in range(Q):
                                o = (q % 2) * (ROW + 1)
                                last = nc.tensor.matmul(pm[b % R][:, q // 2, o:o + ROW + 1], xt[b % B][:, q * P:(q + 1) * P],
                                                        g.w0aug[:, :], start=True, stop=True)
                            last.then_inc(product, 1)
                        for b in step(part, t, 0):
                            pe.wait_ge(loaded[b % B], turn(i, b) * 16)
                            pe.wait_ge(copied, nth_node(i, b))
                            for q in range(Q):
                                last = nc.tensor.transpose(pt[b % R][:, q * P:(q + 1) * P], x[b % B][:, q, :], g.ident[:, :])
                            last.then_inc(turned, 1)

            @block.scalar
            def _(act):
                act.sem_inc(copied, R)
                for i, part in laps(act):
                    for t in steps(part, 2):
                        for b in step(part, t, 2):
                            act.wait_ge(summed, nth_node(i, b))
                            act.wait_ge(loaded[b % B], turn(i, b) * 16)
                            nc.scalar.activation(x2[b % B][:, :, :], x[b % B][:, :, :], ACT.Square)
                            act.wait_ge(moved, nth_node(i, b) + R)
                            nc.scalar.activation(m2[b % B][:, :, :], mx[b % B][:, :, 0:D], ACT.Square).then_inc(squared, 1)
                            act.dma_start(rows(g.mx, i * G + b), mx[b % B][:, :, :]).then_inc(stored[b % B], 16)
                        for b in step(part, t, 0):
                            act.wait_ge(turned, nth_node(i, b))
                            act.wait_ge(freed, nth_node(i, b))
                            nc.scalar.copy(xt[b % B][:, :], pt[b % R][:, :]).then_inc(copied, 1)

            @block.vector
            def _(v):
                v.sem_inc(summed, B)
                v.sem_inc(moved, R)
                v.sem_inc(freed, B)
                for i, part in laps(v):
                    for t in steps(part, 3):
                        for b in step(part, t, 3):
                            col = bass.ds(i * (G * Q) + b * Q, Q)
                            v.wait_ge(squared, nth_node(i, b))
                            v.sem_inc(gate, 1)
                            nc.vector.tensor_reduce(g.sxx[:, col], x2[b % B][:, :, :], AX_X, ALU.add)
                            nc.vector.tensor_reduce(g.smm[:, col], m2[b % B][:, :, :], AX_X, ALU.add).then_inc(summed, 1)
                        for b in step(part, t, 1):
                            col = bass.ds(i * (G * Q) + b * Q, Q)
                            v.wait_ge(product, nth_node(i, b))
                            v.wait_ge(freed, nth_node(i, b))
                            view = pm[b % R][:, :, 0:2 * (ROW + 1)].rearrange("p a (s c) -> p a s c", s=2)
                            v.tensor_scalar(g.sxy[:, col].rearrange("p (a s) -> p a s", s=2), view[:, :, :, ROW],
                                            1.0, None, ALU.mult)
                            nc.vector.tensor_copy(mx[b % B][:, :, :].rearrange("p (a s) c -> p a s c", s=2),
                                                  view[:, :, :, 0:ROW]).then_inc(moved, 1)



def phase_map(g):
    nc = g.nc
    with ExitStack() as ctx:
        t = [ctx.enter_context(nc.sbuf_tensor(f"m_t{n}", [P, COLS], F32)) for n in range(14)]
        asked = g.sem("m_asked")
        rooted = g.sem("m_rooted")
        logged = g.sem("m_logged")
        tanhed = g.sem("m_tanhed")
        ch = g.sem("m_chain")
        tanh_asked = g.sem("m_tanh_asked")
        log_asked = g.sem("m_log_asked")
        xn, mn, n2, ratio, lg = t[0], t[1], t[2], t[3], t[4]
        xsq = t[11]
        with nc.Block() as block:
            @block.scalar
            def _(act):
                act.wait_ge(asked, 2)
                nc.scalar.activation(xn[:, :], t[6][:, :], ACT.Sqrt)
                nc.scalar.activation(mn[:, :], t[7][:, :], ACT.Sqrt).then_inc(rooted, 1)
                act.wait_ge(log_asked, 1)
                nc.scalar.activation(lg[:, :], ratio[:, :], ACT.Ln).then_inc(logged, 1)
                act.wait_ge(tanh_asked, 1)
                nc.scalar.activation(t[5][:, :], t[5][:, :], ACT.Tanh).then_inc(tanhed, 1)
                act.wait_ge(asked, 3)
                nc.scalar.activation(n2[:, :], xsq[:, :], ACT.Sqrt).then_inc(rooted, 1)
                act.wait_ge(log_asked, 2)
                nc.scalar.activation(lg[:, :], ratio[:, :], ACT.Ln).then_inc(logged, 1)

            @block.vector
            def _(v):
                own = Own(v, ch)

                def tt(o, a, b, op):
                    own.link(nc.vector.tensor_tensor(o[:, :], a[:, :], b[:, :], op))

                def ts(o, a, s1, op1, s2=None, op2=ALU.bypass):
                    own.link(nc.vector.tensor_scalar(o[:, :], a[:, :], s1, s2, op1, op2))

                def stt(o, a, s, b, op1, op2):
                    own.link(nc.vector.scalar_tensor_tensor(o[:, :], a[:, :], s, b[:, :], op1, op2))

                def ask(o, a, s1, op1, sem):
                    nc.vector.tensor_scalar(o[:, :], a[:, :], s1, None, op1).then_inc(sem, 1)

                def artanh(o, n, call, a, b, c):
                    ts(a, n, 1.0 - 1e-7, ALU.min)
                    ts(b, a, -1.0, ALU.mult, 1.0, ALU.add)
                    own.link(nc.vector.reciprocal(b[:, :], b[:, :]))
                    stt(ratio, a, 1.0, b, ALU.add, ALU.mult)
                    v.sem_inc(log_asked, 1)
                    tt(b, a, a, ALU.mult)
                    ts(c, b, 1.0 / 15, ALU.mult, 1.0 / 13, ALU.add)
                    for n_ in (11, 9, 7, 5, 3, 1):
                        tt(c, c, b, ALU.mult)
                        ts(c, c, 1.0 / n_, ALU.add)
                    tt(c, c, a, ALU.mult)
                    ts(b, a, 0.3, ALU.is_lt)
                    tt(c, c, b, ALU.mult)
                    ts(b, b, -0.5, ALU.mult, 0.5, ALU.add)
                    v.wait_ge(logged, call)
                    tt(b, b, lg, ALU.mult)
                    tt(o, b, c, ALU.add)

                def newton(r, square, w):
                    own.link(nc.vector.reciprocal(w[:, :], r[:, :]))
                    tt(w, w, square, ALU.mult)
                    tt(w, w, r, ALU.add)
                    ts(r, w, 0.5, ALU.mult)

                ask(t[6], g.sxx, MIN_NORM ** 2, ALU.max, asked)
                ask(t[7], g.smm, MIN_NORM ** 2, ALU.max, asked)
                v.wait_ge(rooted, 1)
                newton(xn, t[6], t[10])
                newton(mn, t[7], t[10])
                arg, rx, rm, c, cm = t[5], t[6], t[7], t[8], t[9]
                artanh(arg, xn, 1, t[10], t[11], t[12])
                own.link(nc.vector.reciprocal(rx[:, :], xn[:, :]))
                own.link(nc.vector.reciprocal(rm[:, :], mn[:, :]))
                tt(rx, rx, mn, ALU.mult)
                tt(arg, arg, rx, ALU.mult)
                v.sem_inc(tanh_asked, 1)
                v.wait_ge(tanhed, 1)
                ts(c, arg, MAX_NORM, ALU.min)
                tt(cm, c, rm, ALU.mult)
                x2, xy2, a, b, den, xy = t[10], t[11], t[12], t[13], t[6], t[7]
                tt(x2, c, c, ALU.mult)
                tt(xy, cm, g.sxy, ALU.mult)
                ts(a, xy, 2.0, ALU.mult, 1.0, ALU.add)
                stt(den, x2, g.y2[:, 0:1], a, ALU.mult, ALU.add)
                ts(den, den, MIN_NORM, ALU.max)
                ts(a, a, g.y2[:, 0:1], ALU.add)
                ts(b, x2, -1.0, ALU.mult, 1.0, ALU.add)
                own.link(nc.vector.reciprocal(den[:, :], den[:, :]))
                tt(a, a, den, ALU.mult)
                tt(b, b, den, ALU.mult)
                tt(xy2, a, xy, ALU.mult)
                ts(xy2, xy2, 2.0, ALU.mult)
                stt(xy2, b, g.y2[:, 0:1], xy2, ALU.mult, ALU.add)
                tt(xy2, xy2, b, ALU.mult)
                tt(x2, x2, a, ALU.mult)
                tt(x2, x2, a, ALU.mult)
                tt(n2, x2, xy2, ALU.add)
                ask(xsq, n2, MIN_NORM ** 2, ALU.max, asked)
                v.wait_ge(rooted, 2)
                newton(n2, xsq, x2)
                tt(cm, cm, a, ALU.mult)
                ts(c, n2, MAX_NORM, ALU.min)
                artanh(rx, c, 2, t[10], t[11], t[12])
                own.link(nc.vector.reciprocal(n2[:, :], n2[:, :]))
                tt(rx, rx, n2, ALU.mult)
                own.mark(nc.vector.tensor_tensor(g.alpha[:, :], rx[:, :], cm[:, :], ALU.mult))
                own.mark(nc.vector.tensor_tensor(g.beta[:, :], rx[:, :], b[:, :], ALU.mult))
                own.wait()


def phase_log(g):
    nc = g.nc
    with ExitStack() as ctx:
        def sb(name, shape, dt=F32):
            return ctx.enter_context(nc.sbuf_tensor(name, shape, dt))

        mx = [sb(f"l_mx{b}", [P, Q, ROW]) for b in range(B)]
        by = [sb(f"l_by{b}", [P, Q, ROW]) for b in range(B)]
        ab = [sb(f"l_ab{b}", [P, 2, Q]) for b in range(B)]
        r = [sb(f"l_r{b}", [P, Q, ROW]) for b in range(B)]
        loaded = [g.sem(f"l_loaded{b}") for b in range(B)]
        factors = g.sem("l_factors")
        scaled = g.sem("l_scaled")
        summed = g.sem("l_summed")
        stored = [g.sem(f"l_stored{b}") for b in range(B)]
        freed = g.sem("l_freed")
        gate = g.sem("l_gate")
        plist = [sb(f"l_plist{h}", [P, 2, KC], I32) for h in range(2)]
        plisted = [g.sem(f"l_plisted{h}") for h in range(2)]
        placed = [g.indirect_sem(f"l_placed{h}") for h in range(2)]
        used = g.sem("l_used")
        pgate = g.sem("l_pgate")
        passes = NCHUNK // G
        g.placed_lists = 1 * (ECHUNK // 2)
        with nc.Block() as block:
            @block.sync
            def _(sp):
                with sp.Fori(0, passes) as i:
                    for b in range(G):
                        sp.wait_ge(summed, nth_node(i, b))
                        sp.dma_start(mx[b % B][:, :, :], rows(g.mx, i * G + b)).then_inc(loaded[b % B], 16)
                        place_list(g, sp, i, b, plist, plisted, used)

            @block.gpsimd
            def _(pool):
                pool.sem_inc(used, 2)
                for i, part in laps(pool):
                    for t in steps(part, 5):
                        for b in step(part, t, 5):
                            gated(pool, stored[b % B], turn(i, b) * 32, freed)
                        for b in step(part, t, 0):
                            place_edges(g, pool, i, b, plist, plisted, placed, used, pgate)

            @block.scalar
            def _(act):
                for i, part in laps(act):
                    for t in steps(part, 3):
                        for b in step(part, t, 3):
                            act.wait_ge(summed, nth_node(i, b) + B)
                            act.dma_start(rows(g.t[0], i * G + b), r[b % B][:, :, 0:TROW]).then_inc(stored[b % B], 16)
                            act.dma_start(rows(g.ai[0], i * G + b), r[b % B][:, :, TROW:ROW]).then_inc(stored[b % B], 16)
                        for b in step(part, t, 0):
                            act.wait_ge(factors, nth_node(i, b))
                            for q in range(Q):
                                last = nc.scalar.activation(by[b % B][:, q, :], g.yrow[:, :], ACT.Copy,
                                                            scale=ab[b % B][:, 1, q:q + 1])
                            last.then_inc(scaled, 1)

            @block.vector
            def _(v):
                v.sem_inc(summed, B)
                v.sem_inc(freed, B)
                for i, part in laps(v):
                    for t in steps(part, 2):
                        for b in step(part, t, 2):
                            v.wait_ge(freed, nth_node(i, b))
                            v.wait_ge(loaded[b % B], turn(i, b) * 16)
                            v.wait_ge(scaled, nth_node(i, b))
                            for q in range(Q):
                                last = nc.vector.scalar_tensor_tensor(r[b % B][:, q, :], mx[b % B][:, q, :], ab[b % B][:, 0, q:q + 1],
                                                                      by[b % B][:, q, :], ALU.mult, ALU.add)
                            last.then_inc(summed, 1)
                        for b in step(part, t, 0):
                            col = bass.ds(i * (G * Q) + b * Q, Q)
                            gated(v, summed, nth_node(i, b), gate)
                            nc.vector.tensor_copy(ab[b % B][:, 0, :], g.alpha[:, col])
                            nc.vector.tensor_copy(ab[b % B][:, 1, :], g.beta[:, col]).then_inc(factors, 1)


def phase_places(g):
    nc = g.nc
    with ExitStack() as ctx:
        row = ctx.enter_context(nc.sbuf_tensor("n_row", [P, 1], F32))
        fix = ctx.enter_context(nc.sbuf_tensor("n_fix", [P, 1], F32))
        loaded = g.sem("n_loaded")
        got = g.indirect_sem("n_got")
        ch = g.sem("n_chain")
        with nc.Block() as block:
            @block.sync
            def _(sp):
                sp.dma_start(g.places[:, 0:NCHUNK * Q].rearrange("p (c q) -> p c q", q=Q),
                             g.place.rearrange("(c p q) o -> p c (q o)", p=P, q=Q)).then_inc(loaded, 16)
                sp.wait_ge(loaded, 16)

            @block.gpsimd
            def _(pool):
                pool.indirect_dma_start(out=g.first_row[:, :], out_offset=None, in_=g.place,
                                        in_offset=bass.IndirectOffsetOnAxis(ap=g.first_i[:, 0:1], axis=0)
                                        ).then_inc(got, 16)

            @block.vector
            def _(v):
                own = Own(v, ch)
                own.mark(nc.vector.memset(g.places[:, NCHUNK * Q:(NCHUNK + B) * Q], EMPTY))
                v.wait_ge(got, 16)
                own.link(nc.vector.tensor_copy(row[:, :], g.first_row[:, :]))
                own.link(nc.vector.scalar_tensor_tensor(fix[:, :], g.goes_on[:, :], float(SKIP), row[:, :],
                                                        ALU.mult, ALU.add))
                own.link(nc.vector.tensor_copy(g.fix_row[:, :], fix[:, :]))


class StateGathers:

    def __init__(self, g, pool, idx, ag, gathered, copied_idx, table):
        self.g, self.pool, self.idx, self.ag, self.gathered, self.table = g, pool, idx, ag, gathered, table
        self.copied_idx = copied_idx
        self.gate = g.sem("gathers_gate")

    def rows(self, i, b, used=None, value=None):
        if used is not None:
            gated(self.pool, used, value, self.copied_idx)
            n = i * (2 * G) + (2 * (b - B) + 2 + B)
        else:
            n = b + 1
        self.pool.tensor_copy(self.idx[b % B][:, :], self.g.places[:, bass.ds(i * (G * Q) + b * Q, Q)]
                              ).then_inc(self.copied_idx, 1)
        if used is None:
            self.pool.wait_ge(self.copied_idx, n)
        else:
            gated(self.pool, self.copied_idx, n, self.gate)

    def gather(self, i, b, q0, q1):
        for q in range(q0, q1):
            self.pool.indirect_dma_start(
                out=self.ag[b % B][:, q, :], out_offset=None, in_=self.table,
                in_offset=bass.IndirectOffsetOnAxis(ap=self.idx[b % B][:, q:q + 1], axis=0)
            ).then_inc(self.gathered[b % B], 16)



def nth(i, b):
    return i * NB + (b + 1)


def edge_streams(g, sp, idx, fac, r, listed, gathered, per_gather, stated, stored, table, more=None):
    passes = ECHUNK // NB
    out = table[0:NPAD].rearrange("(c p k) d -> c p k d", p=P, k=KC)

    def lists(i, b):
        c = bass.ds(i * NB + b, 1)
        sp.dma_start(idx[b][:, :, :], g.edge_idx[c].rearrange("c p n k -> (c p) n k")).then_inc(listed[b], 16)
        sp.dma_start(fac[b][:, :, :], g.edge_fac[c].rearrange("c p n k -> (c p) n k")).then_inc(listed[b], 16)
        if more is not None:
            more(i, b)

    def states(i, b):
        sp.wait_ge(stated, nth(i, b))
        c = bass.ds(i * NB + b, 1)
        sp.dma_start(out[c].rearrange("c p k d -> (c p) k d"), r[b][:, :, :]).then_inc(stored[b], 16)

    for b in range(NB):
        lists(0, b)
    with sp.Fori(0, passes - 1) as i:
        for b in range(NB):
            states(i, b)
            sp.wait_ge(gathered[b], i * (per_gather * KC) + per_gather * KC)
            lists(i + 1, b)
    for b in range(NB):
        states(passes - 1, b)
    for b in range(NB):
        sp.wait_ge(stored[b], 16 * passes)


def with_next(eng):
    with eng.Fori(0, ECHUNK // NB - 1) as i:
        yield i, False
    yield ECHUNK // NB - 1, True


def edge_gathers(g, pool, gathers, listed, per_list, stated, stored, gate):
    for b in range(NB):
        pool.wait_ge(listed[b], per_list)
        if b == NB - 1:
            pool.wait_ge(stated, 1)
        gathers(b)
    with pool.Fori(1, ECHUNK // NB) as i:
        for b in range(NB):
            gated(pool, listed[b], i * per_list + per_list, gate)
            gated(pool, stored[b], i * 16, gate)
            gated(pool, stated, i * NB + (b + 2 - NB), gate)
            gathers(b)


def phase_attend(g, layer, heads):
    nc = g.nc
    dh = D // heads
    pre = f"a{layer}_"
    with ExitStack() as ctx:
        def sb(name, shape, dt=F32):
            return ctx.enter_context(nc.sbuf_tensor(pre + name, shape, dt))

        idx = [sb(f"idx{b}", [P, 2, KC], I32) for b in range(NB)]
        fac = [sb(f"fac{b}", [P, 2, KC]) for b in range(NB)]
        r = [sb(f"r{b}", [P, KC, ROW]) for b in range(NB)]
        ai = [sb(f"ai{b}", [P, KC, HEADS]) for b in range(NB)]
        s = sb("s", [P, heads, KC])
        mx = sb("mx", [P, heads, KC + 1])
        dn = sb("dn", [P, heads, KC + 1])
        e = sb("e", [P, 2, heads, KC])
        tmp = sb("tmp", [P, D])
        listed = [g.sem(pre + f"listed{b}") for b in range(NB)]
        gathered = [g.indirect_sem(pre + f"gathered{b}") for b in range(NB)]
        stored = [g.sem(pre + f"stored{b}") for b in range(NB)]
        asked = g.sem(pre + "asked")
        raised = g.sem(pre + "raised")
        stated = g.sem(pre + "stated")
        cleared = g.sem(pre + "cleared")
        ch = g.sem(pre + "chain")
        gate = g.sem(pre + "gate")
        passes = ECHUNK // NB
        with nc.Block() as block:
            @block.sync
            def _(sp):
                edge_streams(g, sp, idx, fac, r, listed, gathered, 32, stated, stored, g.states)

            @block.gpsimd
            def _(pool):
                pool.wait_ge(cleared, 1)

                def gathers(b):
                    for k in range(KC):
                        pool.indirect_dma_start(
                            out=r[b][:, k, 0:TROW], out_offset=None, in_=g.t[layer],
                            in_offset=bass.IndirectOffsetOnAxis(ap=idx[b][:, 0, k:k + 1], axis=0)
                        ).then_inc(gathered[b], 16)
                        pool.indirect_dma_start(
                            out=ai[b][:, k, :], out_offset=None, in_=g.ai[layer],
                            in_offset=bass.IndirectOffsetOnAxis(ap=idx[b][:, 1, k:k + 1], axis=0)
                        ).then_inc(gathered[b], 16)

                edge_gathers(g, pool, gathers, listed, 32, stated, stored, gate)

            @block.scalar
            def _(act):
                with act.Fori(0, passes) as i:
                    for b in range(NB):
                        act.wait_ge(asked, nth(i, b))
                        nc.scalar.activation(e[:, :, :, :], e[:, :, :, :], ACT.Exp).then_inc(raised, 1)

            @block.vector
            def _(v):
                for b in range(NB):
                    nc.vector.memset(r[b][:, :, :], 0.0)
                nc.vector.memset(dn[:, :, :], 0.0)
                nc.vector.memset(mx[:, :, :], LOWEST).then_inc(cleared, 1)
                v.wait_ge(cleared, 1)
                per = NB * (7 + 2 * heads + (2 if heads > 1 else 1) * KC)
                with v.Fori(0, passes) as i:
                    own = Own(v, ch, i, per)
                    for b in range(NB):
                        v.wait_ge(gathered[b], i * (32 * KC) + 32 * KC)
                        own.link(nc.vector.tensor_tensor(
                            s[:, :, :], r[b][:, :, D:D + heads].rearrange("p k h -> p h k"),
                            ai[b][:, :, 0:heads].rearrange("p k h -> p h k"), ALU.add))
                        own.link(nc.vector.scalar_tensor_tensor(s[:, :, :], s[:, :, :], SLOPE, s[:, :, :],
                                                                ALU.mult, ALU.max))
                        for h in range(heads):
                            own.mark(nc.vector.tensor_tensor_scan(mx[:, h, 1:KC + 1], fac[b][:, 1, :], s[:, h, :],
                                                                  mx[:, h, 0:1], ALU.add, ALU.max))
                        own.wait()
                        own.mark(nc.vector.tensor_tensor(e[:, 1, :, :], s[:, :, :], mx[:, :, 1:KC + 1], ALU.subtract))
                        own.link(nc.vector.tensor_tensor(e[:, 0, :, :], mx[:, :, 0:KC], mx[:, :, 1:KC + 1],
                                                         ALU.subtract))
                        low = fac[b][:, 1:2, :].to_broadcast([P, heads, KC])
                        nc.vector.tensor_tensor(e[:, 0, :, :], e[:, 0, :, :], low, ALU.add).then_inc(asked, 1)
                        v.wait_ge(raised, nth(i, b))
                        for h in range(heads):
                            own.mark(nc.vector.tensor_tensor_scan(dn[:, h, 1:KC + 1], e[:, 0, h, :], e[:, 1, h, :],
                                                                  dn[:, h, 0:1], ALU.mult, ALU.add))
                        w = e[:, 1, :, :].rearrange("p h k -> p k h").unsqueeze(3).to_broadcast([P, KC, heads, dh])
                        rv = r[b][:, :, 0:D].rearrange("p k (h d) -> p k h d", h=heads)
                        own.link(nc.vector.tensor_tensor(rv, rv, w, ALU.mult))
                        for k in range(KC):
                            prev = r[b][:, k - 1, 0:D] if k else r[(b - 1) % NB][:, KC - 1, 0:D]
                            if heads == 1:
                                own.link(nc.vector.scalar_tensor_tensor(
                                    r[b][:, k, 0:D], prev, e[:, 0, 0, k:k + 1], r[b][:, k, 0:D], ALU.mult, ALU.add))
                            else:
                                f = e[:, 0, :, k:k + 1].to_broadcast([P, heads, dh])
                                own.link(nc.vector.tensor_tensor(
                                    tmp[:, :].rearrange("p (h d) -> p h d", h=heads),
                                    prev.rearrange("p (h d) -> p h d", h=heads), f, ALU.mult))
                                own.link(nc.vector.tensor_tensor(r[b][:, k, 0:D], r[b][:, k, 0:D], tmp[:, :],
                                                                 ALU.add))
                        own.mark(nc.vector.tensor_copy(r[b][:, :, DEN:DEN + heads],
                                                       dn[:, :, 1:KC + 1].rearrange("p h k -> p k h")))
                        own.link(nc.vector.tensor_copy(r[b][:, :, MAXC:MAXC + heads],
                                                       mx[:, :, 1:KC + 1].rearrange("p h k -> p k h")))
                        nc.vector.tensor_copy(dn[:, :, 0:1], dn[:, :, KC:KC + 1])
                        nc.vector.tensor_copy(mx[:, :, 0:1], mx[:, :, KC:KC + 1]).then_inc(stated, 1)
                        v.wait_ge(stated, nth(i, b))
                    own.end()
                nc.vector.tensor_copy(g.last[:, :], r[NB - 1][:, KC - 1, :]).then_inc(cleared, 1)
                v.wait_ge(cleared, 2)


def phase_join(g, tag, heads, table, width=ROW):
    nc = g.nc
    pre = f"j{tag}_"
    nh = max(heads, 1)
    sums = min(width, TROW)
    dh = D // nh
    with ExitStack() as ctx:
        def sb(name, shape, dt=F32):
            return ctx.enter_context(nc.sbuf_tensor(pre + name, shape, dt))

        row = sb("row", [P, width])
        new = sb("new", [P, width])
        dgm = sb("dgm", [P, nh, P])
        w = sb("w", [P, nh, P])
        wt = sb("wt", [P, nh, P])
        mc = sb("mc", [P, nh])
        mn = sb("mn", [P, nh])
        e = sb("e", [P, 2, nh])
        t = sb("t", [P, D])
        pa = ctx.enter_context(nc.psum_tensor(pre + "pa", [P, 512], F32))
        pb = ctx.enter_context(nc.psum_tensor(pre + "pb", [P, 512], F32))
        pc = ctx.enter_context(nc.psum_tensor(pre + "pc", [P, 512], F32))
        got = g.indirect_sem(pre + "got")
        put = g.indirect_sem(pre + "put")
        ready = g.sem(pre + "ready")
        spread = g.sem(pre + "spread")
        raised = g.sem(pre + "raised")
        ch = g.sem(pre + "chain")
        with nc.Block() as block:
            @block.gpsimd
            def _(pool):
                pool.indirect_dma_start(out=row[:, :], out_offset=None, in_=table,
                                        in_offset=bass.IndirectOffsetOnAxis(ap=g.first_row[:, 0:1], axis=0)
                                        ).then_inc(got, 16)
                pool.wait_ge(ready, 4 if heads else 1)
                pool.indirect_dma_start(out=table, out_offset=bass.IndirectOffsetOnAxis(ap=g.fix_row[:, 0:1], axis=0),
                                        in_=new[:, :], in_offset=None, bounds_check=NPAD - 1, oob_is_err=False
                                        ).then_inc(put, 16)
                pool.wait_ge(put, 16)

            if not heads:
                @block.tensor
                def _(pe):
                    nc.tensor.matmul(pc[:, 0:sums], g.cross[:, :], g.last[:, 0:sums], start=True,
                                     stop=True).then_inc(spread, 1)

                @block.vector
                def _(v):
                    own = Own(v, ch)
                    v.wait_ge(got, 16)
                    if width > sums:
                        own.mark(nc.vector.tensor_copy(new[:, sums:width], row[:, sums:width]))
                    v.wait_ge(spread, 1)
                    nc.vector.tensor_tensor(new[:, 0:sums], row[:, 0:sums], pc[:, 0:sums], ALU.add).then_inc(ready, 1)
                return

            @block.tensor
            def _(pe):
                pe.wait_ge(ready, 1)
                nc.tensor.matmul(pa[:, 0:nh * P], g.ones[:, :], dgm[:, :, :].rearrange("p h f -> p (h f)"),
                                 start=True, stop=True).then_inc(spread, 1)
                pe.wait_ge(ready, 3)
                for h in range(nh):
                    last = nc.tensor.transpose(pb[:, h * P:(h + 1) * P], w[:, h, :], g.ident[:, :])
                last.then_inc(spread, 1)
                pe.wait_ge(raised, 3)
                for h in range(nh):
                    nc.tensor.matmul(pc[:, h * dh:(h + 1) * dh], wt[:, h, :], g.last[:, h * dh:(h + 1) * dh],
                                     start=True, stop=True)
                    last = nc.tensor.matmul(pc[:, DEN + h:DEN + h + 1], wt[:, h, :], g.last[:, DEN + h:DEN + h + 1],
                                            start=True, stop=True)
                last.then_inc(spread, 1)

            @block.scalar
            def _(act):
                act.wait_ge(ready, 2)
                nc.scalar.activation(w[:, :, :], w[:, :, :], ACT.Exp).then_inc(raised, 1)
                act.wait_ge(raised, 2)
                nc.scalar.activation(e[:, :, :], e[:, :, :], ACT.Exp)
                act.wait_ge(spread, 2)
                nc.scalar.copy(wt[:, :, :].rearrange("p h f -> p (h f)"), pb[:, 0:nh * P]).then_inc(raised, 1)

            @block.vector
            def _(v):
                own = Own(v, ch)
                for h in range(nh):
                    last = nc.vector.tensor_scalar(dgm[:, h, :], g.ident[:, :], g.last[:, MAXC + h:MAXC + h + 1],
                                                   None, ALU.mult)
                last.then_inc(ready, 1)
                v.wait_ge(spread, 1)
                low = g.low_t[:, :].unsqueeze(1).to_broadcast([P, nh, P])
                own.link(nc.vector.tensor_tensor(w[:, :, :], pa[:, 0:nh * P].rearrange("p (h f) -> p h f", h=nh), low,
                                                 ALU.add))
                own.link(nc.vector.tensor_reduce(mc[:, :], w[:, :, :], AX_X, ALU.max))
                nc.vector.tensor_tensor(w[:, :, :], w[:, :, :], mc[:, :].unsqueeze(2).to_broadcast([P, nh, P]),
                                        ALU.subtract).then_inc(ready, 1)
                v.wait_ge(raised, 1)
                cross = g.cross_t[:, :].unsqueeze(1).to_broadcast([P, nh, P])
                nc.vector.tensor_tensor(w[:, :, :], w[:, :, :], cross, ALU.mult).then_inc(ready, 1)
                v.wait_ge(got, 16)
                own.link(nc.vector.tensor_copy(new[:, :], row[:, :]))
                mr = row[:, MAXC:MAXC + nh]
                own.link(nc.vector.tensor_tensor(mn[:, :], mr, mc[:, :], ALU.max))
                own.mark(nc.vector.tensor_tensor(e[:, 0, :], mr, mn[:, :], ALU.subtract))
                own.mark(nc.vector.tensor_copy(new[:, MAXC:MAXC + nh], mn[:, :]))
                nc.vector.tensor_tensor(e[:, 1, :], mc[:, :], mn[:, :], ALU.subtract).then_inc(raised, 1)
                v.wait_ge(raised, 3)
                v.wait_ge(spread, 3)

                def bc(a):
                    return a.unsqueeze(2).to_broadcast([P, nh, dh])

                def hv(a):
                    return a.rearrange("p (h d) -> p h d", h=nh)

                own.mark(nc.vector.tensor_tensor(hv(new[:, 0:D]), hv(row[:, 0:D]), bc(e[:, 0, :]), ALU.mult))
                own.mark(nc.vector.tensor_tensor(new[:, DEN:DEN + nh], row[:, DEN:DEN + nh], e[:, 0, :], ALU.mult))
                own.mark(nc.vector.tensor_tensor(hv(t[:, :]), hv(pc[:, 0:D]), bc(e[:, 1, :]), ALU.mult))
                own.link(nc.vector.tensor_tensor(mn[:, :], pc[:, DEN:DEN + nh], e[:, 1, :], ALU.mult))
                own.mark(nc.vector.tensor_tensor(new[:, 0:D], new[:, 0:D], t[:, :], ALU.add))
                nc.vector.tensor_tensor(new[:, DEN:DEN + nh], new[:, DEN:DEN + nh], mn[:, :],
                                        ALU.add).then_inc(ready, 1)



def norm_stats(nc, own, gate, src, st, mv, ve):
    for q in range(Q):
        own.mark(nc.vector.bn_stats(st[:, q, :], src[:, q, :]))
    own.wait()
    own.eng.sem_inc(gate, 1)
    for q in range(Q):
        own.mark(nc.vector.bn_aggr(mv[:, q, :], st[:, q, :]))
    own.wait()
    return nc.vector.tensor_scalar(ve[:, :], mv[:, :, 1], EPS, None, ALU.add)


def norm_apply(nc, dst, src, mv, rs):
    for q in range(Q):
        last = nc.vector.tensor_scalar(dst[:, q, :], src[:, q, :], mv[:, q, 0:1], rs[:, q:q + 1],
                                       ALU.subtract, ALU.mult)
    return last


def phase_settle(g, layer, heads):
    nc = g.nc
    dh = D // heads
    pre = f"s{layer}_"
    first = layer == 0
    bias = g.bias0 if first else g.bias1
    with ExitStack() as ctx:
        def sb(name, shape, dt=F32):
            return [ctx.enter_context(nc.sbuf_tensor(f"{pre}{name}{b}", shape, dt)) for b in range(B)]

        x = sb("x", [P, Q, D])
        ag = sb("ag", [P, Q, ROW])
        idx = sb("idx", [P, Q], I32)
        se = sb("se", [P, Q, TROW])
        ai = sb("ai", [P, Q, HEADS])
        s = sb("s", [P, Q, heads])
        m = sb("m", [P, Q, heads])
        e = sb("e", [P, 2, Q, heads])
        den = sb("den", [P, Q, heads])
        o = sb("o", [P, Q, D])
        sq = sb("sq", [P, Q, D])
        nr = sb("nr", [P, 4, Q])
        st = sb("st", [P, Q, 6])
        mv = sb("mv", [P, Q, 2])
        ve = sb("ve", [P, Q])
        rs = sb("rs", [P, Q])
        sh = sb("sh", [P, Q])
        xn = sb("xn", [P, Q, D])
        xt = sb("xt", [P, CHUNK])
        tr = sb("tr", [P, Q, TROW])
        ao = sb("ao", [P, Q, HEADS])
        hr = sb("hr", [P, Q, D])
        pt = [ctx.enter_context(nc.psum_tensor(f"{pre}pt{b}", [P, 512], F32)) for b in range(R)]
        pm = [ctx.enter_context(nc.psum_tensor(f"{pre}pm{b}", [P, 2, 512], F32)) for b in range(R)]
        pb = [ctx.enter_context(nc.psum_tensor(f"{pre}pb{b}", [P, 512], F32)) for b in range(R)]
        gathered = [g.indirect_sem(f"{pre}gathered{b}") for b in range(B)]
        copied_idx = g.sem(pre + "copied_idx")
        loaded = [g.sem(f"{pre}loaded{b}") for b in range(B)]
        asked = g.sem(pre + "asked")
        raised = g.sem(pre + "raised")
        biased = g.sem(pre + "biased")
        squared = g.sem(pre + "squared")
        normasked = g.sem(pre + "normasked")
        rooted = g.sem(pre + "rooted")
        tanhed = g.sem(pre + "tanhed")
        varasked = g.sem(pre + "varasked")
        scale = g.sem(pre + "scale")
        normed = g.sem(pre + "normed")
        shifted = g.sem(pre + "shifted")
        turned = g.sem(pre + "turned")
        copied = g.sem(pre + "copied")
        product = g.sem(pre + "product")
        hidden = g.sem(pre + "hidden")
        back = g.sem(pre + "back")
        moved = g.sem(pre + "moved")
        stored = [g.sem(f"{pre}stored{b}") for b in range(B)]
        freed = g.sem(pre + "freed")
        ch = g.sem(pre + "chain")
        gate = g.sem(pre + "gate")
        passes = NCHUNK // G
        xsrc = g.ins["x"] if first else g.x[1]
        nstores = 3
        L = 4 if first else 2
        with nc.Block() as block:
            @block.sync
            def _(sp):
                with sp.Fori(0, passes) as i:
                    for b in range(G):
                        c = i * G + b
                        sp.wait_ge(normed, nth_node(i, b))
                        for dst, src in ((x, xsrc), (se, g.t[layer]), (ai, g.ai[layer])):
                            sp.dma_start(dst[b % B][:, :, :], rows(src, c)).then_inc(loaded[b % B], 16)

            @block.gpsimd
            def _(pool):
                seq = StateGathers(g, pool, idx, ag, gathered, copied_idx, g.states)
                for b in range(B):
                    seq.rows(0, b)
                    seq.gather(0, b, 0, Q)
                for i, part in laps(pool):
                    for t in steps(part, 7):
                        for b in step(part, t, L):
                            pool.wait_ge(varasked, nth_node(i, b))
                            pool.tensor_tensor(rs[b % B][:, :], ve[b % B][:, :], g.mhalf[:, 0:Q], ALU.pow).then_inc(scale, 1)
                            if not first:
                                seq.rows(i, b + B, biased, nth_node(i, b))
                            seq.gather(i, b + B, Q // 2 if first else 0, Q)
                        if first:
                            for b in step(part, t, 2):
                                pool.wait_ge(normasked, nth_node(i, b))
                                pool.tensor_tensor(nr[b % B][:, 1, :], nr[b % B][:, 0, :], g.half[:, 0:Q],
                                                   ALU.pow).then_inc(rooted, 1)
                                seq.rows(i, b + B, biased, nth_node(i, b))
                                seq.gather(i, b + B, 0, Q // 2)
                        for b in step(part, t, 7):
                            gated(pool, stored[b % B], turn(i, b) * 16 * nstores, freed)
                for b in range(B):
                    pool.wait_ge(gathered[b % B], (passes * (G // B) + 1) * 16 * Q)

            @block.scalar
            def _(act):
                act.sem_inc(copied, R)
                for i, part in laps(act):
                    for t in steps(part, (L + 3)):
                        if not first:
                            for b in step(part, t, L + 3):
                                act.wait_ge(hidden, nth_node(i, b) + R)
                                act.dma_start(g.ht[0][bass.ds(i * G + b, 1)].rearrange("c p n -> (c p) n"),
                                              xt[b % B][:, :]).then_inc(stored[b % B], 16)
                                act.wait_ge(back, nth_node(i, b))
                                nc.scalar.copy(hr[b % B][:, :, :].rearrange("p q d -> p (q d)"),
                                               pb[b % R][:, :]).then_inc(moved, 1)
                                act.wait_ge(moved, nth_node(i, b) + R)
                                act.dma_start(rows(g.hr[0], i * G + b), hr[b % B][:, :, :]).then_inc(stored[b % B], 16)
                        if not first:
                            for b in step(part, t, L + 2):
                                act.wait_ge(product, nth_node(i, b))
                                nc.scalar.activation(xt[b % B][:, :], pm[b % R][:, 0, :], ACT.Relu,
                                                     bias=g.projb[:, 0:1]).then_inc(hidden, 1)
                        if first:
                            for b in step(part, t, L + 2):
                                act.wait_ge(product, nth_node(i, b))
                                view = pm[b % R][:, :, 0:2 * (D + 2)].rearrange("p a (s c) -> p a s c", s=2)
                                nc.scalar.copy(tr[b % B][:, :, 0:D + 1].rearrange("p (a s) c -> p a s c", s=2),
                                               view[:, :, :, 0:D + 1])
                                nc.scalar.copy(ao[b % B][:, :, 0:1].rearrange("p (a s) c -> p a s c", s=2),
                                               view[:, :, :, D + 1:D + 2]).then_inc(moved, 1)
                                c = i * G + b
                                act.wait_ge(moved, nth_node(i, b) + R)
                                act.dma_start(rows(g.t[1], c), tr[b % B][:, :, :]).then_inc(stored[b % B], 16)
                                act.dma_start(rows(g.ai[1], c), ao[b % B][:, :, :]).then_inc(stored[b % B], 16)
                        for b in step(part, t, L + 1):
                            c = i * G + b
                            act.wait_ge(shifted, nth_node(i, b))
                            for q in range(Q):
                                last = nc.scalar.activation(xn[b % B][:, q, :], o[b % B][:, q, :], ACT.Identity,
                                                            bias=sh[b % B][:, q:q + 1], scale=rs[b % B][:, q:q + 1])
                            last.then_inc(normed, 1)
                            act.wait_ge(normed, nth_node(i, b) + B)
                            act.dma_start(rows(g.x[layer + 1], c), xn[b % B][:, :, :]).then_inc(stored[b % B], 16)
                            act.wait_ge(turned, nth_node(i, b))
                            nc.scalar.copy(xt[b % B][:, :], pt[b % R][:, :]).then_inc(copied, 1)
                        if first:
                            for b in step(part, t, 3):
                                act.wait_ge(rooted, nth_node(i, b))
                                nc.scalar.activation(nr[b % B][:, 2, :], nr[b % B][:, 1, :], ACT.Tanh).then_inc(tanhed, 1)
                        for b in step(part, t, 0):
                            act.wait_ge(asked, nth_node(i, b))
                            nc.scalar.activation(e[b % B][:, :, :, :], e[b % B][:, :, :, :], ACT.Exp).then_inc(raised, 1)
                        if first:
                            for b in step(part, t, 1):
                                act.wait_ge(biased, nth_node(i, b))
                                nc.scalar.activation(xn[b % B][:, :, :], o[b % B][:, :, :], ACT.Relu).then_inc(squared, 1)
                                act.wait_ge(squared, i * (2 * G) + (2 * b + 1))
                                nc.scalar.activation(sq[b % B][:, :, :], xn[b % B][:, :, :], ACT.Square).then_inc(squared, 1)

            @block.tensor
            def _(pe):
                for i, part in laps(pe):
                    for t in steps(part, (L + 3)):
                        if not first:
                            for b in step(part, t, L + 3):
                                pe.wait_ge(hidden, nth_node(i, b) + R)
                                pe.wait_ge(moved, nth_node(i, b))
                                for q in range(Q):
                                    last = nc.tensor.transpose(pb[b % R][:, q * P:(q + 1) * P],
                                                               xt[b % B][:, q * P:(q + 1) * P], g.ident[:, :])
                                last.then_inc(back, 1)
                        for b in step(part, t, L + 2):
                            pe.wait_ge(copied, nth_node(i, b) + R)
                            pe.wait_ge(moved if first else hidden, nth_node(i, b))
                            if first:
                                for q in range(Q):
                                    w = (q % 2) * (D + 2)
                                    last = nc.tensor.matmul(pm[b % R][:, q // 2, w:w + D + 2], xt[b % B][:, q * P:(q + 1) * P],
                                                            g.w1aug[:, :], start=True, stop=True)
                                last.then_inc(product, 1)
                            else:
                                nc.tensor.matmul(pm[b % R][:, 0, :], g.projw[:, :], xt[b % B][:, :], start=True,
                                                 stop=True).then_inc(product, 1)
                        for b in step(part, t, L + 1):
                            pe.wait_ge(normed, nth_node(i, b) + B)
                            pe.wait_ge(copied, nth_node(i, b))
                            for q in range(Q):
                                last = nc.tensor.transpose(pt[b % R][:, q * P:(q + 1) * P], xn[b % B][:, q, :], g.ident[:, :])
                            last.then_inc(turned, 1)

            @block.vector
            def _(v):
                for b in range(B):
                    nc.vector.memset(tr[b][:, :, :], 0.0)
                    last = nc.vector.memset(ao[b][:, :, :], 0.0)
                last.then_inc(gate, 1)
                v.wait_ge(gate, 1)
                v.sem_inc(normed, B)
                v.sem_inc(moved, R)
                v.sem_inc(hidden, R)
                v.sem_inc(freed, B)
                per = G * (27 if first else 23)
                own = Own(v, ch)
                bb = bias[:, :].unsqueeze(1).to_broadcast([P, Q, D])

                def hv(a):
                    return a.rearrange("p q (h d) -> p q h d", h=heads)

                def score(b, r):
                    scb, mb, eb = s[b % B], m[b % B], e[b % B]
                    ms = ag[b % B][:, :, MAXC:MAXC + heads]
                    if r == 0:
                        v.wait_ge(loaded[b % B], turn(i, b) * 48)
                        v.wait_ge(gathered[b % B], turn(i, b) * 16 * Q)
                        own.mark(nc.vector.tensor_tensor(scb[:, :, :], se[b % B][:, :, D:D + heads],
                                                         ai[b % B][:, :, 0:heads], ALU.add))
                    if r == 1:
                        own.mark(nc.vector.scalar_tensor_tensor(scb[:, :, :], scb[:, :, :], SLOPE, scb[:, :, :],
                                                                ALU.mult, ALU.max))
                    if r == 2:
                        own.mark(nc.vector.tensor_tensor(mb[:, :, :], ms, scb[:, :, :], ALU.max))
                    if r == 3:
                        nc.vector.tensor_tensor(eb[:, 0, :, :], ms, mb[:, :, :], ALU.subtract)
                        nc.vector.tensor_tensor(eb[:, 1, :, :], scb[:, :, :], mb[:, :, :],
                                                ALU.subtract).then_inc(asked, 1)

                def combine(b, r):
                    db, eb, agb, seb, xb, ob = den[b % B], e[b % B], ag[b % B], se[b % B], x[b % B], o[b % B]
                    if r == 0:
                        v.wait_ge(raised, nth_node(i, b))
                        own.mark(nc.vector.tensor_tensor(db[:, :, :], agb[:, :, DEN:DEN + heads], eb[:, 0, :, :],
                                                         ALU.mult))
                    if r == 1:
                        own.mark(nc.vector.tensor_tensor(db[:, :, :], db[:, :, :], eb[:, 1, :, :], ALU.add))
                    if r == 2 and first:
                        own.mark(nc.vector.tensor_scalar(db[:, :, :], db[:, :, :], MIN_NORM, None, ALU.max))
                    if r == 3:
                        own.mark(nc.vector.reciprocal(db[:, :, :], db[:, :, :]))
                    if r == 4:
                        own.mark(nc.vector.tensor_tensor(
                            eb[:, :, :, :], eb[:, :, :, :],
                            db[:, :, :].unsqueeze(1).to_broadcast([P, 2, Q, heads]), ALU.mult))
                    if r == 5:
                        v.wait_ge(freed, nth_node(i, b))
                        if first:
                            for n, rows_ in enumerate((agb, seb)):
                                w = eb[:, n, :, :].unsqueeze(3).to_broadcast([P, Q, heads, dh])
                                own.mark(nc.vector.tensor_tensor(hv(rows_[:, :, 0:D]), hv(rows_[:, :, 0:D]), w, ALU.mult))
                        else:
                            for q in range(Q):
                                own.mark(nc.vector.scalar_tensor_tensor(
                                    xb[:, q, :], agb[:, q, 0:D], eb[:, 0, q, 0:1], xb[:, q, :], ALU.mult, ALU.add))
                    if r == 6:
                        if first:
                            own.mark(nc.vector.tensor_tensor(ob[:, :, :], agb[:, :, 0:D], seb[:, :, 0:D], ALU.add))
                        else:
                            for q in range(Q):
                                own.mark(nc.vector.scalar_tensor_tensor(
                                    ob[:, q, :], seb[:, q, 0:D], eb[:, 1, q, 0:1], xb[:, q, :], ALU.mult, ALU.add))
                    if r == 7:
                        nc.vector.tensor_tensor(ob[:, :, :], ob[:, :, :], bb, ALU.add).then_inc(biased, 1)

                def norm2(b, r):
                    if r == 6:
                        v.wait_ge(squared, i * (2 * G) + (2 * b + 2))
                        own.mark(nc.vector.tensor_reduce(nr[b % B][:, 0, :], sq[b % B][:, :, :], AX_X, ALU.add))
                    if r == 7:
                        nc.vector.tensor_scalar(nr[b % B][:, 0, :], nr[b % B][:, 0, :], MIN_NORM ** 2, None,
                                                ALU.max).then_inc(normasked, 1)

                def onto_ball(b, r):
                    n = nr[b % B]
                    if r == 0:
                        v.wait_ge(rooted, nth_node(i, b))
                        own.mark(nc.vector.reciprocal(n[:, 3, :], n[:, 1, :]))
                        v.wait_ge(tanhed, nth_node(i, b))
                        own.mark(nc.vector.tensor_scalar(n[:, 2, :], n[:, 2, :], MAX_NORM, None, ALU.min))
                    if r == 1:
                        own.mark(nc.vector.tensor_tensor(n[:, 3, :], n[:, 3, :], n[:, 2, :], ALU.mult))
                    if r == 2:
                        for q in range(Q):
                            own.mark(nc.vector.scalar_tensor_tensor(
                                o[b % B][:, q, :], xn[b % B][:, q, :], n[:, 3, q:q + 1], x[b % B][:, q, :],
                                ALU.mult, ALU.add))

                def stats(b, r):
                    if r == 3:
                        v.wait_ge(biased, nth_node(i, b))
                        for q in range(Q):
                            own.mark(nc.vector.bn_stats(st[b % B][:, q, :], o[b % B][:, q, :]))
                    if r == 4:
                        v.sem_inc(gate, 1)
                        for q in range(Q):
                            own.mark(nc.vector.bn_aggr(mv[b % B][:, q, :], st[b % B][:, q, :]))
                    if r == 5:
                        nc.vector.tensor_scalar(ve[b % B][:, :], mv[b % B][:, :, 1], EPS, None,
                                                ALU.add).then_inc(varasked, 1)

                def shift(b, r):
                    if r == 0:
                        v.wait_ge(scale, nth_node(i, b))
                        nc.vector.scalar_tensor_tensor(sh[b % B][:, :], mv[b % B][:, :, 0], -1.0, rs[b % B][:, :],
                                                       ALU.mult, ALU.mult).then_inc(shifted, 1)

                for i, part in laps(v):
                    own.lap(part, i, per)
                    for t in steps(part, L + 1):
                        for r in range(8):
                            for b in step(part, t, L + 1):
                                shift(b, r)
                            for b in step(part, t, L):
                                if first:
                                    onto_ball(b, r)
                                stats(b, r)
                            if first:
                                for b in step(part, t, 2):
                                    norm2(b, r)
                            for b in step(part, t, 1):
                                combine(b, r)
                            for b in step(part, t, 0):
                                score(b, r)
                            own.wait_new()
                    own.end(part)



def phase_relate(g, n):
    nc = g.nc
    pre = f"r{n}_"
    with ExitStack() as ctx:
        def sb(name, shape, dt=F32):
            return ctx.enter_context(nc.sbuf_tensor(pre + name, shape, dt))

        idx = [sb(f"idx{b}", [P, 2, KC], I32) for b in range(NB)]
        fac = [sb(f"fac{b}", [P, 2, KC]) for b in range(NB)]
        r = [sb(f"r{b}", [P, KC, D]) for b in range(NB)]
        ty = [sb(f"ty{b}", [P, KC, P]) for b in range(NB)]
        w = sb("w", [P, TYPES, D])
        ht = [sb(f"ht{b}", [P, 2, P]) for b in range(2)]
        hm = [sb(f"hm{b}", [P, TYPES, 2, P]) for b in range(2)]
        pt = [ctx.enter_context(nc.psum_tensor(f"{pre}pt{b}", [P, 512], F32)) for b in range(2)]
        pm = [ctx.enter_context(nc.psum_tensor(f"{pre}pm{b}", [P, 512], F32)) for b in range(2)]
        wloaded = g.sem(pre + "wloaded")
        listed = [g.sem(pre + f"listed{b}") for b in range(NB)]
        gathered = [g.indirect_sem(pre + f"gathered{b}") for b in range(NB)]
        stored = [g.sem(pre + f"stored{b}") for b in range(NB)]
        turned = g.sem(pre + "turned")
        copied = g.sem(pre + "copied")
        masked = g.sem(pre + "masked")
        product = g.sem(pre + "product")
        added = g.sem(pre + "added")
        stated = g.sem(pre + "stated")
        cleared = g.sem(pre + "cleared")
        gate = g.sem(pre + "gate")
        passes = ECHUNK // NB
        KC2 = KC // 2
        per = NB * KC2
        assert KC % 2 == 0 and per % 2 == 0
        with nc.Block() as block:
            @block.sync
            def _(sp):
                sp.dma_start(w[:, :, :], g.ins["edgew"][n]).then_inc(wloaded, 16)

                def types(i, b):
                    k0 = i * (NB * KC) + b * KC
                    src = g.type_rows[bass.ds(k0, KC)].rearrange("k p -> (k p)").unsqueeze(0).to_broadcast([P, KC * P])
                    sp.dma_start(ty[b][:, :, :].rearrange("p k e -> p (k e)"), src).then_inc(listed[b], 16)

                edge_streams(g, sp, idx, fac, r, listed, gathered, 16, stated, stored, g.sums, types)

            @block.gpsimd
            def _(pool):
                pool.wait_ge(cleared, 1)

                def gathers(b):
                    for k in range(KC):
                        pool.indirect_dma_start(
                            out=r[b][:, k, 0:D], out_offset=None, in_=g.hr[n],
                            in_offset=bass.IndirectOffsetOnAxis(ap=idx[b][:, 0, k:k + 1], axis=0)
                        ).then_inc(gathered[b], 16)

                edge_gathers(g, pool, gathers, listed, 48, stated, stored, gate)

            @block.tensor
            def _(pe):
                pe.wait_ge(wloaded, 16)
                with pe.Fori(0, passes) as i:
                    for j in range(per + 1):
                        if j < per:
                            b, k = divmod(j, KC2)
                            if k == 0:
                                pe.wait_ge(gathered[b], i * (16 * KC) + 16 * KC)
                            pe.wait_ge(copied, i * per + (j + 1))
                            for c in range(2):
                                last = nc.tensor.transpose(pt[j % 2][:, c * P:(c + 1) * P], r[b][:, 2 * k + c, 0:D],
                                                           g.ident[:, :])
                            last.then_inc(turned, 1)
                        if j > 0:
                            u = j - 1
                            pe.wait_ge(masked, i * per + (u + 3))
                            pe.wait_ge(added, i * (2 * per) + (2 * u + 2))
                            for c in range(2):
                                for t in range(TYPES):
                                    last = nc.tensor.matmul(pm[u % 2][:, c * D:(c + 1) * D], hm[u % 2][:, t, c, :],
                                                            w[:, t, :], start=(t == 0), stop=(t == TYPES - 1))
                            last.then_inc(product, 1)

            @block.scalar
            def _(act):
                act.sem_inc(copied, 2)
                with act.Fori(0, passes) as i:
                    for j in range(per):
                        act.wait_ge(turned, i * per + (j + 1))
                        act.wait_ge(masked, i * per + (j + 1))
                        nc.scalar.copy(ht[j % 2][:, :, :].rearrange("p c e -> p (c e)"),
                                       pt[j % 2][:, 0:2 * P]).then_inc(copied, 1)

            @block.vector
            def _(v):
                for b in range(NB):
                    last = nc.vector.memset(r[b][:, :, :], 0.0)
                last.then_inc(cleared, 1)
                v.wait_ge(cleared, 1)
                v.sem_inc(masked, 2)
                v.sem_inc(added, 4)
                with v.Fori(0, passes) as i:
                    for j in range(per + 1):
                        if j < per:
                            b, k = divmod(j, KC2)
                            if k == 0:
                                v.wait_ge(listed[b], i * 48 + 48)
                                v.sem_inc(gate, 1)
                            v.wait_ge(copied, i * per + (j + 3))
                            if j >= 2:
                                v.wait_ge(product, i * per + (j - 1))
                            for t in range(TYPES):
                                last = nc.vector.scalar_tensor_tensor(
                                    hm[j % 2][:, t, :, :], ty[b][:, 2 * k:2 * k + 2, :], float(t), ht[j % 2][:, :, :],
                                    ALU.is_equal, ALU.mult)
                            last.then_inc(masked, 1)
                        if j > 0:
                            b, k2 = divmod(j - 1, KC2)
                            v.wait_ge(product, i * per + j)
                            for c in range(2):
                                k = 2 * k2 + c
                                v.wait_ge(added, i * (2 * per) + (2 * j + 2 + c))
                                prev = r[b][:, k - 1, 0:D] if k else r[(b - 1) % NB][:, KC - 1, 0:D]
                                nc.vector.scalar_tensor_tensor(r[b][:, k, 0:D], prev, fac[b][:, 0, k:k + 1],
                                                               pm[(j - 1) % 2][:, c * D:(c + 1) * D], ALU.mult,
                                                               ALU.add).then_inc(added, 1)
                            if k2 == KC2 - 1:
                                v.wait_ge(added, i * (2 * per) + (2 * j + 4))
                                v.sem_inc(stated, 1)
                nc.vector.tensor_copy(g.last[:, 0:D], r[NB - 1][:, KC - 1, :]).then_inc(cleared, 1)
                v.wait_ge(cleared, 2)


def phase_gru(g, n):
    nc = g.nc
    pre = f"g{n}_"
    final = n == 1
    with ExitStack() as ctx:
        def sb(name, shape, dt=F32):
            return [ctx.enter_context(nc.sbuf_tensor(f"{pre}{name}{b}", shape, dt)) for b in range(B)]

        ag = sb("ag", [P, Q, D])
        idx = sb("idx", [P, Q], I32)
        h = sb("h", [P, CHUNK])
        x = sb("x", [P, Q, D])
        at = sb("at", [P, CHUNK])
        trz = sb("trz", [P, 2, CHUNK])
        hn = sb("hn", [P, CHUNK])
        c = sb("c", [P, CHUNK])
        hy = sb("hy", [P, CHUNK])
        hr = sb("hr", [P, Q, D])
        st = sb("st", [P, Q, 6])
        mv = sb("mv", [P, Q, 2])
        ve = sb("ve", [P, Q])
        rs = sb("rs", [P, Q])
        xn = sb("xn", [P, Q, D]) if final else None
        pa = ctx.enter_context(nc.psum_tensor(pre + "pa", [P, 512], F32))
        pg = [ctx.enter_context(nc.psum_tensor(f"{pre}pg{k}", [P, 512], F32)) for k in range(4)]
        pb = ctx.enter_context(nc.psum_tensor(pre + "pb", [P, 512], F32))
        pp = [ctx.enter_context(nc.psum_tensor(f"{pre}pp{k}", [P, 512], F32)) for k in range(2)]
        gathered = [g.indirect_sem(f"{pre}gathered{b}") for b in range(B)]
        copied_idx = g.sem(pre + "copied_idx")
        loaded = [g.sem(f"{pre}loaded{b}") for b in range(B)]
        turned = g.sem(pre + "turned")
        copied = g.sem(pre + "copied")
        gates = g.sem(pre + "gates")
        squashed = g.sem(pre + "squashed")
        casked = g.sem(pre + "casked")
        cand = g.sem(pre + "cand")
        hidden = g.sem(pre + "hidden")
        read = g.sem(pre + "read")
        back = g.sem(pre + "back")
        moved = g.sem(pre + "moved")
        varasked = g.sem(pre + "varasked")
        scale = g.sem(pre + "scale")
        normed = g.sem(pre + "normed")
        turned2 = g.sem(pre + "turned2")
        copied2 = g.sem(pre + "copied2")
        product = g.sem(pre + "product")
        drawn = g.sem(pre + "drawn")
        stored = [g.sem(f"{pre}stored{b}") for b in range(B)]
        freed = g.sem(pre + "freed")
        ch = g.sem(pre + "chain")
        gate = g.sem(pre + "gate")
        passes = NCHUNK // G
        nload = 2 if final else 1
        nstore = 3 if final else 2
        gb = g.gb[n]
        L = 5
        with nc.Block() as block:
            @block.sync
            def _(sp):
                with sp.Fori(0, passes) as i:
                    for b in range(G):
                        sp.wait_ge(moved, nth_node(i, b))
                        ci = i * G + b
                        sp.dma_start(h[b % B][:, :], g.ht[n][bass.ds(ci, 1)].rearrange(
                            "c p n -> (c p) n")).then_inc(loaded[b % B], 16)
                        if final:
                            sp.dma_start(x[b % B][:, :, :], rows(g.x[2], ci)).then_inc(loaded[b % B], 16)

            @block.gpsimd
            def _(pool):
                seq = StateGathers(g, pool, idx, ag, gathered, copied_idx, g.sums)
                for b in range(B):
                    seq.rows(0, b)
                    seq.gather(0, b, 0, Q)
                for i, part in laps(pool):
                    for t in steps(part, 7):
                        if final:
                            for b in step(part, t, 3):
                                pool.wait_ge(varasked, nth_node(i, b))
                                pool.tensor_tensor(rs[b % B][:, :], ve[b % B][:, :], g.mhalf[:, 0:Q], ALU.pow).then_inc(scale, 1)
                                seq.rows(i, b + B, copied, nth_node(i, b) + 1)
                                seq.gather(i, b + B, 0, Q)
                        if not final:
                            for b in step(part, t, 1):
                                seq.rows(i, b + B, copied, nth_node(i, b) + 1)
                                seq.gather(i, b + B, 0, Q)
                        for b in step(part, t, 7):
                            gated(pool, stored[b % B], turn(i, b) * 16 * nstore, freed)
                for b in range(B):
                    pool.wait_ge(gathered[b % B], (passes * (G // B) + 1) * 16 * Q)

            @block.tensor
            def _(pe):
                for i, part in laps(pe):
                    for t in steps(part, (L + 1)):
                        if final:
                            for b in step(part, t, L + 1):
                                pe.wait_ge(copied2, nth_node(i, b) + 1)
                                pe.wait_ge(drawn, nth_node(i, b) + (B - 1))
                                for q in range(Q):
                                    last = nc.tensor.matmul(pp[q // 2][:, (q % 2) * 2 * D:(q % 2 + 1) * 2 * D],
                                                            at[b % B][:, q * P:(q + 1) * P], g.wm1[:, :], start=True,
                                                            stop=True)
                                last.then_inc(product, 1)
                        if final:
                            for b in step(part, t, L):
                                pe.wait_ge(normed, nth_node(i, b))
                                pe.wait_ge(copied, i * G + (1 + (0 if part == DRAIN else b + L)))
                                pe.wait_ge(copied2, nth_node(i, b))
                                for q in range(Q):
                                    last = nc.tensor.transpose(pa[:, q * P:(q + 1) * P], xn[b % B][:, q, :], g.ident[:, :])
                                last.then_inc(turned2, 1)
                        for b in step(part, t, 3):
                            pe.wait_ge(hidden, nth_node(i, b))
                            pe.wait_ge(read, nth_node(i, b))
                            for q in range(Q):
                                hq = hy[b % B][:, q * P:(q + 1) * P]
                                if final:
                                    last = nc.tensor.matmul(pb[:, q * P:(q + 1) * P], hq, g.outw[:, :], start=True,
                                                            stop=True)
                                else:
                                    last = nc.tensor.transpose(pb[:, q * P:(q + 1) * P], hq, g.ident[:, :])
                            last.then_inc(back, 1)
                        for b in step(part, t, 1):
                            pe.wait_ge(copied, nth_node(i, b) + 1)
                            wi, wh = g.wih[n], g.whh[n]
                            pe.wait_ge(squashed, i * (3 * G) + (3 * b + 1))
                            nc.tensor.matmul(pg[0][:, :], wi[:, 0:D], at[b % B][:, :], start=True, stop=False)
                            nc.tensor.matmul(pg[0][:, :], wh[:, 0:D], h[b % B][:, :], start=False,
                                             stop=True).then_inc(gates, 1)
                            pe.wait_ge(squashed, i * (3 * G) + (3 * b + 2))
                            nc.tensor.matmul(pg[3][:, :], wh[:, 2 * D:3 * D], h[b % B][:, :], start=True,
                                             stop=True).then_inc(gates, 1)
                            pe.wait_ge(casked, nth_node(i, b))
                            nc.tensor.matmul(pg[2][:, :], wi[:, 2 * D:3 * D], at[b % B][:, :], start=True,
                                             stop=True).then_inc(gates, 1)
                            pe.wait_ge(squashed, i * (3 * G) + (3 * b + 3))
                            nc.tensor.matmul(pg[1][:, :], wi[:, D:2 * D], at[b % B][:, :], start=True, stop=False)
                            nc.tensor.matmul(pg[1][:, :], wh[:, D:2 * D], h[b % B][:, :], start=False,
                                             stop=True).then_inc(gates, 1)
                        for b in step(part, t, 0):
                            pe.wait_ge(loaded[b % B], turn(i, b) * 16 * nload)
                            pe.wait_ge(gathered[b % B], turn(i, b) * 16 * Q)
                            pe.wait_ge(copied, nth_node(i, b))
                            if final:
                                pe.wait_ge(copied2, i * G + (1 + (max(0, b + 1 - L) if part == FILL else b + 1 - L)))
                            for q in range(Q):
                                last = nc.tensor.transpose(pa[:, q * P:(q + 1) * P], ag[b % B][:, q, :], g.ident[:, :])
                            last.then_inc(turned, 1)

            @block.scalar
            def _(act):
                act.sem_inc(copied, 1)
                act.sem_inc(copied2, 1)
                act.sem_inc(squashed, 3)
                for i, part in laps(act):
                    for t in steps(part, (L + 1)):
                        if final:
                            for b in step(part, t, L + 1):
                                ci = i * G + b
                                act.wait_ge(drawn, nth_node(i, b) + B)
                                for k, tab in enumerate((g.ta, g.tb)):
                                    act.dma_start(rows(tab, ci), trz[b % B][:, k, :].rearrange("p (q d) -> p q d", q=Q)
                                                  ).then_inc(stored[b % B], 16)
                        if final:
                            for b in step(part, t, L):
                                ci = i * G + b
                                act.wait_ge(normed, nth_node(i, b))
                                act.dma_start(rows(g.x[3], ci), xn[b % B][:, :, :]).then_inc(stored[b % B], 16)
                                act.wait_ge(turned2, nth_node(i, b))
                                nc.scalar.copy(at[b % B][:, :], pa[:, :]).then_inc(copied2, 1)
                        if not final:
                            for b in step(part, t, 4):
                                ci = i * G + b
                                act.wait_ge(hidden, nth_node(i, b))
                                act.dma_start(g.ht[1][bass.ds(ci, 1)].rearrange("c p n -> (c p) n"),
                                              hy[b % B][:, :]).then_inc(stored[b % B], 16)
                                act.wait_ge(moved, nth_node(i, b) + B)
                                act.dma_start(rows(g.hr[1], ci), hr[b % B][:, :, :]).then_inc(stored[b % B], 16)
                        for b in step(part, t, 2):
                            act.wait_ge(casked, nth_node(i, b) + 1)
                            nc.scalar.activation(c[b % B][:, :], c[b % B][:, :], ACT.Tanh, bias=gb[:, 2:3]).then_inc(cand, 1)
                        for b in step(part, t, 1):
                            act.wait_ge(freed, nth_node(i, b))
                            act.wait_ge(gates, i * (4 * G) + (4 * b + 1))
                            nc.scalar.activation(trz[b % B][:, 0, :], pg[0][:, :], ACT.Tanh, bias=gb[:, 0:1],
                                                 scale=0.5).then_inc(squashed, 1)
                            act.wait_ge(gates, i * (4 * G) + (4 * b + 2))
                            nc.scalar.activation(hn[b % B][:, :], pg[3][:, :], ACT.Identity,
                                                 bias=gb[:, 3:4]).then_inc(squashed, 1)
                            act.wait_ge(gates, i * (4 * G) + (4 * b + 4))
                            nc.scalar.activation(trz[b % B][:, 1, :], pg[1][:, :], ACT.Tanh, bias=gb[:, 1:2],
                                                 scale=0.5).then_inc(squashed, 1)
                        for b in step(part, t, 0):
                            act.wait_ge(turned, nth_node(i, b))
                            act.wait_ge(drawn if final else moved, nth_node(i, b))
                            nc.scalar.copy(at[b % B][:, :], pa[:, :]).then_inc(copied, 1)

            @block.vector
            def _(v):
                v.sem_inc(casked, 1)
                v.sem_inc(read, 1)
                v.sem_inc(moved, B)
                v.sem_inc(freed, B)
                v.sem_inc(drawn, B)
                per = G * (15 if final else 4)
                own = Own(v, ch)
                for i, part in laps(v):
                    own.lap(part, i, per)
                    ob = g.outb[:, :].unsqueeze(1).to_broadcast([P, Q, D])
                    for t in steps(part, (L + 1)):
                        if final:
                            for b in step(part, t, L + 1):
                                v.wait_ge(product, nth_node(i, b))
                                for k in range(2):
                                    view = pp[k][:, :].rearrange("p (q a d) -> p a q d", q=2, a=2)
                                    last = nc.vector.tensor_tensor(
                                        trz[b % B][:, :, :].rearrange("p a (q d) -> p a q d", q=Q)[:, :, 2 * k:2 * k + 2, :],
                                        view,
                                        g.bab[:, :, :].unsqueeze(2).to_broadcast([P, 2, 2, D]), ALU.add)
                                last.then_inc(drawn, 1)
                        if final:
                            for b in step(part, t, 4):
                                v.wait_ge(scale, nth_node(i, b))
                                own.mark(norm_apply(nc, xn[b % B], hr[b % B], mv[b % B], rs[b % B]))
                                own.wait()
                                v.sem_inc(normed, 1)
                                v.sem_inc(moved, 1)
                        if not final:
                            for b in step(part, t, 3):
                                v.wait_ge(back, nth_node(i, b))
                                nc.vector.tensor_copy(hr[b % B][:, :, :].rearrange("p q d -> p (q d)"),
                                                      pb[:, :]).then_inc(read, 1)
                                v.wait_ge(read, nth_node(i, b) + 1)
                                v.sem_inc(moved, 1)
                        if final:
                            for b in step(part, t, 3):
                                v.wait_ge(back, nth_node(i, b))
                                own.link(nc.vector.tensor_tensor(hr[b % B][:, :, :],
                                                                 pb[:, :].rearrange("p (q d) -> p q d", q=Q),
                                                                 x[b % B][:, :, :], ALU.add))
                                v.sem_inc(read, 1)
                                own.link(nc.vector.tensor_tensor(hr[b % B][:, :, :], hr[b % B][:, :, :], ob, ALU.add))
                                norm_stats(nc, own, gate, hr[b % B], st[b % B], mv[b % B], ve[b % B]).then_inc(varasked, 1)
                        for b in step(part, t, 2):
                            v.wait_ge(cand, nth_node(i, b))
                            v.wait_ge(freed, nth_node(i, b))
                            own.link(nc.vector.tensor_tensor(h[b % B][:, :], h[b % B][:, :], c[b % B][:, :], ALU.subtract))
                            own.link(nc.vector.scalar_tensor_tensor(h[b % B][:, :], trz[b % B][:, 1, :], 1.0, h[b % B][:, :],
                                                                    ALU.add, ALU.mult))
                            own.link(nc.vector.scalar_tensor_tensor(h[b % B][:, :], h[b % B][:, :], 0.5, c[b % B][:, :],
                                                                    ALU.mult, ALU.add))
                            nc.vector.tensor_scalar(hy[b % B][:, :], h[b % B][:, :], 0.0, None, ALU.max).then_inc(hidden, 1)
                        for b in step(part, t, 1):
                            v.wait_ge(squashed, i * (3 * G) + (3 * b + 5))
                            own.link(nc.vector.scalar_tensor_tensor(hn[b % B][:, :], trz[b % B][:, 0, :], 1.0, hn[b % B][:, :],
                                                                    ALU.add, ALU.mult))
                            v.wait_ge(gates, i * (4 * G) + (4 * b + 3))
                            nc.vector.scalar_tensor_tensor(c[b % B][:, :], hn[b % B][:, :], 0.5, pg[2][:, :],
                                                           ALU.mult, ALU.add).then_inc(casked, 1)
                    own.end(part)



def phase_filter(g):
    nc = g.nc
    pre = "f_"
    with ExitStack() as ctx:
        def sb(name, shape, dt=F32):
            return ctx.enter_context(nc.sbuf_tensor(pre + name, shape, dt))

        idx = [sb(f"idx{b}", [P, 2, KC], I32) for b in range(NB)]
        fac = [sb(f"fac{b}", [P, 2, KC]) for b in range(NB)]
        r = [sb(f"r{b}", [P, KC, ROW]) for b in range(NB)]
        bd = [sb(f"bd{b}", [P, KC, D]) for b in range(NB)]
        ra = [sb(f"ra{b}", [RADIAL, KC, P]) for b in range(NB)]
        dg = sb("dg", [P, KC + 1])
        t1 = [sb(f"t1{b}", [P, P]) for b in range(2)]
        h1 = [sb(f"h1{b}", [P, P]) for b in range(2)]
        t2 = [sb(f"t2{b}", [P, P]) for b in range(2)]
        h2 = [sb(f"h2{b}", [P, P]) for b in range(2)]
        p1 = [ctx.enter_context(nc.psum_tensor(f"{pre}p1{b}", [P, 512], F32)) for b in range(2)]
        p2 = [ctx.enter_context(nc.psum_tensor(f"{pre}p2{b}", [P, 512], F32)) for b in range(2)]
        listed = [g.sem(pre + f"listed{b}") for b in range(NB)]
        gathered = [g.indirect_sem(pre + f"gathered{b}") for b in range(NB)]
        stored = [g.sem(pre + f"stored{b}") for b in range(NB)]
        radial = g.sem(pre + "radial")
        sqd = g.sem(pre + "sqd")
        joined = g.sem(pre + "joined")
        summed = g.sem(pre + "summed")
        tanh1 = g.sem(pre + "tanh1")
        silu1 = g.sem(pre + "silu1")
        summed2 = g.sem(pre + "summed2")
        tanh2 = g.sem(pre + "tanh2")
        silu2 = g.sem(pre + "silu2")
        added = g.sem(pre + "added")
        stated = g.sem(pre + "stated")
        degrees = g.sem(pre + "degrees")
        cleared = g.sem(pre + "cleared")
        gate = g.sem(pre + "gate")
        passes = ECHUNK // NB
        per = NB * KC
        SOON = 6
        coeff = -0.5 / (CUTOFF / (RADIAL - 1)) ** 2
        with nc.Block() as block:
            @block.sync
            def _(sp):
                def distances(i, b):
                    k0 = i * (NB * KC) + b * KC
                    src = g.dist_rows[bass.ds(k0, KC)].rearrange("k p -> (k p)").unsqueeze(0)
                    sp.dma_start(ra[b][:, :, :].rearrange("p k e -> p (k e)"),
                                 src.to_broadcast([RADIAL, KC * P])).then_inc(listed[b], 16)

                edge_streams(g, sp, idx, fac, r, listed, gathered, 32, stated, stored, g.states, distances)

            @block.gpsimd
            def _(pool):
                pool.wait_ge(cleared, 1)

                def gathers(b):
                    for k in range(KC):
                        pool.indirect_dma_start(
                            out=r[b][:, k, 0:D], out_offset=None, in_=g.ta,
                            in_offset=bass.IndirectOffsetOnAxis(ap=idx[b][:, 0, k:k + 1], axis=0)
                        ).then_inc(gathered[b], 16)
                        pool.indirect_dma_start(
                            out=bd[b][:, k, :], out_offset=None, in_=g.tb,
                            in_offset=bass.IndirectOffsetOnAxis(ap=idx[b][:, 1, k:k + 1], axis=0)
                        ).then_inc(gathered[b], 16)

                edge_gathers(g, pool, gathers, listed, 48, stated, stored, gate)

            @block.tensor
            def _(pe):
                with pe.Fori(0, passes) as i:
                    for j in range(per + 1):
                        if j < per:
                            b, k = divmod(j, KC)
                            if k == 0:
                                pe.wait_ge(joined, nth(i, b))
                                pe.wait_ge(radial, nth(i, b))
                            pe.wait_ge(silu1, i * per + (j + 1))
                            o = p1[j % 2][:, 0:P]
                            nc.tensor.matmul(o, r[b][:, k, 0:D], g.ident[:, :], start=True, stop=False)
                            nc.tensor.matmul(o, g.wr[:, :], ra[b][:, k, :], start=False,
                                             stop=True).then_inc(summed, 1)
                        if j > 0:
                            u = j - 1
                            pe.wait_ge(silu1, i * per + (u + 3))
                            pe.wait_ge(added, i * per + (u + 1))
                            o = p2[u % 2][:, 0:D]
                            nc.tensor.matmul(o, h1[u % 2][:, :], g.wm2[:, :], start=True, stop=False)
                            nc.tensor.matmul(o, g.ones[0:1, :], g.bm2[0:1, :], start=False,
                                             stop=True).then_inc(summed2, 1)

            @block.scalar
            def _(act):
                def squares(i, b):
                    act.wait_ge(listed[b], i * 48 + 48)
                    nc.scalar.activation(ra[b][:, :, :], ra[b][:, :, :], ACT.Square,
                                         bias=g.noff[:, 0:1]).then_inc(sqd, 1)

                def gaussians(i, b):
                    act.wait_ge(sqd, nth(i, b))
                    nc.scalar.activation(ra[b][:, :, :], ra[b][:, :, :], ACT.Exp, scale=coeff).then_inc(radial, 1)

                squares(0, 0)
                gaussians(0, 0)
                for i, last in with_next(act):
                    for j in range(per + 2):
                        if j < per:
                            b, k = divmod(j, KC)
                            n = (b + 1) % NB
                            if not (last and b == NB - 1):
                                if k == SOON:
                                    squares(i + (b + 1) // NB, n)
                                if k == SOON + 4:
                                    gaussians(i + (b + 1) // NB, n)
                            act.wait_ge(summed, i * per + (j + 1))
                            nc.scalar.activation(t1[j % 2][:, :], p1[j % 2][:, 0:P], ACT.Tanh,
                                                 scale=0.5).then_inc(tanh1, 1)
                        if 1 <= j <= per:
                            u = j - 1
                            act.wait_ge(summed2, i * per + (u + 1))
                            nc.scalar.activation(t2[u % 2][:, :], p2[u % 2][:, 0:D], ACT.Tanh,
                                                 scale=0.5).then_inc(tanh2, 1)

            @block.vector
            def _(v):
                for b in range(NB):
                    nc.vector.memset(r[b][:, :, :], 0.0)
                nc.vector.memset(dg[:, :], 0.0).then_inc(cleared, 1)
                v.wait_ge(cleared, 1)
                v.sem_inc(silu1, 2)
                v.sem_inc(added, 2)

                def join_rows(i, b):
                    v.wait_ge(gathered[b], i * (32 * KC) + 32 * KC)
                    nc.vector.tensor_tensor(r[b][:, :, 0:D], r[b][:, :, 0:D], bd[b][:, :, :], ALU.add
                                            ).then_inc(joined, 1)

                join_rows(0, 0)
                for i, last in with_next(v):
                    for j in range(per + 1):
                        if j < per:
                            b, k = divmod(j, KC)
                            if k == SOON and not (last and b == NB - 1):
                                join_rows(i + (b + 1) // NB, (b + 1) % NB)
                            v.wait_ge(tanh1, i * per + (j + 1))
                            nc.vector.scalar_tensor_tensor(h1[j % 2][:, :], t1[j % 2][:, :], 1.0,
                                                           p1[j % 2][:, 0:P], ALU.add, ALU.mult).then_inc(silu1, 1)
                        if j > 0:
                            u = j - 1
                            b, k = divmod(u, KC)
                            v.wait_ge(tanh2, i * per + (u + 1))
                            v.wait_ge(added, i * per + (u + 2))
                            nc.vector.scalar_tensor_tensor(h2[u % 2][:, :], t2[u % 2][:, :], 1.0,
                                                           p2[u % 2][:, 0:D], ALU.add, ALU.mult).then_inc(silu2, 1)
                            v.wait_ge(silu2, i * per + (u + 1))
                            prev = r[b][:, k - 1, 0:D] if k else r[(b - 1) % NB][:, KC - 1, 0:D]
                            nc.vector.scalar_tensor_tensor(r[b][:, k, 0:D], prev, fac[b][:, 0, k:k + 1],
                                                           h2[u % 2][:, :], ALU.mult, ALU.add).then_inc(added, 1)
                            if k == KC - 1:
                                nc.vector.tensor_tensor_scan(dg[:, 1:KC + 1], fac[b][:, 0, :],
                                                             g.ones[:, 0:KC], dg[:, 0:1], ALU.mult,
                                                             ALU.add).then_inc(degrees, 1)
                                v.wait_ge(degrees, i * (2 * NB) + (2 * b + 1))
                                nc.vector.tensor_copy(r[b][:, :, DEN], dg[:, 1:KC + 1])
                                nc.vector.tensor_copy(dg[:, 0:1], dg[:, KC:KC + 1]).then_inc(degrees, 1)
                                v.wait_ge(degrees, i * (2 * NB) + (2 * b + 2))
                                v.wait_ge(added, i * per + (u + 3))
                                v.sem_inc(stated, 1)
                nc.vector.tensor_copy(g.last[:, :], r[NB - 1][:, KC - 1, :]).then_inc(cleared, 1)
                v.wait_ge(cleared, 2)


def phase_update(g):
    nc = g.nc
    pre = "u_"
    with ExitStack() as ctx:
        def sb(name, shape, dt=F32):
            return [ctx.enter_context(nc.sbuf_tensor(f"{pre}{name}{b}", shape, dt)) for b in range(B)]

        x = sb("x", [P, Q, D])
        ag = sb("ag", [P, Q, ROW])
        idx = sb("idx", [P, Q], I32)
        xt = sb("xt", [P, CHUNK])
        at = sb("at", [P, CHUNK])
        dt = sb("dt", [2 * HEADS, CHUNK])
        th = sb("th", [P, CHUNK])
        u = sb("u", [P, CHUNK])
        th2 = sb("th2", [P, CHUNK])
        u2 = sb("u2", [P, CHUNK])
        y = sb("y", [P, Q, D])
        st = sb("st", [P, Q, 6])
        mv = sb("mv", [P, Q, 2])
        ve = sb("ve", [P, Q])
        rs = sb("rs", [P, Q])
        xn = sb("xn", [P, Q, D])
        px = ctx.enter_context(nc.psum_tensor(pre + "px", [P, 512], F32))
        pa = ctx.enter_context(nc.psum_tensor(pre + "pa", [P, 512], F32))
        pd = ctx.enter_context(nc.psum_tensor(pre + "pd", [P, 512], F32))
        pu = [ctx.enter_context(nc.psum_tensor(f"{pre}pu{b}", [P, 512], F32)) for b in range(R)]
        pv = [ctx.enter_context(nc.psum_tensor(f"{pre}pv{b}", [P, 512], F32)) for b in range(R)]
        py = ctx.enter_context(nc.psum_tensor(pre + "py", [P, 512], F32))
        gathered = [g.indirect_sem(f"{pre}gathered{b}") for b in range(B)]
        copied_idx = g.sem(pre + "copied_idx")
        loaded = [g.sem(f"{pre}loaded{b}") for b in range(B)]
        turned = g.sem(pre + "turned")
        copied = g.sem(pre + "copied")
        sum1 = g.sem(pre + "sum1")
        tanh1 = g.sem(pre + "tanh1")
        silu1 = g.sem(pre + "silu1")
        sum2 = g.sem(pre + "sum2")
        tanh2 = g.sem(pre + "tanh2")
        silu2 = g.sem(pre + "silu2")
        sum3 = g.sem(pre + "sum3")
        read3 = g.sem(pre + "read3")
        varasked = g.sem(pre + "varasked")
        scale = g.sem(pre + "scale")
        normed = g.sem(pre + "normed")
        stored = [g.sem(f"{pre}stored{b}") for b in range(B)]
        freed = g.sem(pre + "freed")
        ch = g.sem(pre + "chain")
        gate = g.sem(pre + "gate")
        passes = NCHUNK // G
        with nc.Block() as block:
            @block.sync
            def _(sp):
                with sp.Fori(0, passes) as i:
                    for b in range(G):
                        sp.wait_ge(normed, nth_node(i, b))
                        sp.dma_start(x[b % B][:, :, :], rows(g.x[3], i * G + b)).then_inc(loaded[b % B], 16)

            @block.gpsimd
            def _(pool):
                seq = StateGathers(g, pool, idx, ag, gathered, copied_idx, g.states)
                for b in range(B):
                    seq.rows(0, b)
                    seq.gather(0, b, 0, Q)
                for i, part in laps(pool):
                    for t in steps(part, 6):
                        for b in step(part, t, 6):
                            gated(pool, stored[b % B], turn(i, b) * 16, freed)
                        for b in step(part, t, 3):
                            pool.wait_ge(varasked, nth_node(i, b))
                            pool.tensor_tensor(rs[b % B][:, :], ve[b % B][:, :], g.mhalf[:, 0:Q], ALU.pow).then_inc(scale, 1)
                            seq.rows(i, b + B, copied, nth_node(i, b) + 1)
                            seq.gather(i, b + B, 0, Q)
                for b in range(B):
                    pool.wait_ge(gathered[b % B], (passes * (G // B) + 1) * 16 * Q)

            @block.tensor
            def _(pe):
                mm = nc.tensor.matmul
                for i, part in laps(pe):
                    for t in steps(part, 3):
                        for b in step(part, t, 3):
                            pe.wait_ge(silu2, nth_node(i, b) + R)
                            pe.wait_ge(read3, nth_node(i, b))
                            for q in range(Q):
                                last = mm(py[:, q * P:(q + 1) * P], u2[b % B][:, q * P:(q + 1) * P], g.wi2[:, :], start=True,
                                          stop=True)
                            last.then_inc(sum3, 1)
                        for b in step(part, t, 2):
                            pe.wait_ge(silu1, nth_node(i, b) + R)
                            pe.wait_ge(silu2, nth_node(i, b))
                            mm(pv[b % R][:, :], g.wd[:, :], u[b % B][:, :], start=True, stop=True).then_inc(sum2, 1)
                        for b in step(part, t, 1):
                            pe.wait_ge(copied, nth_node(i, b) + 1)
                            pe.wait_ge(silu1, nth_node(i, b))
                            mm(pu[b % R][:, :], g.wu1a[:, :], xt[b % B][:, :], start=True, stop=False)
                            mm(pu[b % R][:, :], g.wc[:, :], at[b % B][:, :], start=False, stop=False)
                            mm(pu[b % R][:, :], g.bc[:, :], dt[b % B][:, :], start=False, stop=True).then_inc(sum1, 1)
                        for b in step(part, t, 0):
                            pe.wait_ge(loaded[b % B], turn(i, b) * 16)
                            pe.wait_ge(gathered[b % B], turn(i, b) * 16 * Q)
                            pe.wait_ge(copied, nth_node(i, b))
                            for q in range(Q):
                                qs = slice(q * P, (q + 1) * P)
                                nc.tensor.transpose(px[:, qs], x[b % B][:, q, :], g.ident[:, :])
                                nc.tensor.transpose(pa[:, qs], ag[b % B][:, q, 0:D], g.ident[:, :])
                                last = nc.tensor.transpose(pd[0:2 * HEADS, qs], ag[b % B][:, q, D:ROW], g.ident[:, :])
                            last.then_inc(turned, 1)

            @block.scalar
            def _(act):
                act.sem_inc(copied, 1)
                for i, part in laps(act):
                    for t in steps(part, 4):
                        for b in step(part, t, 4):
                            act.wait_ge(normed, nth_node(i, b) + B)
                            act.dma_start(rows(g.out, i * G + b), xn[b % B][:, :, :]).then_inc(stored[b % B], 16)
                        for b in step(part, t, 2):
                            act.wait_ge(sum2, nth_node(i, b))
                            nc.scalar.activation(th2[b % B][:, :], pv[b % R][:, :], ACT.Tanh, bias=g.bd[:, 1:2],
                                                 scale=0.5).then_inc(tanh2, 1)
                        for b in step(part, t, 1):
                            act.wait_ge(sum1, nth_node(i, b))
                            nc.scalar.activation(th[b % B][:, :], pu[b % R][:, :], ACT.Tanh, bias=g.bu1[:, 1:2],
                                                 scale=0.5).then_inc(tanh1, 1)
                        for b in step(part, t, 0):
                            act.wait_ge(turned, nth_node(i, b))
                            nc.scalar.copy(xt[b % B][:, :], px[:, :])
                            nc.scalar.copy(at[b % B][:, :], pa[:, :])
                            nc.scalar.copy(dt[b % B][:, :], pd[0:2 * HEADS, :]).then_inc(copied, 1)

            @block.vector
            def _(v):
                v.sem_inc(read3, 1)
                v.sem_inc(silu1, R)
                v.sem_inc(silu2, R)
                v.sem_inc(normed, B)
                v.sem_inc(freed, B)
                per = G * 11
                bb = g.bi2[:, :].unsqueeze(1).to_broadcast([P, Q, D])
                own = Own(v, ch)
                for i, part in laps(v):
                    own.lap(part, i, per)

                    def silu(b, o, t, p, bias, done):
                        own.link(nc.vector.tensor_scalar(o[b % B][:, :], p[b % R][:, :], bias, None, ALU.add))
                        nc.vector.scalar_tensor_tensor(o[b % B][:, :], t[b % B][:, :], 1.0, o[b % B][:, :], ALU.add,
                                                       ALU.mult).then_inc(done, 1)

                    for t in steps(part, 4):
                        for b in step(part, t, 4):
                            v.wait_ge(scale, nth_node(i, b))
                            v.wait_ge(freed, nth_node(i, b))
                            norm_apply(nc, xn[b % B], y[b % B], mv[b % B], rs[b % B]).then_inc(normed, 1)
                        for b in step(part, t, 3):
                            v.wait_ge(sum3, nth_node(i, b))
                            nc.vector.tensor_tensor(y[b % B][:, :, :], py[:, :].rearrange("p (q d) -> p q d", q=Q),
                                                    x[b % B][:, :, :], ALU.add).then_inc(read3, 1)
                            v.wait_ge(read3, nth_node(i, b) + 1)
                            own.link(nc.vector.tensor_tensor(y[b % B][:, :, :], y[b % B][:, :, :], bb, ALU.add))
                            norm_stats(nc, own, gate, y[b % B], st[b % B], mv[b % B], ve[b % B]).then_inc(varasked, 1)
                        for b in step(part, t, 2):
                            v.wait_ge(tanh2, nth_node(i, b))
                            silu(b, u2, th2, pv, g.bd[:, 0:1], silu2)
                        for b in step(part, t, 1):
                            v.wait_ge(tanh1, nth_node(i, b))
                            silu(b, u, th, pu, g.bu1[:, 0:1], silu1)
                    own.end(part)



PHASES = [
    phase_weights, phase_edges,
    phase_product, phase_map, phase_log, phase_places,
    lambda g: phase_attend(g, 0, HEADS), lambda g: phase_join(g, 0, HEADS, g.states),
    lambda g: phase_settle(g, 0, HEADS),
    lambda g: phase_attend(g, 1, 1), lambda g: phase_join(g, 1, 1, g.states), lambda g: phase_settle(g, 1, 1),
    lambda g: phase_relate(g, 0), lambda g: phase_join(g, 2, 0, g.sums, D), lambda g: phase_gru(g, 0),
    lambda g: phase_relate(g, 1), lambda g: phase_join(g, 3, 0, g.sums, D), lambda g: phase_gru(g, 1),
    phase_filter, lambda g: phase_join(g, 4, 0, g.states), phase_update,
]


def gnn_kernel(nc, ins, out):
    with ExitStack() as ctx:
        g = Program(nc, ins, out, ctx)
        for phase in PHASES:
            g.sems = []
            with ExitStack() as g.sem_ctx:
                phase(g)
                with nc.Block() as block:
                    @block.gpsimd
                    def _(pool):
                        for sem in g.sems:
                            pool.sem_clear(sem)



def kernel(**inputs):
    import numpy as np
    import concourse.bacc as bacc
    from concourse.bass_utils import run_bass_kernel_spmd

    a = {k: np.asarray(v) for k, v in inputs.items()}

    def padded(v, n, fill=0):
        out = np.full((n,) + v.shape[1:], fill, v.dtype)
        out[:v.shape[0]] = v
        return out

    def col(v):
        return v.reshape(-1, 1)

    def row(v):
        return v.reshape(1, -1)

    att = a["L0_gnn_att"][0]
    dh = D // HEADS
    attm = np.zeros((HEADS, dh, 2 * HEADS), att.dtype)
    for h in range(HEADS):
        attm[h, :, h] = att[h, dh:]
        attm[h, :, HEADS + h] = att[h, :dh]
    lay = {
        "x": padded(a["x"], NPAD),
        "src": padded(a["src"], P * KE).reshape(P, KE),
        "dst": padded(a["dst"], P * KE, N).reshape(P, KE),
        "etype": padded(a["edge_type_8"], P * KE).reshape(P, KE),
        "dist": padded(a["edge_weight"], P * KE).reshape(P, KE),
        "w0": a["L0_gnn_W"], "w0t": a["L0_gnn_W"].T, "attm": attm.reshape(D, 2 * HEADS),
        "lin_bias": col(a["L0_gnn_lin_bias"]), "conv_bias": row(a["L0_gnn_conv_bias"]),
        "w1": a["L1_gnn_W"], "w1t": a["L1_gnn_W"].T,
        "att1": np.stack([a["L1_gnn_att_src"], a["L1_gnn_att_dst"]], 1), "bias1": row(a["L1_gnn_bias"]),
        "projwt": a["L2_gnn_node_proj_w"].T, "projb": col(a["L2_gnn_node_proj_b"]),
        "edgew": a["L2_gnn_edge_W"].transpose(0, 3, 1, 2),
        "wiht": a["L2_gnn_gru_wih"].transpose(0, 2, 1), "whht": a["L2_gnn_gru_whh"].transpose(0, 2, 1),
        "biht": a["L2_gnn_gru_bih"].reshape(2, 3, D).transpose(0, 2, 1),
        "bhht": a["L2_gnn_gru_bhh"].reshape(2, 3, D).transpose(0, 2, 1),
        "outwt": a["L2_gnn_out_w"].T, "out_b": row(a["L2_gnn_out_b"]),
        "wm1": a["L3_gnn_Wm1"], "bm1": row(a["L3_gnn_bm1"]), "wm2": a["L3_gnn_Wm2"],
        "bm2": row(a["L3_gnn_bm2"]), "wm3t": a["L3_gnn_Wm3"].T, "bm3": col(a["L3_gnn_bm3"]),
        "wu1": a["L3_gnn_Wu1"], "bu1": col(a["L3_gnn_bu1"]), "wu2t": a["L3_gnn_Wu2"].T,
        "bu2": col(a["L3_gnn_bu2"]), "wi1": a["L3_gnn_Wi1"], "bi1": col(a["L3_gnn_bi1"]),
        "wi2": a["L3_gnn_Wi2"], "bi2": row(a["L3_gnn_bi2"]),
    }
    lay = {k: np.ascontiguousarray(v) for k, v in lay.items()}
    nc = bacc.Bacc("TRN2", target_bir_lowering=False, num_devices=1)
    ins = {k: nc.dram_tensor(f"in_{k}", v.shape, mybir.dt.from_np(v.dtype), kind="ExternalInput").ap()
           for k, v in lay.items()}
    out = nc.dram_tensor("out", [NPAD, D], F32, kind="ExternalOutput").ap()
    gnn_kernel(nc, ins, out)
    r = run_bass_kernel_spmd(nc, [{f"in_{k}": v for k, v in lay.items()}], core_ids=[0])
    return r.results[0]["out"][:N]
```
